# Optimizing a Trainium2 kernel written in Bass

```python
import numpy as np
import jax
import jax.numpy as jnp

def _softmax(x, axis=-1):
    return jax.nn.softmax(x, axis=axis)
def _gelu(x):
    return jax.nn.gelu(x, approximate=True)
def _silu(x):
    return jax.nn.silu(x)
def _sigmoid(x):
    return jax.nn.sigmoid(x)
def _layernorm(x, axis=-1, eps=1e-5):
    m = jnp.mean(x, axis=axis, keepdims=True)
    v = jnp.var(x, axis=axis, keepdims=True)
    return (x - m) / jnp.sqrt(v + eps)
def _scatter_add(tgt, idx, src, axis=0):
    return tgt.at[idx].add(src)
def _segment_sum(src, seg, n):
    return jax.ops.segment_sum(src, seg, n)

kernel_name = 'mk_adj_ffn_d1_adj_512_3ea8b1'

def setup_inputs(seed: int = 0):
    np.random.seed(seed)
    _w = jnp.asarray
    def _rec_inputs():
        import jax
        import jax.numpy as jnp
        _gk = jax.random.key(seed)
        x = 7.34e-05 + 1 * jax.random.normal(jax.random.fold_in(_gk, 1), (128, 64, 512), jnp.float32)
        _w = (1.0 + jnp.arange(64, dtype=jnp.float32)) ** -0.5
        _w = _w / _w.mean()
        _pij = jnp.clip(0.0625 * _w[:, None] * _w[None, :], 0.0, 1.0)
        _a = jax.random.uniform(jax.random.fold_in(_gk, 2), (64, 64)) < _pij
        _a = jnp.logical_or(_a, jnp.swapaxes(_a, -1, -2))
        _a = jnp.logical_or(_a, jnp.eye(64, dtype=bool))
        _af = _a.astype(jnp.float32)
        adj = _af
        return x, adj
    x, adj = _rec_inputs()
    def _L0_gnn_setup():
        import jax, jax.numpy as jnp
        import numpy as np
        B, N, D, H = (16, 1025, 512, 8)
        LN_EPS = 1e-05

        def _make_mask(key, n):
            n_proto = n - 1
            adj = jax.random.bernoulli(key, 0.03, (n_proto, n_proto)).astype(jnp.float32)
            adj = jnp.clip(adj + adj.T + jnp.eye(n_proto, dtype=jnp.float32), 0.0, 1.0)
            mask = jnp.zeros((n, n), dtype=jnp.float32)
            mask = mask.at[0, :].set(1.0).at[:, 0].set(1.0)
            mask = mask.at[1:, 1:].set(adj)
            return mask
        key = jax.random.key(seed)
        ks = jax.random.split(key, 7)
        s = 1.0 / np.sqrt(D)
        return {'x': jax.random.normal(ks[0], (B, N, D), dtype=jnp.float32), 'w_qkv': jax.random.uniform(ks[1], (D, 3 * D), dtype=jnp.float32, minval=-s, maxval=s), 'w_proj': jax.random.uniform(ks[2], (D, D), dtype=jnp.float32, minval=-s, maxval=s), 'b_proj': jnp.zeros((D,), dtype=jnp.float32), 'ln_gamma': jnp.ones((D,), dtype=jnp.float32), 'ln_beta': jnp.zeros((D,), dtype=jnp.float32), 'attn_mask': _make_mask(ks[3], N)}
    _L0_gnn_all = _L0_gnn_setup()
    _L0_gnn_in = {k: v for k, v in _L0_gnn_all.items() if k in ('w_qkv', 'w_proj', 'b_proj', 'ln_gamma', 'ln_beta', )}
    del _L0_gnn_all

    def _L0_ffn_setup():
        import jax, jax.numpy as jnp
        import numpy as np
        B, S, D, F, E = (8, 4096, 512, 2048, 8)
        INIT_LAMBDA = 0.2
        LN_EPS = 1e-05
        LN_MERGE = 0.03
        key = jax.random.key(seed)
        ks = jax.random.split(key, 12)
        n = lambda k, shp, s=1.0: jax.random.normal(k, shp, dtype=jnp.float32) * s
        return {'hidden_states': n(ks[0], (B, S, D)), 'gfc1_w': n(ks[1], (D, D), 0.01), 'gfc1_b': jnp.zeros((D,), jnp.float32), 'gfc2_w': n(ks[2], (E, D), 0.01), 'gfc2_b': jnp.full((E,), INIT_LAMBDA, dtype=jnp.float32), 'W1': n(ks[3], (F, D), 0.02), 'b1': jnp.zeros((F,), jnp.float32), 'W2': n(ks[4], (D, F), 0.02), 'b2': jnp.zeros((D,), jnp.float32), 'ln_g': jnp.ones((D,), jnp.float32), 'ln_b': jnp.zeros((D,), jnp.float32), 'tv_W1': n(ks[5], (E, F, D), 0.02), 'tv_b1': n(ks[6], (E, F), 0.02), 'tv_W2': n(ks[7], (E, D, F), 0.02), 'tv_b2': n(ks[8], (E, D), 0.02), 'tv_ln_g': n(ks[9], (E, D), 0.02), 'tv_ln_b': n(ks[10], (E, D), 0.02)}
    _L0_ffn_all = _L0_ffn_setup()
    _L0_ffn_in = {k: v for k, v in _L0_ffn_all.items() if k in ('gfc1_w', 'gfc1_b', 'gfc2_w', 'gfc2_b', 'W1', 'b1', 'W2', 'b2', 'ln_g', 'ln_b', 'tv_W1', 'tv_b1', 'tv_W2', 'tv_b2', 'tv_ln_g', 'tv_ln_b', )}
    del _L0_ffn_all

    return {
        "x": x,
        "adj": adj,
        "L0_gnn_w_qkv": _L0_gnn_in["w_qkv"],
        "L0_gnn_w_proj": _L0_gnn_in["w_proj"],
        "L0_gnn_b_proj": _L0_gnn_in["b_proj"],
        "L0_gnn_ln_gamma": _L0_gnn_in["ln_gamma"],
        "L0_gnn_ln_beta": _L0_gnn_in["ln_beta"],
        "L0_ffn_gfc1_w": _L0_ffn_in["gfc1_w"],
        "L0_ffn_gfc1_b": _L0_ffn_in["gfc1_b"],
        "L0_ffn_gfc2_w": _L0_ffn_in["gfc2_w"],
        "L0_ffn_gfc2_b": _L0_ffn_in["gfc2_b"],
        "L0_ffn_W1": _L0_ffn_in["W1"],
        "L0_ffn_b1": _L0_ffn_in["b1"],
        "L0_ffn_W2": _L0_ffn_in["W2"],
        "L0_ffn_b2": _L0_ffn_in["b2"],
        "L0_ffn_ln_g": _L0_ffn_in["ln_g"],
        "L0_ffn_ln_b": _L0_ffn_in["ln_b"],
        "L0_ffn_tv_W1": _L0_ffn_in["tv_W1"],
        "L0_ffn_tv_b1": _L0_ffn_in["tv_b1"],
        "L0_ffn_tv_W2": _L0_ffn_in["tv_W2"],
        "L0_ffn_tv_b2": _L0_ffn_in["tv_b2"],
        "L0_ffn_tv_ln_g": _L0_ffn_in["tv_ln_g"],
        "L0_ffn_tv_ln_b": _L0_ffn_in["tv_ln_b"],
    }

def reference(x, adj, L0_gnn_w_qkv, L0_gnn_w_proj, L0_gnn_b_proj, L0_gnn_ln_gamma, L0_gnn_ln_beta, L0_ffn_gfc1_w, L0_ffn_gfc1_b, L0_ffn_gfc2_w, L0_ffn_gfc2_b, L0_ffn_W1, L0_ffn_b1, L0_ffn_W2, L0_ffn_b2, L0_ffn_ln_g, L0_ffn_ln_b, L0_ffn_tv_W1, L0_ffn_tv_b1, L0_ffn_tv_W2, L0_ffn_tv_b2, L0_ffn_tv_ln_g, L0_ffn_tv_ln_b):
    import jax
    import jax.numpy as jnp
    def _L0_gnn_ref(x, w_qkv, w_proj, b_proj, ln_gamma, ln_beta, attn_mask):
        import jax, jax.numpy as jnp
        import numpy as np
        B, N, D, H = (16, 1025, 512, 8)
        LN_EPS = 1e-05

        def _make_mask(key, n):
            n_proto = n - 1
            adj = jax.random.bernoulli(key, 0.03, (n_proto, n_proto)).astype(jnp.float32)
            adj = jnp.clip(adj + adj.T + jnp.eye(n_proto, dtype=jnp.float32), 0.0, 1.0)
            mask = jnp.zeros((n, n), dtype=jnp.float32)
            mask = mask.at[0, :].set(1.0).at[:, 0].set(1.0)
            mask = mask.at[1:, 1:].set(adj)
            return mask
        b, n, d = x.shape
        hd = d // H
        scale = hd ** (-0.5)
        qkv = (x @ w_qkv).reshape(b, n, 3, H, hd).transpose(2, 0, 3, 1, 4)
        q, k, v = (qkv[0], qkv[1], qkv[2])
        attn = jnp.einsum('bhnd,bhmd->bhnm', q, k) * scale
        attn = jnp.where(attn_mask[None, None] == 0, -jnp.inf, attn)
        attn = jax.nn.softmax(attn, axis=-1)
        o = jnp.einsum('bhnm,bhmd->bhnd', attn, v).transpose(0, 2, 1, 3).reshape(b, n, d)
        o = o @ w_proj + b_proj
        mu = jnp.mean(o, axis=-1, keepdims=True)
        var = jnp.mean(jnp.square(o - mu), axis=-1, keepdims=True)
        ln = (o - mu) * jax.lax.rsqrt(var + LN_EPS) * ln_gamma + ln_beta
        return o + ln

    def _L0_ffn_ref(hidden_states, gfc1_w, gfc1_b, gfc2_w, gfc2_b, W1, b1, W2, b2, ln_g, ln_b, tv_W1, tv_b1, tv_W2, tv_b2, tv_ln_g, tv_ln_b):
        import jax, jax.numpy as jnp
        import numpy as np
        B, S, D, F, E = (8, 4096, 512, 2048, 8)
        INIT_LAMBDA = 0.2
        LN_EPS = 1e-05
        LN_MERGE = 0.03
        x = hidden_states
        gh = jax.nn.relu(jnp.einsum('bsd,hd->bsh', x, gfc1_w) + gfc1_b)
        g = (jnp.einsum('bsh,eh->bse', gh, gfc2_w) + gfc2_b).mean(axis=1)
        W1m = W1 + jnp.einsum('be,efd->bfd', g, tv_W1)
        b1m = b1 + g @ tv_b1
        W2m = W2 + jnp.einsum('be,edf->bdf', g, tv_W2)
        b2m = b2 + g @ tv_b2
        lng = ln_g + LN_MERGE * (tv_ln_g - ln_g).sum(axis=0)
        lnb = ln_b + LN_MERGE * (tv_ln_b - ln_b).sum(axis=0)
        h = jax.nn.relu(jnp.einsum('bsd,bfd->bsf', x, W1m) + b1m[:, None, :])
        out = jnp.einsum('bsf,bdf->bsd', h, W2m) + b2m[:, None, :]
        res = x + out
        mu = res.mean(axis=-1, keepdims=True)
        var = res.var(axis=-1, keepdims=True)
        return (res - mu) * jax.lax.rsqrt(var + LN_EPS) * lng + lnb

    x = x + _L0_gnn_ref(_layernorm(x, axis=-1), L0_gnn_w_qkv, L0_gnn_w_proj, L0_gnn_b_proj, L0_gnn_ln_gamma, L0_gnn_ln_beta, adj)
    x = x + _L0_ffn_ref(_layernorm(x, axis=-1), L0_ffn_gfc1_w, L0_ffn_gfc1_b, L0_ffn_gfc2_w, L0_ffn_gfc2_b, L0_ffn_W1, L0_ffn_b1, L0_ffn_W2, L0_ffn_b2, L0_ffn_ln_g, L0_ffn_ln_b, L0_ffn_tv_W1, L0_ffn_tv_b1, L0_ffn_tv_W2, L0_ffn_tv_b2, L0_ffn_tv_ln_g, L0_ffn_tv_ln_b)
    return x


_drawn_inputs = setup_inputs


def setup_inputs(seed=0):
    import zlib

    import numpy as np

    out = dict(_drawn_inputs(seed))
    spreads = {'L0_gnn_b_proj': (0.0, 0.1),
     'L0_gnn_ln_gamma': (1.0, 0.2),
     'L0_gnn_ln_beta': (0.0, 0.1),
     'L0_ffn_gfc1_b': (0.0, 0.8),
     'L0_ffn_gfc2_b': (0.20000000298023224, 0.6),
     'L0_ffn_b1': (0.0, 0.361),
     'L0_ffn_b2': (0.0, 0.27),
     'L0_ffn_ln_g': (1.0, 0.2),
     'L0_ffn_ln_b': (0.0, 0.1)}
    factors = {'L0_ffn_gfc1_w': 8.0,
     'L0_ffn_gfc2_w': 4.254,
     'L0_ffn_tv_b1': 8.0,
     'L0_ffn_tv_b2': 8.0,
     'L0_ffn_tv_ln_g': 64.0,
     'L0_ffn_tv_ln_b': 64.0}
    for name, (base, spread) in spreads.items():
        noise = np.random.default_rng([zlib.crc32(name.encode()), seed]).standard_normal(out[name].shape)
        drawn = base * np.exp(spread * noise) if base else spread * noise
        out[name] = jnp.asarray(drawn.astype(out[name].dtype))
    for name, factor in factors.items():
        out[name] = (out[name] * factor).astype(out[name].dtype)
    return out
```

```python
from contextlib import ExitStack

import concourse.bass as bass
import numpy as np
from concourse import mybir

P = 128
GRAPHS, NODES, D = 128, 64, 512
F, E, H = 2048, 8, 8
HD = D // H
TOK = GRAPHS * NODES
KD = D // P
EPS = 1e-5
LN_MERGE = 0.03
NEG = -1e30

T_PART = [0, 1, 2, 0, 1, 0]
G_PART = [0, 0, 0, 1, 1, 2]
PAIRS = len(T_PART)
BASE_ROW = PAIRS * E
HALF = 56
KROWS = 2 * HALF
MAT = F * D
HROW = MAT // 2

GB = 32
GROUPS = GRAPHS // GB
GT = GB * NODES
PR = GT // P
FT = F // P
UNIT = 16384
PIECE = UNIT // 4

ALU = mybir.AluOpType
ACT = mybir.ActivationFunctionType
AX = mybir.AxisListType
F32 = mybir.dt.float32
BF16 = mybir.dt.bfloat16


def wait_apart(eng, sem, value, met, met_value):
    if not isinstance(value, int):
        value = eng.to_reg(value)
        eng.wait_ge(met, met_value)
    eng.wait_ge(sem, value)


def selection():
    sel = np.zeros((P, 2, 4), np.float32)
    for half in range(2):
        for c in range(PAIRS):
            for e in range(E):
                sel[half * HALF + c * E + e, half, G_PART[c]] = 1.0
        for part in range(3):
            sel[half * HALF + BASE_ROW + part, half, 3] = 1.0
    return sel.reshape(P, 8)


class Step:

    def __init__(self, j, par):
        self.j, self.par = j, par
        self.n = 2 * j + par

    def __add__(self, k):
        q = self.par + k
        return Step(self.j + q // 2, q % 2)

    def exists(self):
        return not isinstance(self.n, int) or self.n >= 0


ST = 256
NST = TOK // ST
TI = ST // P
CUT_E = E * MAT // NST // P
CUT_B = MAT // NST // P
CUT = CUT_E + CUT_B


def attend(nc, t, keep):
    gate_sum = keep["gate_sum"]
    ident = keep["ident"]
    with ExitStack() as ctx:
        def sb(name, shape, dt=F32):
            return ctx.enter_context(nc.sbuf_tensor(name, shape, dt))

        def sem(name):
            return ctx.enter_context(nc.semaphore(name))

        wqkv = sb("wqkv", [P, KD, 3 * D])
        wproj = sb("wproj", [P, KD, D])
        gfc1 = sb("gfc1", [P, KD, D])
        gfc1_b = sb("gfc1_b", [P, KD])
        bproj = sb("bproj", [P, D])
        gamma = sb("gamma", [P, D])
        beta = sb("beta", [P, D])
        adj = sb("adj", [P, NODES])
        mask = sb("mask", [P, NODES])
        power = sb("power", [P, TI])
        x_in = sb("x_in", [P, 2, TI, D])
        x_res = sb("x_res", [P, TI, D])
        n1 = sb("n1", [P, TI, D])
        n1T = sb("n1T", [P, KD, ST])
        qkT = sb("qkT", [P, 2, 2 * KD, ST])
        v = sb("v", [P, 2, TI, D])
        scores = sb("scores", [P, 2, H, NODES])
        top = sb("top", [P, 2, H])
        total = sb("total", [P, 2, H])
        inv = sb("inv", [P, 2, H])
        probs = sb("probs", [P, TI, 2, H // 2, P])
        probsT = sb("probsT", [P, TI, H, P])
        oT = sb("oT", [P, TI, KD, P])
        o2 = sb("o2", [P, TI, D])
        ln = sb("ln", [P, TI, D])
        x1 = sb("x1", [P, TI, D])
        n2 = sb("n2", [P, TI, D])
        n2T = sb("n2T", [P, KD, ST])
        gate_h = sb("gate_h", [P, 2, 2, ST])
        whole = sb("whole", [P, 2, CUT])
        part = [sb(f"part{k}", [P, 2, CUT], BF16) for k in range(3)]
        zero = sb("zero", [P, 512], BF16)
        st_x, ag_x, rs_x = sb("st_x", [P, TI, 6]), sb("ag_x", [P, TI, 2]), sb("rs_x", [P, TI])
        ve_x = sb("ve_x", [P, TI])
        st_y, ag_y, rs_y = sb("st_y", [P, 2 * TI, 6]), sb("ag_y", [P, 2 * TI, 2]), sb("rs_y", [P, 2 * TI])
        ve_y = sb("ve_y", [P, 2 * TI])

        ps_x = ctx.enter_context(nc.psum_tensor("ps_x", [P, 4, 512], F32))
        ps_y = ctx.enter_context(nc.psum_tensor("ps_y", [P, 2, 512], F32))
        ps_z = ctx.enter_context(nc.psum_tensor("ps_z", [P, 2, 512], F32))

        consts_in, consts_set = sem("consts_in"), sem("consts_set")
        x_loaded = [sem("x_loaded0"), sem("x_loaded1")]
        res_loaded = sem("res_loaded")
        x_filled, y_filled, z_filled = sem("x_filled"), sem("y_filled"), sem("z_filled")
        x_emptied = sem("x_emptied")
        y_emptied_act, y_emptied_dve = sem("y_emptied_act"), sem("y_emptied_dve")
        z_emptied = sem("z_emptied")
        gate_summed = sem("gate_summed")
        n1_ready, var_x, rstd_x = sem("n1_ready"), sem("var_x"), sem("rstd_x")
        shifted, exp_done, inv_ready, probs_ready = sem("shifted"), sem("exp_done"), sem("inv_ready"), sem("probs_ready")
        var_y, rstd_y = sem("var_y"), sem("rstd_y")
        x1_ready, n2_ready = sem("x1_ready"), sem("n2_ready")
        x1_stored, n2_stored, n2T_stored = sem("x1_stored"), sem("n2_stored"), sem("n2T_stored")
        dve_link = sem("dve_link")
        whole_in = [sem(f"whole_in{m}") for m in range(2)]
        high_cut = [sem(f"high_cut{m}") for m in range(2)]
        high_off = [sem(f"high_off{m}") for m in range(2)]
        mid_cut = [sem(f"mid_cut{m}") for m in range(2)]
        low_cut = [sem(f"low_cut{m}") for m in range(2)]
        parts_stored = [sem(f"parts_stored{m}") for m in range(2)]
        zero_set, zero_stored = sem("zero_set"), sem("zero_stored")

        rows_e = [t[f"s{m}"].rearrange("(h a p c) -> a h p c", h=2, p=64, c=CUT_E) for m in (1, 2)]
        rows_b = [t[f"s{m}"].rearrange("(h a p c) -> a h p c", h=2, p=64, c=CUT_B) for m in (1, 2)]
        BLOCKS_E = HROW // (64 * CUT_E)
        BLOCKS_B = HROW // (64 * CUT_B)
        STORES = 16 * (PAIRS + 3)

        XU, YU, ZU = 8, 10, 4
        Y_ORDER = ["S0", "S1", "P0a", "P0b", "O0", "P1a", "P1b", "R0", "O1", "R1"]
        Y_DVE = [u[0] in "SR" for u in Y_ORDER]
        NDVE = sum(Y_DVE)

        def yi(name):
            return Y_ORDER.index(name)

        def y_free(pe, s, k, needed=None):
            if needed is not None:
                rank = act_rank(needed)
                if not Y_DVE[k - 2]:
                    rank = max(rank, act_rank(Y_ORDER[k - 2]))
                pe.wait_ge(y_emptied_act, s.n * (YU - NDVE) + rank)
                if not Y_DVE[k - 2]:
                    return
            prev, back = (k - 2) % YU, k < 2
            ps = s + (-1) if back else s
            if not ps.exists():
                return
            rank = sum(1 for i in range(prev + 1) if Y_DVE[i] == Y_DVE[prev])
            if Y_DVE[prev]:
                wait_apart(pe, y_emptied_dve, ps.n * NDVE + rank, consts_in, 16 * NCONST)
            else:
                wait_apart(pe, y_emptied_act, ps.n * (YU - NDVE) + rank, consts_in, 16 * NCONST)

        def bank_y(k):
            return ps_y[:, k % 2, :]

        def act_rank(name):
            return sum(1 for i in range(yi(name) + 1) if not Y_DVE[i])

        def dve_rank(name):
            return sum(1 for i in range(yi(name) + 1) if Y_DVE[i])

        xt = t["x"].rearrange("(s i p) d -> s p i d", i=TI, p=P)
        x1t = t["x1"].rearrange("(s i p) d -> s p i d", i=TI, p=P)
        n2t = t["n2"].rearrange("(s i p) d -> s p i d", i=TI, p=P)
        n2Tt = t["n2T"].rearrange("k p (s c) -> s p k c", c=ST)

        def tile_of(dram, s):
            return dram[bass.ds(s.n, 1)].rearrange("s p i d -> (s p) i d")

        def run(engine, body, before, after):
            before()
            body(Step(0, 0), True, True)
            body(Step(0, 1), True, True)
            with engine.Fori(1, NST // 2 - 1) as j:
                body(Step(j, 0), True, True)
                body(Step(j, 1), True, True)
            body(Step(NST // 2 - 1, 0), True, False)
            body(Step(NST // 2 - 1, 1), False, False)
            after()

        NCONST = 9
        with nc.Block() as block:
            @block.sync
            def _(sp):
                def load_x(s):
                    q = s + (-2)
                    if q.exists():
                        sp.wait_ge(n1_ready, q.n + 1)
                    sp.dma_start(x_in[:, s.par], tile_of(xt, s)).then_inc(x_loaded[s.par], 16)

                def load_whole(s, m):
                    for src, at, n in ((t[f"tvW{m + 1}"], 0, CUT_E), (t[f"W{m + 1}"], CUT_E, CUT_B)):
                        src = src.rearrange("(s p c) -> s p c", p=P, c=n)
                        sp.dma_start(whole[:, m, at:at + n], src[bass.ds(s.n, 1)].rearrange("s p c -> (s p) c")
                                     ).then_inc(whole_in[m], 16)

                def store_parts(s, m):
                    wait_apart(sp, low_cut[m], s.n + 1, zero_set, 1)
                    for c in range(PAIRS):
                        sp.dma_start(rows_e[m][bass.ds(c * E * BLOCKS_E + s.n, 1)].rearrange("a h p c -> (a h) p c"),
                                     part[T_PART[c]][:, m, 0:CUT_E]).then_inc(parts_stored[m], 16)
                    for k in range(3):
                        sp.dma_start(rows_b[m][bass.ds((BASE_ROW + k) * BLOCKS_B + s.n, 1)
                                               ].rearrange("a h p c -> (a h) p c"),
                                     part[k][:, m, CUT_E:CUT]).then_inc(parts_stored[m], 16)

                def before():
                    load_x(Step(0, 0))
                    for dst, src in ((wqkv, "wqkv"), (gfc1, "gfc1T"), (wproj, "wproj")):
                        sp.dma_start(dst[:], t[src].rearrange("(k p) n -> p k n", p=P)).then_inc(consts_in, 16)
                    sp.dma_start(gfc1_b[:], t["gfc1_b"]).then_inc(consts_in, 16)
                    for dst, src in ((bproj, "bproj"), (gamma, "gamma"), (beta, "beta")):
                        sp.dma_start(dst[:], t[src].partition_broadcast(P)).then_inc(consts_in, 16)
                    for h in range(2):
                        sp.dma_start(adj[64 * h:64 * h + 64, :], t["adj"]).then_inc(consts_in, 16)
                    load_x(Step(0, 1))
                    for m in range(2):
                        load_whole(Step(0, 0), m)
                    sp.wait_ge(zero_set, 1)
                    for m in (1, 2):
                        for row in range(KROWS):
                            if row % HALF >= BASE_ROW + 3:
                                dst = t[f"s{m}"][row * HROW:(row + 1) * HROW].rearrange("(p a c) -> p a c", p=P, c=512)
                                sp.dma_start(dst, zero[:].unsqueeze(1).broadcast_to([P, dst.shape[1], 512])
                                             ).then_inc(zero_stored, 16)

                def body(s, has_x, has_l):
                    if has_l:
                        load_x(s + 2)
                    q = s + (-1)
                    if q.exists():
                        sp.wait_ge(x1_ready, TI * (q.n + 1))
                    sp.dma_start(x_res[:], tile_of(xt, s)).then_inc(res_loaded, 16)
                    if q.exists():
                        sp.wait_ge(z_emptied, 4 * q.n + 2)
                        sp.dma_start(n2Tt[bass.ds(q.n, 1)].rearrange("s p k c -> (s p) k c"),
                                     n2T[:]).then_inc(n2T_stored, 16)
                    for m in range(2):
                        store_parts(s, m)
                        if has_x:
                            load_whole(s + 1, m)
                    sp.wait_ge(x1_ready, TI * (s.n + 1))
                    sp.dma_start(tile_of(x1t, s), x1[:]).then_inc(x1_stored, 16)
                    sp.wait_ge(n2_ready, TI * (s.n + 1))
                    sp.dma_start(tile_of(n2t, s), n2[:]).then_inc(n2_stored, 16)

                def after():
                    sp.wait_ge(z_emptied, 4 * (NST - 1) + 2)
                    sp.dma_start(n2Tt[NST - 1], n2T[:]).then_inc(n2T_stored, 16)
                    sp.wait_ge(n2T_stored, 16 * NST)
                    sp.wait_ge(x1_stored, 16 * NST)
                    sp.wait_ge(n2_stored, 16 * NST)
                    sp.wait_ge(zero_stored, 16 * 2 * 2 * (HALF - BASE_ROW - 3))
                    for m in range(2):
                        sp.wait_ge(parts_stored[m], STORES * NST)

                run(sp, body, before, after)

            @block.tensor
            def _(pe):
                def x_fill(s, k):
                    q, prev = (s, k - 4) if k >= 4 else (s + (-1), k + 4)
                    if k == 2:
                        pe.wait_ge(x_emptied, XU * s.n + 2)
                    elif q.exists():
                        pe.wait_ge(x_emptied, XU * q.n + prev + 1)
                    bank = ps_x[:, k % 4, :]
                    if k < 2:
                        if k == 0:
                            pe.wait_ge(n1_ready, s.n + 1)
                        for c in range(KD):
                            last = pe.transpose(bank[:, c * P:(c + 1) * P], n1[:, k, c * P:(c + 1) * P], ident[:])
                    elif k < 6:
                        for m in range(2):
                            ch = 2 * (k - 2) + m
                            for c in range(KD):
                                last = pe.matmul(bank[:, m * ST:(m + 1) * ST], wqkv[:, c, ch * P:(ch + 1) * P],
                                                 n1T[:, c, :], start=(c == 0), stop=(c == KD - 1))
                    else:
                        i = k - 6
                        for c in range(KD):
                            last = pe.matmul(bank[:], n1T[:, c, i * P:(i + 1) * P], wqkv[:, c, 2 * D:3 * D],
                                             start=(c == 0), stop=(c == KD - 1))
                    last.then_inc(x_filled, 1)

                def y_fill(s, name):
                    k, i = yi(name), int(name[1])
                    y_free(pe, s, k, {"O": f"P{i}b", "R": f"O{i}"}.get(name[0]))
                    bank = bank_y(k)
                    if name[0] == "S":
                        if i == 0:
                            wait_apart(pe, x_emptied, XU * (s.n + 1), consts_in, 16 * NCONST)
                        r = HD * i
                        for at in range(0, ST, NODES):
                            g = at // NODES
                            out_rows = slice(NODES * (g % 2), NODES * (g % 2) + NODES)
                            for h in range(H // 2):
                                col = ((g // 2) * (H // 2) + h) * NODES
                                last = pe.matmul(bank[out_rows, col:col + NODES],
                                                 qkT[r:r + HD, s.par, h, at:at + NODES],
                                                 qkT[r:r + HD, s.par, KD + h, at:at + NODES],
                                                 start=True, stop=True)
                    elif name[0] == "P":
                        odd = int(name[2] == "b")
                        pe.wait_ge(probs_ready, 2 * s.n + odd + 1)
                        for h in range(4):
                            last = pe.transpose(bank[:, h * P:(h + 1) * P], probs[:, i, odd, h, :], ident[:])
                    elif name[0] == "O":
                        for h in range(H):
                            r = HD * (h % 2)
                            last = pe.matmul(bank[r:r + HD, (h // 2) * P:(h // 2 + 1) * P],
                                             v[:, s.par, i, h * HD:(h + 1) * HD],
                                             probsT[:, i, (h % 2) * (H // 2) + h // 2, :],
                                             start=True, stop=True)
                    else:
                        for c in range(KD):
                            last = pe.matmul(bank[:], oT[:, i, c, :], wproj[:, c, :],
                                             start=(c == 0), stop=(c == KD - 1))
                    last.then_inc(y_filled, 1)

                def z_fill(s, k):
                    if not s.exists():
                        return
                    q, prev = (s, k - 2) if k >= 2 else (s + (-1), k + 2)
                    if k == 2:
                        pe.wait_ge(z_emptied, ZU * s.n + 2)
                    elif q.exists():
                        pe.wait_ge(z_emptied, ZU * q.n + prev + 1)
                    bank = ps_z[:, k % 2, :]
                    if k < 2:
                        pe.wait_ge(n2_ready, TI * s.n + k + 1)
                        for c in range(KD):
                            last = pe.transpose(bank[:, c * P:(c + 1) * P], n2[:, k, c * P:(c + 1) * P], ident[:])
                    else:
                        for m in range(2):
                            ch = 2 * (k - 2) + m
                            for c in range(KD):
                                last = pe.matmul(bank[:, m * ST:(m + 1) * ST], gfc1[:, c, ch * P:(ch + 1) * P],
                                                 n2T[:, c, :], start=(c == 0), stop=(c == KD - 1))
                    last.then_inc(z_filled, 1)

                def before():
                    pe.wait_ge(consts_in, 16 * NCONST)
                    for k in range(XU):
                        x_fill(Step(0, 0), k)

                def body(s, has_x, has_l):
                    z = s + (-1)

                    def x(k):
                        if has_x:
                            x_fill(s + 1, k)
                    y_fill(s, "S0")
                    y_fill(s, "S1")
                    z_fill(z, 0)
                    z_fill(z, 1)
                    x(0)
                    x(1)
                    x(2)
                    x(3)
                    y_fill(s, "P0a")
                    y_fill(s, "P0b")
                    z_fill(z, 2)
                    y_fill(s, "O0")
                    x(4)
                    y_fill(s, "P1a")
                    y_fill(s, "P1b")
                    z_fill(z, 3)
                    y_fill(s, "R0")
                    y_fill(s, "O1")
                    x(5)
                    y_fill(s, "R1")
                    x(6)
                    x(7)

                def after():
                    for k in range(ZU):
                        z_fill(Step(NST // 2 - 1, 1), k)

                run(pe, body, before, after)

            @block.scalar
            def _(act):
                def x_empty(s, k):
                    act.wait_ge(x_filled, XU * s.n + k + 1)
                    bank = ps_x[:, k % 4, :]
                    if k < 2:
                        dst = n1T[:, :, k * P:(k + 1) * P]
                        src = bank.rearrange("p (c n) -> p c n", n=P)
                    elif k < 6:
                        dst = qkT[:, s.par, 2 * (k - 2):2 * (k - 2) + 2, :]
                        src = bank.rearrange("p (c n) -> p c n", n=ST)
                    else:
                        dst, src = v[:, s.par, k - 6, :], bank
                    nc.scalar.activation(dst, src, ACT.Copy).then_inc(x_emptied, 1)

                def y_empty(s, name):
                    k, i = yi(name), int(name[1])
                    act.wait_ge(y_filled, YU * s.n + k + 1)
                    src = bank_y(k).rearrange("p (c n) -> p c n", n=P)
                    if name[0] == "P":
                        h = (H // 2) * (name[2] == "b")
                        dst = probsT[:, i, h:h + 4, :]
                    else:
                        dst = oT[:, i]
                    nc.scalar.activation(dst, src, ACT.Copy).then_inc(y_emptied_act, 1)

                def exponent(s, i):
                    act.wait_ge(shifted, TI * s.n + i + 1)
                    nc.scalar.activation(scores[:, i], scores[:, i], ACT.Exp).then_inc(exp_done, 1)

                def z_empty(s, k):
                    if not s.exists():
                        return
                    q = s + (-1)
                    act.wait_ge(z_filled, ZU * s.n + k + 1)
                    bank = ps_z[:, k % 2, :]
                    if k < 2:
                        if k == 0 and q.exists():
                            act.wait_ge(n2T_stored, 16 * (q.n + 1))
                        nc.scalar.activation(n2T[:, :, k * P:(k + 1) * P], bank.rearrange("p (c n) -> p c n", n=P),
                                             ACT.Copy).then_inc(z_emptied, 1)
                        return
                    if q.exists():
                        act.wait_ge(gate_summed, 2 * q.n + k - 1)
                    for m in range(2):
                        ch = 2 * (k - 2) + m
                        last = nc.scalar.activation(gate_h[:, k - 2, m, :], bank[:, m * ST:(m + 1) * ST], ACT.Relu,
                                                    bias=gfc1_b[:, ch:ch + 1])
                    last.then_inc(z_emptied, 1)

                def cut_high(s, m):
                    act.wait_ge(whole_in[m], 32 * (s.n + 1))
                    q = s + (-1)
                    if q.exists():
                        act.wait_ge(parts_stored[m], STORES * (q.n + 1))
                    nc.scalar.activation(part[0][:, m, :], whole[:, m, :], ACT.Copy).then_inc(high_cut[m], 1)

                def cut_mid(s, m):
                    act.wait_ge(high_off[m], s.n + 1)
                    nc.scalar.activation(part[1][:, m, :], whole[:, m, :], ACT.Copy).then_inc(mid_cut[m], 1)

                def before():
                    act.wait_ge(consts_in, 16 * NCONST)
                    for k in range(XU):
                        x_empty(Step(0, 0), k)

                def body(s, has_x, has_l):
                    z = s + (-1)

                    def x(k):
                        if has_x:
                            x_empty(s + 1, k)
                    z_empty(z, 0)
                    z_empty(z, 1)
                    x(0)
                    x(1)
                    cut_high(s, 0)
                    exponent(s, 0)
                    exponent(s, 1)
                    x(2)
                    x(3)
                    cut_high(s, 1)
                    y_empty(s, "P0a")
                    y_empty(s, "P0b")
                    z_empty(z, 2)
                    y_empty(s, "O0")
                    x(4)
                    cut_mid(s, 0)
                    y_empty(s, "P1a")
                    y_empty(s, "P1b")
                    z_empty(z, 3)
                    y_empty(s, "O1")
                    x(5)
                    cut_mid(s, 1)
                    x(6)
                    x(7)

                def after():
                    for k in range(ZU):
                        z_empty(Step(NST // 2 - 1, 1), k)

                run(act, body, before, after)

            @block.vector
            def _(dve):
                L_LINKS, Y_LINKS = 2, TI * (2 + 8)

                def linker(base):
                    count = [0]

                    def link(ins, by_stats=False):
                        count[0] += 1
                        ins.then_inc(dve_link, 1)
                        if by_stats:
                            wait_apart(dve, dve_link, base + count[0], consts_in, 16 * NCONST)
                        else:
                            dve.wait_ge(dve_link, base + count[0])
                    return link, count

                def normalise(s, base):
                    link, count = linker(base)
                    q = s + (-1)
                    dve.wait_ge(x_loaded[s.par], 16 * (s.j + 1))
                    for i in range(TI):
                        last = nc.vector.bn_stats(st_x[:, i, :], x_in[:, s.par, i, :])
                    link(last, True)
                    for i in range(TI):
                        last = nc.vector.bn_aggr(ag_x[:, i, :], st_x[:, i, :])
                    link(last)
                    if q.exists():
                        dve.wait_ge(rstd_x, q.n + 1)
                    nc.vector.tensor_scalar(ve_x[:], ag_x[:, :, 1], EPS, None, ALU.add).then_inc(var_x, 1)
                    dve.wait_ge(rstd_x, s.n + 1)
                    if q.exists():
                        dve.wait_ge(x_filled, XU * q.n + 2)
                    for i in range(TI):
                        last = nc.vector.tensor_scalar(n1[:, i, :], x_in[:, s.par, i, :], ag_x[:, i, 0:1],
                                                       rs_x[:, i:i + 1], ALU.subtract, ALU.mult)
                    last.then_inc(n1_ready, 1)
                    assert count[0] == L_LINKS

                def softmax_shift(s, i, link):
                    q = s + (-1)
                    dve.wait_ge(y_filled, YU * s.n + yi(f"S{i}") + 1)
                    if q.exists():
                        dve.wait_ge(probs_ready, 2 * q.n + i + 1)
                    nc.vector.scalar_tensor_tensor(
                        out=scores[:, i], in0=bank_y(yi(f"S{i}")).rearrange("p (h m) -> p h m", h=H),
                        scalar=float(HD) ** -0.5, in1=mask[:].unsqueeze(1).broadcast_to([P, H, NODES]),
                        op0=ALU.mult, op1=ALU.add).then_inc(y_emptied_dve, 1)
                    dve.wait_ge(y_emptied_dve, NDVE * s.n + dve_rank(f"S{i}"))
                    link(nc.vector.tensor_reduce(top[:, i, :], scores[:, i], AX.X, ALU.max))
                    nc.vector.tensor_tensor(scores[:, i], scores[:, i],
                                            top[:, i, :].unsqueeze(2).broadcast_to([P, H, NODES]),
                                            ALU.subtract).then_inc(shifted, 1)

                def softmax_total(s, i, link):
                    dve.wait_ge(exp_done, TI * s.n + i + 1)
                    link(nc.vector.tensor_reduce(total[:, i, :], scores[:, i], AX.X, ALU.add))
                    nc.vector.reciprocal(inv[:, i, :], total[:, i, :]).then_inc(inv_ready, 1)

                def gate_total(s, k):
                    if not s.exists():
                        return
                    dve.wait_ge(z_emptied, ZU * s.n + k + 1)
                    nc.vector.tensor_reduce(
                        gate_sum[:, 2 * (k - 2):2 * (k - 2) + 2, bass.ds(4 * s.n, 4)],
                        gate_h[:, k - 2].rearrange("p m (b n) -> p m b n", n=NODES), AX.X,
                        ALU.add).then_inc(gate_summed, 1)

                def norm(s, i, which, src, link):
                    c = 2 * i + which
                    q = s + (-1)
                    link(nc.vector.bn_stats(st_y[:, c, :], src), True)
                    link(nc.vector.bn_aggr(ag_y[:, c, :], st_y[:, c, :]))
                    if q.exists():
                        dve.wait_ge(rstd_y, 4 * q.n + c + 1)
                    nc.vector.tensor_scalar(ve_y[:, c:c + 1], ag_y[:, c, 1:2], EPS, None, ALU.add).then_inc(var_y, 1)
                    dve.wait_ge(rstd_y, 4 * s.n + c + 1)
                    return ag_y[:, c, 0:1], rs_y[:, c:c + 1]

                def finish(s, i, link):
                    q = s + (-1)
                    dve.wait_ge(y_filled, YU * s.n + yi(f"R{i}") + 1)
                    first = nc.vector.tensor_tensor(o2[:, i, :], bank_y(yi(f"R{i}")), bproj[:], ALU.add)
                    first.then_inc(y_emptied_dve, 1)
                    dve.wait_ge(y_emptied_dve, NDVE * s.n + dve_rank(f"R{i}"))
                    mean, rstd = norm(s, i, 0, o2[:, i, :], link)
                    link(nc.vector.tensor_scalar(ln[:, i, :], o2[:, i, :], mean, rstd, ALU.subtract, ALU.mult))
                    link(nc.vector.tensor_tensor(ln[:, i, :], ln[:, i, :], gamma[:], ALU.mult))
                    link(nc.vector.tensor_tensor(ln[:, i, :], ln[:, i, :], beta[:], ALU.add))
                    link(nc.vector.tensor_tensor(ln[:, i, :], ln[:, i, :], o2[:, i, :], ALU.add))
                    dve.wait_ge(res_loaded, 16 * (s.n + 1))
                    if q.exists():
                        dve.wait_ge(x1_stored, 16 * (q.n + 1))
                        dve.wait_ge(n2_stored, 16 * (q.n + 1))
                        dve.wait_ge(z_filled, ZU * q.n + 2)
                    nc.vector.tensor_tensor(x1[:, i, :], x_res[:, i, :], ln[:, i, :], ALU.add).then_inc(x1_ready, 1)
                    dve.wait_ge(x1_ready, TI * s.n + i + 1)
                    mean, rstd = norm(s, i, 1, x1[:, i, :], link)
                    nc.vector.tensor_scalar(n2[:, i, :], x1[:, i, :], mean, rstd, ALU.subtract,
                                            ALU.mult).then_inc(n2_ready, 1)

                def take_high(s, m):
                    dve.wait_ge(high_cut[m], s.n + 1)
                    nc.vector.tensor_tensor(whole[:, m, :], whole[:, m, :], part[0][:, m, :],
                                            ALU.subtract).then_inc(high_off[m], 1)

                def cut_low(s, m):
                    dve.wait_ge(mid_cut[m], s.n + 1)
                    nc.vector.tensor_tensor(part[2][:, m, :], whole[:, m, :], part[1][:, m, :],
                                            ALU.subtract).then_inc(low_cut[m], 1)

                def before():
                    nc.vector.memset(zero[:], 0.0).then_inc(zero_set, 1)
                    nc.vector.memset(power[:], -0.5).then_inc(consts_set, 1)
                    nc.vector.memset(probs[:], 0.0).then_inc(consts_set, 1)
                    dve.wait_ge(consts_in, 16 * NCONST)
                    nc.vector.tensor_scalar(mask[:], adj[:], 0.0, NEG, ALU.is_equal, ALU.mult).then_inc(consts_set, 1)
                    dve.wait_ge(consts_set, 3)
                    normalise(Step(0, 0), 0)
                    normalise(Step(0, 1), L_LINKS)

                def body(s, has_x, has_l):
                    base = (L_LINKS + Y_LINKS) * s.n + 2 * L_LINKS
                    if not has_x:
                        base -= L_LINKS
                    z = s + (-1)
                    link, count = linker(base)
                    for i in range(TI):
                        softmax_shift(s, i, link)
                    take_high(s, 0)
                    for i in range(TI):
                        softmax_total(s, i, link)
                    take_high(s, 1)
                    gate_total(z, 2)
                    gate_total(z, 3)
                    for i in range(TI):
                        cut_low(s, i)
                        finish(s, i, link)
                    assert count[0] == Y_LINKS
                    if has_l:
                        normalise(s + 2, base + count[0])

                def after():
                    gate_total(Step(NST // 2 - 1, 1), 2)
                    gate_total(Step(NST // 2 - 1, 1), 3)
                    dve.wait_ge(gate_summed, 2 * NST)

                run(dve, body, before, after)

            @block.gpsimd
            def _(pool):
                def power_x(s):
                    pool.wait_ge(var_x, s.n + 1)
                    if (s + (-1)).exists():
                        pool.wait_ge(n1_ready, s.n)
                    nc.gpsimd.tensor_tensor(rs_x[:], ve_x[:], power[:], ALU.pow).then_inc(rstd_x, 1)

                def scale(s, i):
                    q = s + (-1)
                    pool.wait_ge(inv_ready, TI * s.n + i + 1)
                    if q.exists():
                        pool.wait_ge(y_filled, YU * q.n + yi("P1" + "ab"[i]) + 1)
                    for g in range(2):
                        r = slice(g * NODES, (g + 1) * NODES)
                        for tile in range(TI):
                            hs = slice(tile * (H // 2), (tile + 1) * (H // 2))
                            last = nc.gpsimd.tensor_tensor(
                                probs[r, tile, i, :, g * NODES:(g + 1) * NODES], scores[r, i, hs],
                                inv[r, i, hs].unsqueeze(2).broadcast_to([NODES, H // 2, NODES]), ALU.mult)
                    last.then_inc(probs_ready, 1)

                def power_y(s, c):
                    pool.wait_ge(var_y, 4 * s.n + c + 1)
                    nc.gpsimd.tensor_tensor(rs_y[:, c:c + 1], ve_y[:, c:c + 1], power[:, 0:1],
                                            ALU.pow).then_inc(rstd_y, 1)

                def before():
                    pool.wait_ge(consts_set, 3)
                    power_x(Step(0, 0))
                    power_x(Step(0, 1))

                def body(s, has_x, has_l):
                    scale(s, 0)
                    scale(s, 1)
                    for c in range(4):
                        power_y(s, c)
                    if has_l:
                        power_x(s + 2)

                run(pool, body, before, lambda: None)


def gates(nc, t, keep):
    with ExitStack() as ctx:
        def sb(name, shape, dt=F32):
            return ctx.enter_context(nc.sbuf_tensor(name, shape, dt))

        def sem(name):
            return ctx.enter_context(nc.semaphore(name))

        fc2 = sb("fc2", [P, KD, P])
        fc2_b = sb("fc2_b", [P, 1])
        sel = sb("sel", [P, 8])
        sel9 = sb("sel9", [E + 1, 2])
        g = sb("g", [P, GRAPHS])
        rest = sb("g_rest", [P, GRAPHS])
        part = [sb(f"g_part{k}", [P, GRAPHS], BF16) for k in range(3)]
        mix = sb("g_mix", [P, 2, GRAPHS])
        tvb1 = sb("tvb1", [E + 1, F])
        lnp = sb("lnp", [E, 2, D])
        lnq = sb("lnq", [E, 2, D])
        lnr = sb("lnr", [P, 2, D])
        ones = sb("ones", [E, P])
        ps = ctx.enter_context(nc.psum_tensor("ps_g", [P, 8, 512], F32))
        loaded, cleared, filled, cut, emptied = sem("g_loaded"), sem("g_cleared"), sem("g_filled"), sem("g_cut"), sem("g_emptied")
        gate_sum, gblk, g9, b1m, lnw = keep["gate_sum"], keep["gblk"], keep["g9"], keep["b1m"], keep["lnw"]
        nload = [0]

        with nc.Block() as block:
            @block.sync
            def _(sp):
                def load(dst, src):
                    sp.dma_start(dst, src).then_inc(loaded, 16)
                    nload[0] += 1
                sp.wait_ge(cleared, 3)
                for half in range(2):
                    for c in range(PAIRS):
                        at = half * HALF + c * E
                        load(fc2[:, :, at:at + E], t["fc2T"].rearrange("(k p) e -> p k e", p=P))
                        load(fc2_b[at:at + E, :], t["fc2_b"])
                load(sel[:], t["sel"])
                load(sel9[:], t["sel9"])
                load(tvb1[0:E, :], t["tvb1"])
                load(tvb1[E:E + 1, :], t["b1"].unsqueeze(0))
                load(keep["tvb2"][0:E, :], t["tvb2"])
                load(keep["tvb2"][E:E + 1, :], t["b2"].unsqueeze(0))
                for m, (w, tvw) in enumerate((("ln_g", "tv_ln_g"), ("ln_b", "tv_ln_b"))):
                    load(lnp[:, m, :], t[tvw])
                    load(lnq[:, m, :], t[w].partition_broadcast(E))
                    load(lnr[:, m, :], t[w].partition_broadcast(P))

            NLOAD = 2 * PAIRS * 2 + 6 + 6

            @block.vector
            def _(dve):
                nc.vector.memset(fc2[:], 0.0).then_inc(cleared, 1)
                nc.vector.memset(fc2_b[:], 0.0).then_inc(cleared, 1)
                nc.vector.memset(ones[:], 1.0).then_inc(cleared, 1)
                dve.wait_ge(loaded, 16 * NLOAD)
                count = [0]

                def link(ins):
                    count[0] += 1
                    ins.then_inc(cut, 1)
                    dve.wait_ge(cut, count[0])

                link(nc.vector.tensor_tensor(lnp[:], lnp[:], lnq[:], ALU.subtract))
                dve.wait_ge(filled, 1)
                link(nc.vector.tensor_scalar(g[:], ps[:, 0, 0:GRAPHS], 1.0 / NODES, fc2_b[:, 0:1],
                                             ALU.mult, ALU.add))
                link(nc.vector.tensor_scalar(g9[:], g[0:E + 1, :], sel9[:, 0:1], sel9[:, 1:2],
                                             ALU.mult, ALU.add))
                link(nc.vector.tensor_copy(part[0][:], g[:]))
                link(nc.vector.tensor_tensor(rest[:], g[:], part[0][:], ALU.subtract))
                link(nc.vector.tensor_copy(part[1][:], rest[:]))
                link(nc.vector.tensor_tensor(part[2][:], rest[:], part[1][:], ALU.subtract))
                for half in range(2):
                    one = sel[:, 4 * half + 3:4 * half + 4]
                    link(nc.vector.tensor_scalar(mix[:, 0, :], part[0][:], sel[:, 4 * half:4 * half + 1], one,
                                                 ALU.mult, ALU.add))
                    link(nc.vector.scalar_tensor_tensor(out=mix[:, 1, :], in0=part[1][:],
                                                        scalar=sel[:, 4 * half + 1:4 * half + 2],
                                                        in1=mix[:, 0, :], op0=ALU.mult, op1=ALU.add))
                    link(nc.vector.scalar_tensor_tensor(
                        out=gblk[:, :, half, :], in0=part[2][:].rearrange("p (g b) -> p g b", b=GB),
                        scalar=sel[:, 4 * half + 2:4 * half + 3],
                        in1=mix[:, 1, :].rearrange("p (g b) -> p g b", b=GB), op0=ALU.mult, op1=ALU.add))
                for m in range(2):
                    dve.wait_ge(filled, 2 + m)
                    link(nc.vector.scalar_tensor_tensor(out=lnw[:, m, :], in0=ps[:, 1 + m, :], scalar=LN_MERGE,
                                                        in1=lnr[:, m, :], op0=ALU.mult, op1=ALU.add))
                for k in range(4):
                    dve.wait_ge(filled, 4 + k)
                    link(nc.vector.tensor_copy(b1m[:, 4 * k:4 * k + 4, :],
                                               ps[:, 3 + k, :].rearrange("p (a b) -> p a b", b=GRAPHS)))

            @block.tensor
            def _(pe):
                pe.wait_ge(loaded, 16 * NLOAD)
                for c in range(KD):
                    last = pe.matmul(ps[:, 0, 0:GRAPHS], fc2[:, c, :], gate_sum[:, c, :],
                                     start=(c == 0), stop=(c == KD - 1))
                last.then_inc(filled, 1)
                pe.wait_ge(cut, 1)
                for m in range(2):
                    pe.matmul(ps[:, 1 + m, :], ones[:], lnp[:, m, :], start=True, stop=True).then_inc(filled, 1)
                pe.wait_ge(cut, 3)
                for k in range(4):
                    for a in range(4):
                        last = pe.matmul(ps[:, 3 + k, a * GRAPHS:(a + 1) * GRAPHS],
                                         tvb1[:, (4 * k + a) * P:(4 * k + a + 1) * P], g9[:],
                                         start=True, stop=True)
                    last.then_inc(filled, 1)


def feed(nc, t, keep):
    gblk, g9, b1m, lnw, ident = keep["gblk"], keep["g9"], keep["b1m"], keep["lnw"], keep["ident"]
    tvb2 = keep["tvb2"]
    with ExitStack() as ctx:
        def sb(name, shape, dt=F32):
            return ctx.enter_context(nc.sbuf_tensor(name, shape, dt))

        def sem(name):
            return ctx.enter_context(nc.semaphore(name))

        SLOT = 8192
        slot = sb("slot", [P, 2, SLOT])
        nT = sb("nT", [P, KD, GT])
        acc = sb("acc", [P, PR, D])
        pieces = sb("pieces", [KROWS, 4, PIECE], BF16)
        hid = sb("hid", [P, PR, P])
        hT = sb("hT", [P, GT])
        gnow = sb("gnow", [KROWS, 2 * GB], BF16)
        bnow = sb("bnow", [P, GB])
        gtok = sb("gtok", [E + 1, 2, P])
        x_row = sb("x_row", [P, 2, D])
        y_row = sb("y_row", [P, 2, D])
        st, ag, ve, rs = sb("st_f", [P, 6]), sb("ag_f", [P, 2]), sb("ve_f", [P, 1]), sb("rs_f", [P, 1])
        power = sb("power_f", [P, 1])
        ps_m = ctx.enter_context(nc.psum_tensor("ps_m", [P, 2, 1024], F32))
        ps_w = ctx.enter_context(nc.psum_tensor("ps_w", [P, 4, 512], F32))

        nT_loaded, acc_loaded = sem("nT_loaded"), sem("acc_loaded")
        piece_in = [sem(f"piece_in{k}") for k in range(4)]
        merged = sem("merged")
        kept_act, kept_dve = sem("kept_act"), sem("kept_dve")
        work = sem("work")
        work_act, work_dve = sem("work_act"), sem("work_dve")
        g_ready, b_ready, gtok_ready = sem("g_ready"), sem("b_ready"), sem("gtok_ready")
        power_set = sem("power_set")
        var_f, rstd_f = sem("var_f"), sem("rstd_f")
        x_in = [sem("x_in0"), sem("x_in1")]
        y_out = [sem("y_out0"), sem("y_out1")]
        y_ready = sem("y_ready")
        link_f = sem("link_f")

        INIT, NL1, NTR, NL2 = PR, 4, 4, 16
        PER_T = NL1 + NTR + NL2
        PER_G = INIT + FT * PER_T
        UNITS = 4 * FT
        KEPT = 1
        s1 = t["s1"].rearrange("(p v c) -> v p c", p=KROWS, c=PIECE)
        s2 = t["s2"].rearrange("(p v c) -> v p c", p=KROWS, c=PIECE)
        nTt = t["n2T"].rearrange("k p (g c) -> g p k c", c=GT)
        n2t = t["n2"].rearrange("(g i p) d -> g p i d", i=PR, p=P)
        x1t = t["x1"].rearrange("(i p) d -> i p d", p=P)
        yt = t["y"].rearrange("(i p) d -> i p d", p=P)

        with nc.Block() as block:
            @block.sync
            def _(sp):
                def unit(u, src, at):
                    for k in range(4):
                        sp.wait_ge(merged, 8 * u + 2 * k + 2)
                        sp.dma_start(pieces[:, k, :], src[bass.ds(at + k, 1)].rearrange("a p c -> (a p) c")
                                     ).then_inc(piece_in[k], 16)

                with sp.Fori(0, GROUPS) as g:
                    with sp.Fori(0, FT) as f:
                        u = g * UNITS + f * 4
                        unit(u, s1, f * 8)
                        unit(u + 1, s1, f * 8 + 4)
                        unit(u + 2, s2, f * 4)
                        unit(u + 3, s2, f * 4 + 4 * FT)

            @block.tensor
            def _(pe):
                def merge(u, second):
                    for q in range(8):
                        if q % 2 == 0:
                            pe.wait_ge(piece_in[q // 2], 16 * (u + 1))
                        pe.wait_ge(kept_act if q % 2 == 0 else kept_dve, KEPT + 4 * u + q // 2)
                        for r in range(16):
                            if second:
                                at = ((q % 2) * 16 + r) * P
                            else:
                                at = (r % 8) * D + ((q % 2) * 2 + r // 8) * P
                            last = pe.matmul(ps_m[:, q % 2, r * 64:(r + 1) * 64], pieces[:, q // 2, at:at + P],
                                             gnow[:], start=True, stop=True)
                        last.then_inc(merged, 1)

                def kept(u):
                    pe.wait_ge(kept_act, KEPT + 4 * u + 4)
                    pe.wait_ge(kept_dve, KEPT + 4 * u + 4)

                def work_free(g, f, k):
                    a = (g * FT + f) * (NL1 + NTR)
                    d = g * (INIT + FT * NL2) + INIT + f * NL2 + 4
                    if k < 4:
                        pe.wait_ge(work_dve, d - 4 + k + 1)
                    elif k < 12:
                        pe.wait_ge(work_act, a + k - 4 + 1)
                    else:
                        pe.wait_ge(work_dve, d + k - 12 + 1)

                def first_layer(g, f, ab, s):
                    kept(g * UNITS + f * 4 + ab)
                    w = slot[:, s, :].rearrange("p (k b f) -> p k b f", k=KD, b=GB)
                    for bank in range(2):
                        k = 2 * ab + bank
                        work_free(g, f, k)
                        for b in range(16):
                            bb, r = bank * 16 + b, NODES * (b % 2)
                            for c in range(KD):
                                last = pe.matmul(ps_w[r:r + NODES, k % 4, (b // 2) * 64:(b // 2 + 1) * 64],
                                                 nT[:, c, bb * NODES:(bb + 1) * NODES], w[:, c, bb, :],
                                                 start=(c == 0), stop=(c == KD - 1))
                        last.then_inc(work, 1)

                def turn(g, f):
                    for q in range(4):
                        k = NL1 + q
                        if q == 0:
                            pe.wait_ge(work_act, (g * FT + f) * (NL1 + NTR) + NL1)
                        else:
                            work_free(g, f, k)
                        for p in range(4):
                            last = pe.transpose(ps_w[:, k % 4, p * P:(p + 1) * P], hid[:, 4 * q + p, :], ident[:])
                        last.then_inc(work, 1)

                def second_layer(g, f, cd, s):
                    kept(g * UNITS + f * 4 + 2 + cd)
                    w = slot[:, s, :].rearrange("p (b d) -> p b d", b=GB)
                    for q in range(8):
                        k = NL1 + NTR + 8 * cd + q
                        work_free(g, f, k)
                        if cd == 0 and q in (4, 6):
                            pe.wait_ge(work_act, (g * FT + f) * (NL1 + NTR) + NL1 + q // 2 + 1)
                        for b in range(4):
                            bb, r = 4 * q + b, NODES * (b % 2)
                            last = pe.matmul(ps_w[r:r + NODES, k % 4, (b // 2) * 256:(b // 2 + 1) * 256],
                                             hT[:, bb * NODES:(bb + 1) * NODES], w[:, bb, :], start=True, stop=True)
                        last.then_inc(work, 1)

                def tile(g, f, more):
                    u = g * UNITS + f * 4
                    merge(u + 1, False)
                    first_layer(g, f, 0, 0)
                    merge(u + 2, True)
                    first_layer(g, f, 1, 1)
                    turn(g, f)
                    merge(u + 3, True)
                    second_layer(g, f, 0, 0)
                    if more:
                        merge(u + 4, False)
                    second_layer(g, f, 1, 1)

                pe.sem_inc(merged, 8)
                with pe.Fori(0, GROUPS) as g:
                    for i in range(INIT):
                        pe.wait_ge(work_dve, g * (INIT + FT * NL2) + i + 1)
                        pe.wait_ge(gtok_ready, g * INIT + i + 1)
                        pe.matmul(ps_w[:, i % 4, :], gtok[:, i % 2, :], tvb2[:], start=True, stop=True).then_inc(work, 1)
                    pe.wait_ge(g_ready, g + 1)
                    merge(g * UNITS, False)
                    wait_apart(pe, nT_loaded, 16 * (g + 1), power_set, 1)
                    with pe.Fori(0, FT - 1) as f:
                        tile(g, f, True)
                    tile(g, FT - 1, False)

            def keep_half(eng, copy, u, second, which, done):
                s = which["slot"]
                par = which["par"]
                for q in range(par, 8, 2):
                    eng.wait_ge(merged, 8 + 8 * u + q + 1)
                    if second:
                        src = ps_m[:, par, :].rearrange("p (r h b) -> p b h r", r=16, h=2)
                        dst = slot[:, s, :].rearrange("p (b h r) -> p b h r", b=GB, h=2)[:, :, :, 16 * q:16 * q + 16]
                        copy(dst, src).then_inc(done, 1)
                    else:
                        for m in range(2):
                            c = 2 * (q % 2) + m
                            src = ps_m[:, par, 512 * m:512 * (m + 1)].rearrange("p (r h b) -> p b h r", r=8, h=2)
                            dst = slot[:, s, :].rearrange("p (k b h r) -> p k b h r", k=KD, b=GB, h=2)[
                                :, c, :, :, 8 * (q // 2):8 * (q // 2) + 8]
                            last = copy(dst, src)
                        last.then_inc(done, 1)

            @block.scalar
            def _(act):
                def copy(dst, src):
                    return nc.scalar.activation(dst, src, ACT.Copy)

                def keep_unit(u, second, s):
                    keep_half(act, copy, u, second, {"slot": s, "par": 0}, kept_act)

                def first_out(g, f, ab):
                    for bank in range(2):
                        k = 2 * ab + bank
                        act.wait_ge(work, g * PER_G + INIT + f * PER_T + k + 1)
                        nc.scalar.activation(hid[:, 8 * bank:8 * bank + 8, 64 * ab:64 * ab + 64],
                                             ps_w[:, k % 4, :].rearrange("p (i f) -> p i f", f=64),
                                             ACT.Copy).then_inc(work_act, 1)

                def relu(g, f):
                    for q in range(4):
                        k = NL1 + q
                        act.wait_ge(work, g * PER_G + INIT + f * PER_T + k + 1)
                        for b in range(8):
                            bb = 8 * q + b
                            last = nc.scalar.activation(hT[:, bb * NODES:(bb + 1) * NODES],
                                                        ps_w[:, k % 4, b * NODES:(b + 1) * NODES], ACT.Relu,
                                                        bias=bnow[:, bb:bb + 1])
                        last.then_inc(work_act, 1)

                def tile(g, f, more):
                    u = g * UNITS + f * 4
                    nc.scalar.activation(bnow[:].unsqueeze(1), b1m[:, bass.ds(f, 1), bass.ds(g * GB, GB)],
                                         ACT.Copy).then_inc(b_ready, 1)
                    act.wait_ge(b_ready, g * FT + f + 1)
                    keep_unit(u + 1, False, 1)
                    first_out(g, f, 0)
                    keep_unit(u + 2, True, 0)
                    first_out(g, f, 1)
                    relu(g, f)
                    keep_unit(u + 3, True, 1)
                    if more:
                        keep_unit(u + 4, False, 0)

                act.sem_inc(kept_act, KEPT)
                with act.Fori(0, GROUPS) as g:
                    act.wait_ge(merged, 8 + 8 * UNITS * g)
                    nc.scalar.activation(gnow[:].rearrange("p (h b) -> p h b", b=GB).unsqueeze(1),
                                         gblk[0:KROWS, bass.ds(g, 1)], ACT.Copy).then_inc(g_ready, 1)
                    keep_unit(g * UNITS, False, 0)
                    with act.Fori(0, FT - 1) as f:
                        tile(g, f, True)
                    tile(g, FT - 1, False)

            @block.vector
            def _(dve):
                LINKS = PR * 5

                def copy(dst, src):
                    return nc.vector.tensor_copy(dst, src)

                def keep_unit(u, second, s):
                    keep_half(dve, copy, u, second, {"slot": s, "par": 1}, kept_dve)

                def add_second(g, f, cd):
                    for q in range(8):
                        k = NL1 + NTR + 8 * cd + q
                        dve.wait_ge(work_dve, 4 + g * (INIT + FT * NL2) + INIT + f * NL2 + 8 * cd + q - 8)
                        dve.wait_ge(work, g * PER_G + INIT + f * PER_T + k + 1)
                        part = acc[:, 2 * q:2 * q + 2, 256 * cd:256 * cd + 256]
                        nc.vector.tensor_tensor(part, ps_w[:, k % 4, :].rearrange("p (i d) -> p i d", d=256),
                                                part, ALU.add).then_inc(work_dve, 1)

                def tile(g, f, more):
                    u = g * UNITS + f * 4
                    keep_unit(u + 1, False, 1)
                    keep_unit(u + 2, True, 0)
                    keep_unit(u + 3, True, 1)
                    add_second(g, f, 0)
                    if more:
                        keep_unit(u + 4, False, 0)
                    add_second(g, f, 1)

                def finish(g):
                    count = [0]
                    base = g * LINKS

                    def link(ins, by_stats=False):
                        count[0] += 1
                        ins.then_inc(link_f, 1)
                        if by_stats:
                            wait_apart(dve, link_f, base + count[0], power_set, 1)
                        else:
                            dve.wait_ge(link_f, base + count[0])

                    dve.wait_ge(work_dve, 4 + (g + 1) * (INIT + FT * NL2))
                    for i in range(PR):
                        b = i % 2
                        link(nc.vector.bn_stats(st[:], acc[:, i, :]), True)
                        link(nc.vector.bn_aggr(ag[:], st[:]))
                        nc.vector.tensor_scalar(ve[:], ag[:, 1:2], EPS, None, ALU.add).then_inc(var_f, 1)
                        dve.wait_ge(rstd_f, g * PR + i + 1)
                        link(nc.vector.tensor_scalar(acc[:, i, :], acc[:, i, :], ag[:, 0:1], rs[:, 0:1],
                                                     ALU.subtract, ALU.mult))
                        link(nc.vector.tensor_tensor(acc[:, i, :], acc[:, i, :], lnw[:, 0, :], ALU.mult))
                        link(nc.vector.tensor_tensor(acc[:, i, :], acc[:, i, :], lnw[:, 1, :], ALU.add))
                        dve.wait_ge(x_in[b], 16 * (g * (PR // 2) + i // 2 + 1))
                        if i >= 2:
                            dve.wait_ge(y_out[b], 16 * (g * (PR // 2) + i // 2))
                        nc.vector.tensor_tensor(y_row[:, b, :], acc[:, i, :], x_row[:, b, :],
                                                ALU.add).then_inc(y_ready, 1)
                    assert count[0] == LINKS

                nc.vector.memset(power[:], -0.5).then_inc(power_set, 1)
                dve.sem_inc(work_dve, 4)
                dve.sem_inc(kept_dve, KEPT)
                dve.sem_inc(y_ready, 1)
                with dve.Fori(0, GROUPS) as g:
                    dve.wait_ge(acc_loaded, 16 * (g + 1))
                    for i in range(INIT):
                        if i >= 2:
                            dve.wait_ge(work, g * PER_G + i - 1)
                        for h in range(2):
                            last = nc.vector.tensor_copy(
                                gtok[:, i % 2, h * NODES:(h + 1) * NODES],
                                g9[:, bass.ds(g * GB + 2 * i + h, 1)].broadcast_to([E + 1, NODES]))
                        last.then_inc(gtok_ready, 1)
                        if i >= 1:
                            add_bias(nc, dve, work, work_dve, acc, ps_w, i - 1, g * PER_G)
                    add_bias(nc, dve, work, work_dve, acc, ps_w, INIT - 1, g * PER_G)
                    keep_unit(g * UNITS, False, 0)
                    with dve.Fori(0, FT - 1) as f:
                        tile(g, f, True)
                    tile(g, FT - 1, False)
                    finish(g)

            @block.gpsimd
            def _(pool):
                def rows(g):
                    def load(i):
                        pool.dma_start(x_row[:, i % 2, :], x1t[bass.ds(g * PR + i, 1)].rearrange("a p d -> (a p) d")
                                       ).then_inc(x_in[i % 2], 16)
                    load(0)
                    load(1)
                    for i in range(PR):
                        pool.wait_ge(var_f, g * PR + i + 1)
                        nc.gpsimd.tensor_tensor(rs[:], ve[:], power[:], ALU.pow).then_inc(rstd_f, 1)
                        wait_apart(pool, y_ready, g * PR + i + 2, power_set, 1)
                        pool.dma_start(yt[bass.ds(g * PR + i, 1)].rearrange("a p d -> (a p) d"),
                                       y_row[:, i % 2, :]).then_inc(y_out[i % 2], 16)
                        if i + 2 < PR:
                            load(i + 2)
                    for b in range(2):
                        wait_apart(pool, y_out[b], 16 * (g + 1) * (PR // 2), power_set, 1)

                def load_nT(g):
                    pool.dma_start(nT[:], nTt[bass.ds(g, 1)].rearrange("g p k c -> (g p) k c")).then_inc(nT_loaded, 16)

                def group(g, more):
                    wait_apart(pool, y_ready, g * PR + 1, power_set, 1)
                    pool.dma_start(acc[:], n2t[bass.ds(g, 1)].rearrange("g p i d -> (g p) i d")).then_inc(acc_loaded, 16)
                    if more:
                        wait_apart(pool, work, g * PER_G + INIT + (FT - 1) * PER_T + NL1, power_set, 1)
                        load_nT(g + 1)
                    rows(g)

                pool.wait_ge(power_set, 1)
                load_nT(0)
                with pool.Fori(0, GROUPS - 1) as g:
                    group(g, True)
                group(GROUPS - 1, False)
                for b in range(2):
                    pool.wait_ge(y_out[b], 16 * GROUPS * PR // 2)


def add_bias(nc, dve, work, work_dve, acc, ps_w, i, base):
    dve.wait_ge(work, base + i + 1)
    nc.vector.tensor_tensor(acc[:, i, :], ps_w[:, i % 4, :], acc[:, i, :], ALU.add).then_inc(work_dve, 1)


def graph_ffn(nc, t):
    with ExitStack() as ctx:
        def sb(name, shape, dt=F32):
            return ctx.enter_context(nc.sbuf_tensor(name, shape, dt))

        keep = {
            "ident": sb("ident", [P, P]),
            "gate_sum": sb("gate_sum", [P, KD, GRAPHS]),
            "gblk": sb("gblk", [P, GROUPS, 2, GB], BF16),
            "g9": sb("g9", [E + 1, GRAPHS]),
            "b1m": sb("b1m", [P, FT, GRAPHS]),
            "lnw": sb("lnw", [P, 2, D]),
            "tvb2": sb("tvb2", [E + 1, D]),
        }
        ident_in = ctx.enter_context(nc.semaphore("ident_in"))
        with nc.Block() as block:
            @block.sync
            def _(sp):
                sp.dma_start(keep["ident"][:], t["ident"]).then_inc(ident_in, 16)
                sp.wait_ge(ident_in, 16)
        attend(nc, t, keep)
        gates(nc, t, keep)
        feed(nc, t, keep)


def kernel(**inputs):
    import concourse.bacc as bacc
    from concourse.bass_utils import run_bass_kernel_spmd

    i = {k: np.asarray(v) for k, v in inputs.items()}

    def rows_of(w, matrix):
        n = w.shape[0]
        if matrix == 1:
            return w.reshape(n, F // 64, 2, 32, D).transpose(0, 2, 1, 3, 4).reshape(n, 2, HROW)
        return w.reshape(n, 2, 2, P, FT, P).transpose(0, 2, 1, 4, 3, 5).reshape(n, 2, HROW)

    def shares(w, matrix, count):
        r = rows_of(w, matrix)
        return r.reshape(r.shape[0], 2, count, -1).transpose(0, 2, 1, 3).reshape(-1)

    sel9 = np.zeros((E + 1, 2), np.float32)
    sel9[:E, 0] = 1.0
    sel9[E, 1] = 1.0
    arrays = {
        "x": i["x"].reshape(TOK, D),
        "adj": i["adj"],
        "wqkv": i["L0_gnn_w_qkv"],
        "wproj": i["L0_gnn_w_proj"],
        "bproj": i["L0_gnn_b_proj"],
        "gamma": i["L0_gnn_ln_gamma"],
        "beta": i["L0_gnn_ln_beta"],
        "gfc1T": i["L0_ffn_gfc1_w"].T,
        "gfc1_b": i["L0_ffn_gfc1_b"].reshape(KD, P).T,
        "fc2T": i["L0_ffn_gfc2_w"].T,
        "fc2_b": i["L0_ffn_gfc2_b"].reshape(E, 1),
        "W1": shares(i["L0_ffn_W1"][None], 1, NST),
        "b1": i["L0_ffn_b1"],
        "W2": shares(i["L0_ffn_W2"][None], 2, NST),
        "b2": i["L0_ffn_b2"],
        "ln_g": i["L0_ffn_ln_g"],
        "ln_b": i["L0_ffn_ln_b"],
        "tvW1": shares(i["L0_ffn_tv_W1"], 1, NST // E),
        "tvb1": i["L0_ffn_tv_b1"],
        "tvW2": shares(i["L0_ffn_tv_W2"], 2, NST // E),
        "tvb2": i["L0_ffn_tv_b2"],
        "tv_ln_g": i["L0_ffn_tv_ln_g"],
        "tv_ln_b": i["L0_ffn_tv_ln_b"],
        "ident": np.eye(P, dtype=np.float32),
        "sel": selection(),
        "sel9": sel9,
    }
    arrays = {k: np.ascontiguousarray(v) for k, v in arrays.items()}
    nc = bacc.Bacc("TRN2", target_bir_lowering=False, num_devices=1)
    t = {}
    for name, a in arrays.items():
        t[name] = nc.dram_tensor(f"in_{name}", a.shape, mybir.dt.from_np(a.dtype), kind="ExternalInput").ap()
    t["y"] = nc.dram_tensor("out_y", (TOK, D), F32, kind="ExternalOutput").ap()
    for name, shape, dt in (("x1", (TOK, D), F32), ("n2", (TOK, D), F32), ("n2T", (KD, P, TOK), F32),
                            ("s1", (KROWS * HROW,), BF16), ("s2", (KROWS * HROW,), BF16)):
        t[name] = nc.dram_tensor(f"scratch_{name}", shape, dt, kind="Internal").ap()
    graph_ffn(nc, t)
    r = run_bass_kernel_spmd(nc, [{f"in_{k}": v for k, v in arrays.items()}], core_ids=[0])
    return r.results[0]["out_y"].reshape(GRAPHS, NODES, D)
```

```python
from contextlib import ExitStack

import concourse.bass as bass
import numpy as np
from concourse import mybir

P = 128
GRAPHS, NODES, D = 128, 64, 512
F, E, H = 2048, 8, 8
HD = D // H
TOK = GRAPHS * NODES
KD = D // P
EPS = 1e-5
LN_MERGE = 0.03
NEG = -1e30

T_PART = [0, 1, 2, 0, 1, 0]
G_PART = [0, 0, 0, 1, 1, 2]
PAIRS = len(T_PART)
BASE_ROW = PAIRS * E
HALF = 56
KROWS = 2 * HALF
MAT = F * D
HROW = MAT // 2

GB = 32
GROUPS = GRAPHS // GB
GT = GB * NODES
PR = GT // P
FT = F // P
UNIT = 16384
PIECE = UNIT // 4

ALU = mybir.AluOpType
ACT = mybir.ActivationFunctionType
AX = mybir.AxisListType
F32 = mybir.dt.float32
BF16 = mybir.dt.bfloat16


def wait_apart(eng, sem, value, met, met_value):
    if not isinstance(value, int):
        value = eng.to_reg(value)
        eng.wait_ge(met, met_value)
    eng.wait_ge(sem, value)


def selection():
    sel = np.zeros((P, 2, 4), np.float32)
    for half in range(2):
        for c in range(PAIRS):
            for e in range(E):
                sel[half * HALF + c * E + e, half, G_PART[c]] = 1.0
        for part in range(3):
            sel[half * HALF + BASE_ROW + part, half, 3] = 1.0
    return sel.reshape(P, 8)


class Step:

    def __init__(self, j, par):
        self.j, self.par = j, par
        self.n = 2 * j + par

    def __add__(self, k):
        q = self.par + k
        return Step(self.j + q // 2, q % 2)

    def exists(self):
        return not isinstance(self.n, int) or self.n >= 0


ST = 256
NST = TOK // ST
TI = ST // P
CUT_E = E * MAT // NST // P
CUT_B = MAT // NST // P
CUT = CUT_E + CUT_B


def attend(nc, t, keep):
    gate_sum = keep["gate_sum"]
    ident = keep["ident"]
    with ExitStack() as ctx:
        def sb(name, shape, dt=F32):
            return ctx.enter_context(nc.sbuf_tensor(name, shape, dt))

        def sem(name):
            return ctx.enter_context(nc.semaphore(name))

        wqkv = sb("wqkv", [P, KD, 3 * D])
        wproj = sb("wproj", [P, KD, D])
        gfc1 = sb("gfc1", [P, KD, D])
        gfc1_b = sb("gfc1_b", [P, KD])
        bproj = sb("bproj", [P, D])
        gamma = sb("gamma", [P, D])
        beta = sb("beta", [P, D])
        adj = sb("adj", [P, NODES])
        mask = sb("mask", [P, NODES])
        power = sb("power", [P, TI])
        x_in = sb("x_in", [P, 2, TI, D])
        x_res = sb("x_res", [P, TI, D])
        n1 = sb("n1", [P, TI, D])
        n1T = sb("n1T", [P, KD, ST])
        qkT = sb("qkT", [P, 2, 2 * KD, ST])
        v = sb("v", [P, 2, TI, D])
        scores = sb("scores", [P, 2, H, NODES])
        top = sb("top", [P, 2, H])
        total = sb("total", [P, 2, H])
        inv = sb("inv", [P, 2, H])
        probs = sb("probs", [P, TI, 2, H // 2, P])
        probsT = sb("probsT", [P, TI, H, P])
        oT = sb("oT", [P, TI, KD, P])
        o2 = sb("o2", [P, TI, D])
        ln = sb("ln", [P, TI, D])
        x1 = sb("x1", [P, TI, D])
        n2 = sb("n2", [P, TI, D])
        n2T = sb("n2T", [P, KD, ST])
        gate_h = sb("gate_h", [P, 2, 2, ST])
        whole = sb("whole", [P, 2, CUT])
        part = [sb(f"part{k}", [P, 2, CUT], BF16) for k in range(3)]
        zero = sb("zero", [P, 512], BF16)
        st_x, ag_x, rs_x = sb("st_x", [P, TI, 6]), sb("ag_x", [P, TI, 2]), sb("rs_x", [P, TI])
        ve_x = sb("ve_x", [P, TI])
        st_y, ag_y, rs_y = sb("st_y", [P, 2 * TI, 6]), sb("ag_y", [P, 2 * TI, 2]), sb("rs_y", [P, 2 * TI])
        ve_y = sb("ve_y", [P, 2 * TI])

        ps_x = ctx.enter_context(nc.psum_tensor("ps_x", [P, 4, 512], F32))
        ps_y = ctx.enter_context(nc.psum_tensor("ps_y", [P, 2, 512], F32))
        ps_z = ctx.enter_context(nc.psum_tensor("ps_z", [P, 2, 512], F32))

        consts_in, consts_set = sem("consts_in"), sem("consts_set")
        rest_added = sem("rest_added")
        x_loaded = [sem("x_loaded0"), sem("x_loaded1")]
        res_loaded = sem("res_loaded")
        x_filled, y_filled, z_filled = sem("x_filled"), sem("y_filled"), sem("z_filled")
        x_emptied = sem("x_emptied")
        y_emptied_act, y_emptied_dve = sem("y_emptied_act"), sem("y_emptied_dve")
        z_emptied = sem("z_emptied")
        gate_summed = sem("gate_summed")
        n1_ready, var_x, rstd_x = sem("n1_ready"), sem("var_x"), sem("rstd_x")
        shifted, exp_done, inv_ready, probs_ready = sem("shifted"), sem("exp_done"), sem("inv_ready"), sem("probs_ready")
        var_y, rstd_y = sem("var_y"), sem("rstd_y")
        x1_ready, n2_ready = sem("x1_ready"), sem("n2_ready")
        x1_stored, n2_stored, n2T_stored = sem("x1_stored"), sem("n2_stored"), sem("n2T_stored")
        dve_link = sem("dve_link")
        whole_in = [sem(f"whole_in{m}") for m in range(2)]
        high_cut = [sem(f"high_cut{m}") for m in range(2)]
        high_off = [sem(f"high_off{m}") for m in range(2)]
        mid_cut = [sem(f"mid_cut{m}") for m in range(2)]
        low_cut = [sem(f"low_cut{m}") for m in range(2)]
        parts_stored = [sem(f"parts_stored{m}") for m in range(2)]
        zero_set, zero_stored = sem("zero_set"), sem("zero_stored")

        rows_e = [t[f"s{m}"].rearrange("(h a p c) -> a h p c", h=2, p=64, c=CUT_E) for m in (1, 2)]
        rows_b = [t[f"s{m}"].rearrange("(h a p c) -> a h p c", h=2, p=64, c=CUT_B) for m in (1, 2)]
        BLOCKS_E = HROW // (64 * CUT_E)
        BLOCKS_B = HROW // (64 * CUT_B)
        STORES = 16 * (PAIRS + 3)

        XU, YU, ZU = 8, 10, 4
        Y_ORDER = ["S0", "S1", "P0a", "P0b", "O0", "P1a", "P1b", "R0", "O1", "R1"]
        Y_DVE = [u[0] in "SR" for u in Y_ORDER]
        NDVE = sum(Y_DVE)

        def yi(name):
            return Y_ORDER.index(name)

        def y_free(pe, s, k, needed=None):
            if needed is not None:
                rank = act_rank(needed)
                if not Y_DVE[k - 2]:
                    rank = max(rank, act_rank(Y_ORDER[k - 2]))
                pe.wait_ge(y_emptied_act, s.n * (YU - NDVE) + rank)
                if not Y_DVE[k - 2]:
                    return
            prev, back = (k - 2) % YU, k < 2
            ps = s + (-1) if back else s
            if not ps.exists():
                return
            rank = sum(1 for i in range(prev + 1) if Y_DVE[i] == Y_DVE[prev])
            if Y_DVE[prev]:
                wait_apart(pe, y_emptied_dve, ps.n * NDVE + rank, consts_in, 16 * NCONST)
            else:
                wait_apart(pe, y_emptied_act, ps.n * (YU - NDVE) + rank, consts_in, 16 * NCONST)

        def bank_y(k):
            return ps_y[:, k % 2, :]

        def act_rank(name):
            return sum(1 for i in range(yi(name) + 1) if not Y_DVE[i])

        def dve_rank(name):
            return sum(1 for i in range(yi(name) + 1) if Y_DVE[i])

        xt = t["x"].rearrange("(s i p) d -> s p i d", i=TI, p=P)
        x1t = t["x1"].rearrange("(s i p) d -> s p i d", i=TI, p=P)
        n2t = t["n2"].rearrange("(s i p) d -> s p i d", i=TI, p=P)
        n2Tt = t["n2T"].rearrange("k p (s c) -> s p k c", c=ST)

        def tile_of(dram, s):
            return dram[bass.ds(s.n, 1)].rearrange("s p i d -> (s p) i d")

        def run(engine, body, before, after):
            before()
            body(Step(0, 0), True, True)
            body(Step(0, 1), True, True)
            with engine.Fori(1, NST // 2 - 1) as j:
                body(Step(j, 0), True, True)
                body(Step(j, 1), True, True)
            body(Step(NST // 2 - 1, 0), True, False)
            body(Step(NST // 2 - 1, 1), False, False)
            after()

        NCONST = 9
        with nc.Block() as block:
            @block.sync
            def _(sp):
                def load_x(s):
                    q = s + (-2)
                    if q.exists():
                        sp.wait_ge(n1_ready, q.n + 1)
                    sp.dma_start(x_in[:, s.par], tile_of(xt, s)).then_inc(x_loaded[s.par], 16)

                def load_whole(s, m):
                    for src, at, n in ((t[f"tvW{m + 1}"], 0, CUT_E), (t[f"W{m + 1}"], CUT_E, CUT_B)):
                        src = src.rearrange("(s p c) -> s p c", p=P, c=n)
                        sp.dma_start(whole[:, m, at:at + n], src[bass.ds(s.n, 1)].rearrange("s p c -> (s p) c")
                                     ).then_inc(whole_in[m], 16)

                def store_parts(s, m):
                    wait_apart(sp, low_cut[m], s.n + 1, zero_set, 1)
                    for c in range(PAIRS):
                        sp.dma_start(rows_e[m][bass.ds(c * E * BLOCKS_E + s.n, 1)].rearrange("a h p c -> (a h) p c"),
                                     part[T_PART[c]][:, m, 0:CUT_E]).then_inc(parts_stored[m], 16)
                    for k in range(3):
                        sp.dma_start(rows_b[m][bass.ds((BASE_ROW + k) * BLOCKS_B + s.n, 1)
                                               ].rearrange("a h p c -> (a h) p c"),
                                     part[k][:, m, CUT_E:CUT]).then_inc(parts_stored[m], 16)

                def store_n2T(s):
                    sp.wait_ge(z_emptied, ZU * s.n + 2)
                    sp.dma_start(n2Tt[bass.ds(s.n, 1)].rearrange("s p k c -> (s p) k c"),
                                 n2T[:]).then_inc(n2T_stored, 16)

                def store_x1(s):
                    sp.wait_ge(x1_ready, TI * (s.n + 1))
                    sp.dma_start(tile_of(x1t, s), x1[:]).then_inc(x1_stored, 16)

                def store_n2(s):
                    sp.wait_ge(n2_ready, TI * (s.n + 1))
                    sp.dma_start(tile_of(n2t, s), n2[:]).then_inc(n2_stored, 16)

                def before():
                    load_x(Step(0, 0))
                    for dst, src in ((wqkv, "wqkv"), (gfc1, "gfc1T"), (wproj, "wproj")):
                        sp.dma_start(dst[:], t[src].rearrange("(k p) n -> p k n", p=P)).then_inc(consts_in, 16)
                    sp.dma_start(gfc1_b[:], t["gfc1_b"]).then_inc(consts_in, 16)
                    for dst, src in ((bproj, "bproj"), (gamma, "gamma"), (beta, "beta")):
                        sp.dma_start(dst[:], t[src].partition_broadcast(P)).then_inc(consts_in, 16)
                    for h in range(2):
                        sp.dma_start(adj[64 * h:64 * h + 64, :], t["adj"]).then_inc(consts_in, 16)
                    load_x(Step(0, 1))
                    for m in range(2):
                        load_whole(Step(0, 0), m)
                    sp.wait_ge(zero_set, 1)
                    for m in (1, 2):
                        for row in range(KROWS):
                            if row % HALF >= BASE_ROW + 3:
                                dst = t[f"s{m}"][row * HROW:(row + 1) * HROW].rearrange("(p a c) -> p a c", p=P, c=512)
                                sp.dma_start(dst, zero[:].unsqueeze(1).broadcast_to([P, dst.shape[1], 512])
                                             ).then_inc(zero_stored, 16)

                def body(s, has_x, has_l):
                    if has_l:
                        load_x(s + 2)
                    r = s + (-2)
                    if r.exists():
                        store_n2T(r)
                    store_parts(s, 0)
                    if has_x:
                        load_whole(s + 1, 0)
                    q = s + (-1)
                    if q.exists():
                        store_x1(q)
                    sp.dma_start(x_res[:], tile_of(xt, s)).then_inc(res_loaded, 16)
                    if q.exists():
                        store_n2(q)
                    store_parts(s, 1)
                    if has_x:
                        load_whole(s + 1, 1)

                def after():
                    end = Step(NST // 2 - 1, 1)
                    store_n2T(end + (-1))
                    store_x1(end)
                    store_n2(end)
                    store_n2T(end)
                    sp.wait_ge(n2T_stored, 16 * NST)
                    sp.wait_ge(x1_stored, 16 * NST)
                    sp.wait_ge(n2_stored, 16 * NST)
                    sp.wait_ge(zero_stored, 16 * 2 * 2 * (HALF - BASE_ROW - 3))
                    for m in range(2):
                        sp.wait_ge(parts_stored[m], STORES * NST)

                run(sp, body, before, after)

            @block.tensor
            def _(pe):
                def x_fill(s, k):
                    q, prev = (s, k - 4) if k >= 4 else (s + (-1), k + 4)
                    if k == 2:
                        pe.wait_ge(x_emptied, XU * s.n + 2)
                    elif q.exists():
                        pe.wait_ge(x_emptied, XU * q.n + prev + 1)
                    bank = ps_x[:, k % 4, :]
                    if k < 2:
                        if k == 0:
                            pe.wait_ge(n1_ready, s.n + 1)
                        for c in range(KD):
                            last = pe.transpose(bank[:, c * P:(c + 1) * P], n1[:, k, c * P:(c + 1) * P], ident[:])
                    elif k < 6:
                        for m in range(2):
                            ch = 2 * (k - 2) + m
                            for c in range(KD):
                                last = pe.matmul(bank[:, m * ST:(m + 1) * ST], wqkv[:, c, ch * P:(ch + 1) * P],
                                                 n1T[:, c, :], start=(c == 0), stop=(c == KD - 1))
                    else:
                        i = k - 6
                        for c in range(KD):
                            last = pe.matmul(bank[:], n1T[:, c, i * P:(i + 1) * P], wqkv[:, c, 2 * D:3 * D],
                                             start=(c == 0), stop=(c == KD - 1))
                    last.then_inc(x_filled, 1)

                def y_fill(s, name):
                    k, i = yi(name), int(name[1])
                    y_free(pe, s, k, {"O": f"P{i}b", "R": f"O{i}"}.get(name[0]))
                    bank = bank_y(k)
                    if name[0] == "S":
                        if i == 0:
                            wait_apart(pe, x_emptied, XU * (s.n + 1), consts_in, 16 * NCONST)
                        r = HD * i
                        for at in range(0, ST, NODES):
                            g = at // NODES
                            out_rows = slice(NODES * (g % 2), NODES * (g % 2) + NODES)
                            for h in range(H // 2):
                                col = ((g // 2) * (H // 2) + h) * NODES
                                last = pe.matmul(bank[out_rows, col:col + NODES],
                                                 qkT[r:r + HD, s.par, h, at:at + NODES],
                                                 qkT[r:r + HD, s.par, KD + h, at:at + NODES],
                                                 start=True, stop=True)
                    elif name[0] == "P":
                        odd = int(name[2] == "b")
                        pe.wait_ge(probs_ready, 2 * s.n + odd + 1)
                        for h in range(4):
                            last = pe.transpose(bank[:, h * P:(h + 1) * P], probs[:, i, odd, h, :], ident[:])
                    elif name[0] == "O":
                        for h in range(H):
                            r = HD * (h % 2)
                            last = pe.matmul(bank[r:r + HD, (h // 2) * P:(h // 2 + 1) * P],
                                             v[:, s.par, i, h * HD:(h + 1) * HD],
                                             probsT[:, i, (h % 2) * (H // 2) + h // 2, :],
                                             start=True, stop=True)
                    else:
                        for c in range(KD):
                            last = pe.matmul(bank[:], oT[:, i, c, :], wproj[:, c, :],
                                             start=(c == 0), stop=(c == KD - 1))
                    last.then_inc(y_filled, 1)

                def z_fill(s, k):
                    if not s.exists():
                        return
                    q, prev = (s, k - 2) if k >= 2 else (s + (-1), k + 2)
                    if k == 2:
                        pe.wait_ge(z_emptied, ZU * s.n + 2)
                    elif q.exists():
                        pe.wait_ge(z_emptied, ZU * q.n + prev + 1)
                    bank = ps_z[:, k % 2, :]
                    if k < 2:
                        pe.wait_ge(n2_ready, TI * s.n + k + 1)
                        for c in range(KD):
                            last = pe.transpose(bank[:, c * P:(c + 1) * P], n2[:, k, c * P:(c + 1) * P], ident[:])
                    else:
                        for m in range(2):
                            ch = 2 * (k - 2) + m
                            for c in range(KD):
                                last = pe.matmul(bank[:, m * ST:(m + 1) * ST], gfc1[:, c, ch * P:(ch + 1) * P],
                                                 n2T[:, c, :], start=(c == 0), stop=(c == KD - 1))
                    last.then_inc(z_filled, 1)

                def before():
                    pe.wait_ge(consts_in, 16 * NCONST)
                    for k in range(XU):
                        x_fill(Step(0, 0), k)

                def body(s, has_x, has_l):
                    z = s + (-1)

                    def x(k):
                        if has_x:
                            x_fill(s + 1, k)
                    y_fill(s, "S0")
                    y_fill(s, "S1")
                    x(0)
                    x(1)
                    x(2)
                    x(3)
                    y_fill(s, "P0a")
                    y_fill(s, "P0b")
                    y_fill(s, "O0")
                    x(4)
                    y_fill(s, "P1a")
                    y_fill(s, "P1b")
                    y_fill(s, "R0")
                    y_fill(s, "O1")
                    x(5)
                    y_fill(s, "R1")
                    z_fill(z, 0)
                    z_fill(z, 1)
                    x(6)
                    z_fill(z, 2)
                    x(7)
                    z_fill(z, 3)

                def after():
                    for k in range(ZU):
                        z_fill(Step(NST // 2 - 1, 1), k)

                run(pe, body, before, after)

            @block.scalar
            def _(act):
                def x_empty(s, k):
                    act.wait_ge(x_filled, XU * s.n + k + 1)
                    bank = ps_x[:, k % 4, :]
                    if k < 2:
                        dst = n1T[:, :, k * P:(k + 1) * P]
                        src = bank.rearrange("p (c n) -> p c n", n=P)
                    elif k < 6:
                        dst = qkT[:, s.par, 2 * (k - 2):2 * (k - 2) + 2, :]
                        src = bank.rearrange("p (c n) -> p c n", n=ST)
                    else:
                        dst, src = v[:, s.par, k - 6, :], bank
                    nc.scalar.activation(dst, src, ACT.Copy).then_inc(x_emptied, 1)

                def y_empty(s, name):
                    k, i = yi(name), int(name[1])
                    act.wait_ge(y_filled, YU * s.n + k + 1)
                    src = bank_y(k).rearrange("p (c n) -> p c n", n=P)
                    if name[0] == "P":
                        h = (H // 2) * (name[2] == "b")
                        dst = probsT[:, i, h:h + 4, :]
                    else:
                        dst = oT[:, i]
                    nc.scalar.activation(dst, src, ACT.Copy).then_inc(y_emptied_act, 1)

                def exponent(s, i):
                    act.wait_ge(shifted, TI * s.n + i + 1)
                    nc.scalar.activation(scores[:, i], scores[:, i], ACT.Exp).then_inc(exp_done, 1)

                def z_empty(s, k):
                    if not s.exists():
                        return
                    q = s + (-1)
                    act.wait_ge(z_filled, ZU * s.n + k + 1)
                    bank = ps_z[:, k % 2, :]
                    if k < 2:
                        if k == 0 and q.exists():
                            act.wait_ge(n2T_stored, 16 * (q.n + 1))
                        nc.scalar.activation(n2T[:, :, k * P:(k + 1) * P], bank.rearrange("p (c n) -> p c n", n=P),
                                             ACT.Copy).then_inc(z_emptied, 1)
                        return
                    if q.exists():
                        act.wait_ge(gate_summed, 2 * q.n + k - 1)
                    for m in range(2):
                        ch = 2 * (k - 2) + m
                        last = nc.scalar.activation(gate_h[:, k - 2, m, :], bank[:, m * ST:(m + 1) * ST], ACT.Relu,
                                                    bias=gfc1_b[:, ch:ch + 1])
                    last.then_inc(z_emptied, 1)

                def cut_high(s, m):
                    act.wait_ge(whole_in[m], 32 * (s.n + 1))
                    q = s + (-1)
                    if q.exists():
                        act.wait_ge(parts_stored[m], STORES * (q.n + 1))
                    nc.scalar.activation(part[0][:, m, :], whole[:, m, :], ACT.Copy).then_inc(high_cut[m], 1)

                def cut_mid(s, m):
                    act.wait_ge(high_off[m], s.n + 1)
                    nc.scalar.activation(part[1][:, m, :], whole[:, m, :], ACT.Copy).then_inc(mid_cut[m], 1)

                def before():
                    act.wait_ge(consts_in, 16 * NCONST)
                    for k in range(XU):
                        x_empty(Step(0, 0), k)

                def body(s, has_x, has_l):
                    z = s + (-1)

                    def x(k):
                        if has_x:
                            x_empty(s + 1, k)
                    x(0)
                    x(1)
                    cut_high(s, 0)
                    exponent(s, 0)
                    exponent(s, 1)
                    x(2)
                    x(3)
                    cut_mid(s, 0)
                    y_empty(s, "P0a")
                    y_empty(s, "P0b")
                    y_empty(s, "O0")
                    cut_high(s, 1)
                    x(4)
                    y_empty(s, "P1a")
                    y_empty(s, "P1b")
                    y_empty(s, "O1")
                    x(5)
                    cut_mid(s, 1)
                    z_empty(z, 0)
                    z_empty(z, 1)
                    x(6)
                    z_empty(z, 2)
                    x(7)
                    z_empty(z, 3)

                def after():
                    for k in range(ZU):
                        z_empty(Step(NST // 2 - 1, 1), k)

                run(act, body, before, after)

            @block.vector
            def _(dve):
                L_LINKS, Y_LINKS, W_LINKS = 2, TI * 2, TI * 6

                def linker(base):
                    count = [0]

                    def link(ins, by_stats=False):
                        count[0] += 1
                        ins.then_inc(dve_link, 1)
                        if by_stats:
                            wait_apart(dve, dve_link, base + count[0], consts_in, 16 * NCONST)
                        else:
                            dve.wait_ge(dve_link, base + count[0])
                    return link, count

                def normalise(s, base):
                    link, count = linker(base)
                    q = s + (-1)
                    dve.wait_ge(x_loaded[s.par], 16 * (s.j + 1))
                    for i in range(TI):
                        last = nc.vector.bn_stats(st_x[:, i, :], x_in[:, s.par, i, :])
                    link(last, True)
                    for i in range(TI):
                        last = nc.vector.bn_aggr(ag_x[:, i, :], st_x[:, i, :])
                    link(last)
                    if q.exists():
                        dve.wait_ge(rstd_x, q.n + 1)
                    nc.vector.tensor_scalar(ve_x[:], ag_x[:, :, 1], EPS, None, ALU.add).then_inc(var_x, 1)
                    dve.wait_ge(rstd_x, s.n + 1)
                    if q.exists():
                        dve.wait_ge(x_filled, XU * q.n + 2)
                    for i in range(TI):
                        last = nc.vector.tensor_scalar(n1[:, i, :], x_in[:, s.par, i, :], ag_x[:, i, 0:1],
                                                       rs_x[:, i:i + 1], ALU.subtract, ALU.mult)
                    last.then_inc(n1_ready, 1)
                    assert count[0] == L_LINKS

                def softmax_shift(s, i, link):
                    q = s + (-1)
                    dve.wait_ge(y_filled, YU * s.n + yi(f"S{i}") + 1)
                    if q.exists():
                        dve.wait_ge(probs_ready, 2 * q.n + i + 1)
                    nc.vector.scalar_tensor_tensor(
                        out=scores[:, i], in0=bank_y(yi(f"S{i}")).rearrange("p (h m) -> p h m", h=H),
                        scalar=float(HD) ** -0.5, in1=mask[:].unsqueeze(1).broadcast_to([P, H, NODES]),
                        op0=ALU.mult, op1=ALU.add).then_inc(y_emptied_dve, 1)
                    dve.wait_ge(y_emptied_dve, NDVE * s.n + dve_rank(f"S{i}"))
                    link(nc.vector.tensor_reduce(top[:, i, :], scores[:, i], AX.X, ALU.max))
                    nc.vector.tensor_tensor(scores[:, i], scores[:, i],
                                            top[:, i, :].unsqueeze(2).broadcast_to([P, H, NODES]),
                                            ALU.subtract).then_inc(shifted, 1)

                def softmax_total(s, i, link):
                    dve.wait_ge(exp_done, TI * s.n + i + 1)
                    link(nc.vector.tensor_reduce(total[:, i, :], scores[:, i], AX.X, ALU.add))
                    nc.vector.reciprocal(inv[:, i, :], total[:, i, :]).then_inc(inv_ready, 1)

                def gate_total(s, k):
                    if not s.exists():
                        return
                    dve.wait_ge(z_emptied, ZU * s.n + k + 1)
                    nc.vector.tensor_reduce(
                        gate_sum[:, 2 * (k - 2):2 * (k - 2) + 2, bass.ds(4 * s.n, 4)],
                        gate_h[:, k - 2].rearrange("p m (b n) -> p m b n", n=NODES), AX.X,
                        ALU.add).then_inc(gate_summed, 1)

                def norm(s, i, which, src, link):
                    c = 2 * i + which
                    q = s + (-1)
                    link(nc.vector.bn_stats(st_y[:, c, :], src), True)
                    link(nc.vector.bn_aggr(ag_y[:, c, :], st_y[:, c, :]))
                    if q.exists():
                        dve.wait_ge(rstd_y, 4 * q.n + c + 1)
                    nc.vector.tensor_scalar(ve_y[:, c:c + 1], ag_y[:, c, 1:2], EPS, None, ALU.add).then_inc(var_y, 1)
                    dve.wait_ge(rstd_y, 4 * s.n + c + 1)
                    return ag_y[:, c, 0:1], rs_y[:, c:c + 1]

                def empty_projection(s, i):
                    dve.wait_ge(y_filled, YU * s.n + yi(f"R{i}") + 1)
                    nc.vector.tensor_tensor(o2[:, i, :], bank_y(yi(f"R{i}")), bproj[:],
                                            ALU.add).then_inc(y_emptied_dve, 1)

                def finish(s, i, link):
                    q = s + (-1)
                    dve.wait_ge(y_emptied_dve, NDVE * s.n + dve_rank(f"R{i}"))
                    mean, rstd = norm(s, i, 0, o2[:, i, :], link)
                    link(nc.vector.tensor_scalar(ln[:, i, :], o2[:, i, :], mean, rstd, ALU.subtract, ALU.mult))
                    link(nc.vector.tensor_tensor(ln[:, i, :], ln[:, i, :], gamma[:], ALU.mult))
                    if q.exists():
                        dve.wait_ge(x1_stored, 16 * (q.n + 1))
                        dve.wait_ge(n2_stored, 16 * (q.n + 1))
                        dve.wait_ge(z_filled, ZU * q.n + 2)
                    dve.wait_ge(rest_added, 2 * TI * s.n + 2 * i + 2)
                    nc.vector.tensor_tensor(x1[:, i, :], x_res[:, i, :], ln[:, i, :], ALU.add).then_inc(x1_ready, 1)
                    dve.wait_ge(x1_ready, TI * s.n + i + 1)
                    mean, rstd = norm(s, i, 1, x1[:, i, :], link)
                    nc.vector.tensor_scalar(n2[:, i, :], x1[:, i, :], mean, rstd, ALU.subtract,
                                            ALU.mult).then_inc(n2_ready, 1)

                def take_high(s, m):
                    dve.wait_ge(high_cut[m], s.n + 1)
                    nc.vector.tensor_tensor(whole[:, m, :], whole[:, m, :], part[0][:, m, :],
                                            ALU.subtract).then_inc(high_off[m], 1)

                def cut_low(s, m):
                    dve.wait_ge(mid_cut[m], s.n + 1)
                    nc.vector.tensor_tensor(part[2][:, m, :], whole[:, m, :], part[1][:, m, :],
                                            ALU.subtract).then_inc(low_cut[m], 1)

                def before():
                    nc.vector.memset(zero[:], 0.0).then_inc(zero_set, 1)
                    nc.vector.memset(power[:], -0.5).then_inc(consts_set, 1)
                    nc.vector.memset(probs[:], 0.0).then_inc(consts_set, 1)
                    dve.wait_ge(consts_in, 16 * NCONST)
                    nc.vector.tensor_scalar(mask[:], adj[:], 0.0, NEG, ALU.is_equal, ALU.mult).then_inc(consts_set, 1)
                    dve.wait_ge(consts_set, 3)
                    normalise(Step(0, 0), 0)
                    normalise(Step(0, 1), L_LINKS)

                def body(s, has_x, has_l):
                    base = (L_LINKS + Y_LINKS + W_LINKS) * s.n + 2 * L_LINKS
                    z, y = s + (-1), s + (-2)
                    if z.exists():
                        base -= W_LINKS
                    if not has_x:
                        base -= L_LINKS
                    link, count = linker(base)
                    for i in range(TI):
                        softmax_shift(s, i, link)
                    take_high(s, 0)
                    for i in range(TI):
                        softmax_total(s, i, link)
                    gate_total(y, 2)
                    gate_total(y, 3)
                    if z.exists():
                        finish(z, 0, link)
                    cut_low(s, 0)
                    empty_projection(s, 0)
                    take_high(s, 1)
                    if z.exists():
                        finish(z, 1, link)
                    empty_projection(s, 1)
                    cut_low(s, 1)
                    assert count[0] == Y_LINKS + (W_LINKS if z.exists() else 0)
                    if has_l:
                        normalise(s + 2, base + count[0])

                def after():
                    end = Step(NST // 2 - 1, 1)
                    link, _ = linker((L_LINKS + Y_LINKS + W_LINKS) * NST - W_LINKS)
                    gate_total(end + (-1), 2)
                    gate_total(end + (-1), 3)
                    for i in range(TI):
                        finish(end, i, link)
                    gate_total(end, 2)
                    gate_total(end, 3)
                    dve.wait_ge(gate_summed, 2 * NST)

                run(dve, body, before, after)

            @block.gpsimd
            def _(pool):
                def power_x(s):
                    pool.wait_ge(var_x, s.n + 1)
                    if (s + (-1)).exists():
                        pool.wait_ge(n1_ready, s.n)
                    nc.gpsimd.tensor_tensor(rs_x[:], ve_x[:], power[:], ALU.pow).then_inc(rstd_x, 1)

                def scale(s, i):
                    q = s + (-1)
                    pool.wait_ge(inv_ready, TI * s.n + i + 1)
                    if q.exists():
                        pool.wait_ge(y_filled, YU * q.n + yi("P1" + "ab"[i]) + 1)
                    for g in range(2):
                        r = slice(g * NODES, (g + 1) * NODES)
                        for tile in range(TI):
                            hs = slice(tile * (H // 2), (tile + 1) * (H // 2))
                            last = nc.gpsimd.tensor_tensor(
                                probs[r, tile, i, :, g * NODES:(g + 1) * NODES], scores[r, i, hs],
                                inv[r, i, hs].unsqueeze(2).broadcast_to([NODES, H // 2, NODES]), ALU.mult)
                    last.then_inc(probs_ready, 1)

                def power_y(s, c):
                    pool.wait_ge(var_y, 4 * s.n + c + 1)
                    nc.gpsimd.tensor_tensor(rs_y[:, c:c + 1], ve_y[:, c:c + 1], power[:, 0:1],
                                            ALU.pow).then_inc(rstd_y, 1)

                def add_rest(s, i):
                    if i == 0:
                        pool.wait_ge(res_loaded, 16 * (s.n + 1))
                    nc.gpsimd.tensor_tensor(x_res[:, i, :], x_res[:, i, :], beta[:], ALU.add).then_inc(rest_added, 1)
                    pool.wait_ge(rest_added, 2 * TI * s.n + 2 * i + 1)
                    pool.wait_ge(y_emptied_dve, NDVE * s.n + dve_rank(f"R{i}"))
                    nc.gpsimd.tensor_tensor(x_res[:, i, :], x_res[:, i, :], o2[:, i, :], ALU.add).then_inc(rest_added, 1)

                def before():
                    pool.wait_ge(consts_set, 3)
                    power_x(Step(0, 0))
                    power_x(Step(0, 1))

                def finish(s):
                    for i in range(TI):
                        power_y(s, 2 * i)
                        add_rest(s, i)
                        power_y(s, 2 * i + 1)

                def body(s, has_x, has_l):
                    scale(s, 0)
                    scale(s, 1)
                    pool.wait_ge(probs_ready, 2 * s.n + 2)
                    if (s + (-1)).exists():
                        finish(s + (-1))
                    if has_l:
                        power_x(s + 2)

                run(pool, body, before, lambda: finish(Step(NST // 2 - 1, 1)))


def gates(nc, t, keep):
    with ExitStack() as ctx:
        def sb(name, shape, dt=F32):
            return ctx.enter_context(nc.sbuf_tensor(name, shape, dt))

        def sem(name):
            return ctx.enter_context(nc.semaphore(name))

        fc2 = sb("fc2", [P, KD, P])
        fc2_b = sb("fc2_b", [P, 1])
        sel = sb("sel", [P, 8])
        sel9 = sb("sel9", [E + 1, 2])
        g = sb("g", [P, GRAPHS])
        rest = sb("g_rest", [P, GRAPHS])
        part = [sb(f"g_part{k}", [P, GRAPHS], BF16) for k in range(3)]
        mix = sb("g_mix", [P, 2, GRAPHS])
        tvb1 = sb("tvb1", [E + 1, F])
        lnp = sb("lnp", [E, 2, D])
        lnq = sb("lnq", [E, 2, D])
        lnr = sb("lnr", [P, 2, D])
        ones = sb("ones", [E, P])
        ps = ctx.enter_context(nc.psum_tensor("ps_g", [P, 8, 512], F32))
        loaded, cleared, filled, cut, emptied = sem("g_loaded"), sem("g_cleared"), sem("g_filled"), sem("g_cut"), sem("g_emptied")
        gate_sum, gblk, g9, b1m, lnw = keep["gate_sum"], keep["gblk"], keep["g9"], keep["b1m"], keep["lnw"]
        nload = [0]

        with nc.Block() as block:
            @block.sync
            def _(sp):
                def load(dst, src):
                    sp.dma_start(dst, src).then_inc(loaded, 16)
                    nload[0] += 1
                sp.wait_ge(cleared, 3)
                for half in range(2):
                    for c in range(PAIRS):
                        at = half * HALF + c * E
                        load(fc2[:, :, at:at + E], t["fc2T"].rearrange("(k p) e -> p k e", p=P))
                        load(fc2_b[at:at + E, :], t["fc2_b"])
                load(sel[:], t["sel"])
                load(sel9[:], t["sel9"])
                load(tvb1[0:E, :], t["tvb1"])
                load(tvb1[E:E + 1, :], t["b1"].unsqueeze(0))
                load(keep["tvb2"][0:E, :], t["tvb2"])
                load(keep["tvb2"][E:E + 1, :], t["b2"].unsqueeze(0))
                for m, (w, tvw) in enumerate((("ln_g", "tv_ln_g"), ("ln_b", "tv_ln_b"))):
                    load(lnp[:, m, :], t[tvw])
                    load(lnq[:, m, :], t[w].partition_broadcast(E))
                    load(lnr[:, m, :], t[w].partition_broadcast(P))

            NLOAD = 2 * PAIRS * 2 + 6 + 6

            @block.vector
            def _(dve):
                nc.vector.memset(fc2[:], 0.0).then_inc(cleared, 1)
                nc.vector.memset(fc2_b[:], 0.0).then_inc(cleared, 1)
                nc.vector.memset(ones[:], 1.0).then_inc(cleared, 1)
                dve.wait_ge(loaded, 16 * NLOAD)
                count = [0]

                def link(ins):
                    count[0] += 1
                    ins.then_inc(cut, 1)
                    dve.wait_ge(cut, count[0])

                link(nc.vector.tensor_tensor(lnp[:], lnp[:], lnq[:], ALU.subtract))
                dve.wait_ge(filled, 1)
                link(nc.vector.tensor_scalar(g[:], ps[:, 0, 0:GRAPHS], 1.0 / NODES, fc2_b[:, 0:1],
                                             ALU.mult, ALU.add))
                link(nc.vector.tensor_scalar(g9[:], g[0:E + 1, :], sel9[:, 0:1], sel9[:, 1:2],
                                             ALU.mult, ALU.add))
                link(nc.vector.tensor_copy(part[0][:], g[:]))
                link(nc.vector.tensor_tensor(rest[:], g[:], part[0][:], ALU.subtract))
                link(nc.vector.tensor_copy(part[1][:], rest[:]))
                link(nc.vector.tensor_tensor(part[2][:], rest[:], part[1][:], ALU.subtract))
                for half in range(2):
                    one = sel[:, 4 * half + 3:4 * half + 4]
                    link(nc.vector.tensor_scalar(mix[:, 0, :], part[0][:], sel[:, 4 * half:4 * half + 1], one,
                                                 ALU.mult, ALU.add))
                    link(nc.vector.scalar_tensor_tensor(out=mix[:, 1, :], in0=part[1][:],
                                                        scalar=sel[:, 4 * half + 1:4 * half + 2],
                                                        in1=mix[:, 0, :], op0=ALU.mult, op1=ALU.add))
                    link(nc.vector.scalar_tensor_tensor(
                        out=gblk[:, :, half, :], in0=part[2][:].rearrange("p (g b) -> p g b", b=GB),
                        scalar=sel[:, 4 * half + 2:4 * half + 3],
                        in1=mix[:, 1, :].rearrange("p (g b) -> p g b", b=GB), op0=ALU.mult, op1=ALU.add))
                for m in range(2):
                    dve.wait_ge(filled, 2 + m)
                    link(nc.vector.scalar_tensor_tensor(out=lnw[:, m, :], in0=ps[:, 1 + m, :], scalar=LN_MERGE,
                                                        in1=lnr[:, m, :], op0=ALU.mult, op1=ALU.add))
                for k in range(4):
                    dve.wait_ge(filled, 4 + k)
                    link(nc.vector.tensor_copy(b1m[:, 4 * k:4 * k + 4, :],
                                               ps[:, 3 + k, :].rearrange("p (a b) -> p a b", b=GRAPHS)))

            @block.tensor
            def _(pe):
                pe.wait_ge(loaded, 16 * NLOAD)
                for c in range(KD):
                    last = pe.matmul(ps[:, 0, 0:GRAPHS], fc2[:, c, :], gate_sum[:, c, :],
                                     start=(c == 0), stop=(c == KD - 1))
                last.then_inc(filled, 1)
                pe.wait_ge(cut, 1)
                for m in range(2):
                    pe.matmul(ps[:, 1 + m, :], ones[:], lnp[:, m, :], start=True, stop=True).then_inc(filled, 1)
                pe.wait_ge(cut, 3)
                for k in range(4):
                    for a in range(4):
                        last = pe.matmul(ps[:, 3 + k, a * GRAPHS:(a + 1) * GRAPHS],
                                         tvb1[:, (4 * k + a) * P:(4 * k + a + 1) * P], g9[:],
                                         start=True, stop=True)
                    last.then_inc(filled, 1)


def feed(nc, t, keep):
    gblk, g9, b1m, lnw, ident = keep["gblk"], keep["g9"], keep["b1m"], keep["lnw"], keep["ident"]
    tvb2 = keep["tvb2"]
    with ExitStack() as ctx:
        def sb(name, shape, dt=F32):
            return ctx.enter_context(nc.sbuf_tensor(name, shape, dt))

        def sem(name):
            return ctx.enter_context(nc.semaphore(name))

        SLOT = 8192
        slot = sb("slot", [P, 2, SLOT])
        nT = sb("nT", [P, KD, GT])
        acc = sb("acc", [P, PR, D])
        pieces = sb("pieces", [KROWS, 4, PIECE], BF16)
        hid = sb("hid", [P, PR, P])
        hT = sb("hT", [P, GT])
        gnow = sb("gnow", [KROWS, 2 * GB], BF16)
        bnow = sb("bnow", [P, GB])
        gtok = sb("gtok", [E + 1, 2, P])
        x_row = sb("x_row", [P, 2, 2, D])
        st, ag = sb("st_f", [P, PR, 6]), sb("ag_f", [P, PR, 2])
        ve, rs, shift = sb("ve_f", [P, PR]), sb("rs_f", [P, PR]), sb("shift_f", [P, PR])
        power = sb("power_f", [P, PR])
        ps_m = ctx.enter_context(nc.psum_tensor("ps_m", [P, 2, 1024], F32))
        ps_w = ctx.enter_context(nc.psum_tensor("ps_w", [P, 4, 512], F32))

        nT_loaded = sem("nT_loaded")
        piece_in = [sem(f"piece_in{k}") for k in range(4)]
        merged = sem("merged")
        kept_act, kept_dve = sem("kept_act"), sem("kept_dve")
        work = sem("work")
        work_act, work_dve = sem("work_act"), sem("work_dve")
        g_ready, b_ready, gtok_ready = sem("g_ready"), sem("b_ready"), sem("gtok_ready")
        power_set = sem("power_set")
        var_f, rstd_f = sem("var_f"), sem("rstd_f")
        x_in = [sem("x_in0"), sem("x_in1")]
        acc_in = [sem(f"acc_in{a}") for a in range(PR // 4)]
        y_out = [sem("y_out0"), sem("y_out1")]
        shift_ready, normed, scaled, y_ready = sem("shift_ready"), sem("normed"), sem("scaled"), sem("y_ready")
        link_f = sem("link_f")

        FIRST = ["La0", "La1", "Lb0", "T0", "T1", "Lb1", "T2", "T3"]
        INIT, NL1, NL2 = PR, len(FIRST), 16
        PER_T = NL1 + NL2
        PER_G = INIT + FT * PER_T
        DVE_G = INIT + FT * NL2
        CREDIT = 4
        UNITS = 4 * FT
        KEPT = 1

        def first_index(g, f, k):
            start = 0 if isinstance(f, int) and f == 0 else INIT + f * PER_T
            return g * PER_G + start + k + 1

        def second_index(g, f, k):
            return g * PER_G + INIT + f * PER_T + NL1 + k + 1

        def init_index(g, i):
            return g * PER_G + NL1 + i + 1

        def all_groups(engine, group):
            group(0, True, False)
            with engine.Fori(1, GROUPS - 1) as g:
                group(g, False, False)
            group(GROUPS - 1, False, True)

        s1 = t["s1"].rearrange("(p v c) -> v p c", p=KROWS, c=PIECE)
        s2 = t["s2"].rearrange("(p v c) -> v p c", p=KROWS, c=PIECE)
        nTt = t["n2T"].rearrange("k p (g c) -> g p k c", c=GT)
        n2t = t["n2"].rearrange("(a i p) d -> a p i d", i=4, p=P)
        x1t = t["x1"].rearrange("(a i p) d -> a p i d", i=2, p=P)
        yt = t["y"].rearrange("(a i p) d -> a p i d", i=2, p=P)

        with nc.Block() as block:
            @block.sync
            def _(sp):
                def unit(u, src, at):
                    for k in range(4):
                        sp.wait_ge(merged, 8 * u + 2 * k + 2)
                        sp.dma_start(pieces[:, k, :], src[bass.ds(at + k, 1)].rearrange("a p c -> (a p) c")
                                     ).then_inc(piece_in[k], 16)

                with sp.Fori(0, GROUPS) as g:
                    with sp.Fori(0, FT) as f:
                        u = g * UNITS + f * 4
                        unit(u, s1, f * 8)
                        unit(u + 1, s1, f * 8 + 4)
                        unit(u + 2, s2, f * 4)
                        unit(u + 3, s2, f * 4 + 4 * FT)

            @block.tensor
            def _(pe):
                def merge(u, second, q):
                    if q % 2 == 0:
                        pe.wait_ge(piece_in[q // 2], 16 * (u + 1))
                    pe.wait_ge(kept_act if q % 2 == 0 else kept_dve, KEPT + 4 * u + q // 2)
                    for r in range(16):
                        if second:
                            at = ((q % 2) * 16 + r) * P
                        else:
                            at = (r % 8) * D + ((q % 2) * 2 + r // 8) * P
                        last = pe.matmul(ps_m[:, q % 2, r * 64:(r + 1) * 64], pieces[:, q // 2, at:at + P],
                                         gnow[:], start=True, stop=True)
                    last.then_inc(merged, 1)

                def kept(u):
                    pe.wait_ge(kept_act, KEPT + 4 * u + 4)
                    pe.wait_ge(kept_dve, KEPT + 4 * u + 4)

                def act_base(g, f):
                    return (g * FT + f) * NL1

                def dve_base(g, f):
                    return CREDIT + g * DVE_G + INIT + f * NL2

                def free_first(g, f, k):
                    before = dve_base(g, f) - (INIT if isinstance(f, int) and f == 0 else 0)
                    pe.wait_ge(work_dve, before - 4 + k + 1)

                def first_graphs(g, f, ab, bank, graphs):
                    k = FIRST.index("L" + "ab"[ab] + str(bank))
                    w = slot[:, ab, :].rearrange("p (k b f) -> p k b f", k=KD, b=GB)
                    for b in graphs:
                        bb, r = bank * 16 + b, NODES * (b % 2)
                        for c in range(KD):
                            last = pe.matmul(ps_w[r:r + NODES, k % 4, (b // 2) * 64:(b // 2 + 1) * 64],
                                             nT[:, c, bb * NODES:(bb + 1) * NODES], w[:, c, bb, :],
                                             start=(c == 0), stop=(c == KD - 1))
                    if graphs[-1] == 15:
                        last.then_inc(work, 1)

                def turn(g, f, q):
                    k = FIRST.index(f"T{q}")
                    if q == 0:
                        free_first(g, f, k)
                    pe.wait_ge(work_act, act_base(g, f) + FIRST.index("Lb0" if q < 2 else "Lb1") + 1)
                    for p in range(4):
                        last = pe.transpose(ps_w[:, k % 4, p * P:(p + 1) * P], hid[:, 4 * q + p, :], ident[:])
                    last.then_inc(work, 1)

                def second_graphs(g, f, cd, q):
                    k = 8 * cd + q
                    if k >= 4:
                        pe.wait_ge(work_dve, dve_base(g, f) + k - 4 + 1)
                    elif isinstance(f, int) and f == 0:
                        pe.wait_ge(work_dve, dve_base(g, f) - 4 + k + 1)
                    else:
                        pe.wait_ge(work_act, act_base(g, f) + 4 + k + 1)
                    w = slot[:, cd, :].rearrange("p (b d) -> p b d", b=GB)
                    for b in range(4):
                        bb, r = 4 * q + b, NODES * (b % 2)
                        last = pe.matmul(ps_w[r:r + NODES, k % 4, (b // 2) * 256:(b // 2 + 1) * 256],
                                         hT[:, bb * NODES:(bb + 1) * NODES], w[:, bb, :], start=True, stop=True)
                    last.then_inc(work, 1)

                def second_bias(g):
                    for i in range(INIT):
                        if i < 4:
                            pe.wait_ge(work_act, act_base(g, 0) + 4 + i + 1)
                        else:
                            pe.wait_ge(work_dve, CREDIT + g * DVE_G + i - 4 + 1)
                        pe.wait_ge(gtok_ready, g * INIT + i + 1)
                        pe.matmul(ps_w[:, i % 4, :], gtok[:, i % 2, :], tvb2[:], start=True, stop=True
                                  ).then_inc(work, 1)

                def tile(g, f, following):
                    u = g * UNITS + f * 4
                    kept(u)
                    for q in range(8):
                        merge(u + 1, False, q)
                        if q % 4 == 0:
                            free_first(g, f, q // 4)
                        first_graphs(g, f, 0, q // 4, range(4 * (q % 4), 4 * (q % 4) + 4))
                    kept(u + 1)
                    for q in range(8):
                        merge(u + 2, True, q)
                        if q == 0:
                            free_first(g, f, 2)
                        if q == 4:
                            pe.wait_ge(work_act, act_base(g, f) + 2)
                        first_graphs(g, f, 1, q // 4, range(4 * (q % 4), 4 * (q % 4) + 4))
                        if q == 4:
                            turn(g, f, 0)
                        if q == 6:
                            turn(g, f, 1)
                    merge(u + 3, True, 0)
                    turn(g, f, 2)
                    turn(g, f, 3)
                    if isinstance(f, int) and f == 0:
                        second_bias(g)
                    kept(u + 2)
                    for q in range(8):
                        if q:
                            merge(u + 3, True, q)
                        second_graphs(g, f, 0, q)
                    kept(u + 3)
                    if following == 2:
                        pe.wait_ge(g_ready, g + 2)
                    for q in range(8):
                        if following:
                            merge(u + 4, False, q)
                        second_graphs(g, f, 1, q)

                def group(g, first, last):
                    wait_apart(pe, nT_loaded, 16 * (g + 1), power_set, 1)
                    tile(g, 0, 1)
                    with pe.Fori(1, FT - 1) as f:
                        tile(g, f, 1)
                    tile(g, FT - 1, 0 if last else 2)

                pe.sem_inc(merged, 8)
                pe.wait_ge(g_ready, 1)
                for q in range(8):
                    merge(0, False, q)
                all_groups(pe, group)

            def keep(eng, copy, u, second, s, q, done):
                eng.wait_ge(merged, 8 + 8 * u + q + 1)
                bank = ps_m[:, q % 2, :]
                if second:
                    src = bank.rearrange("p (r h b) -> p b h r", r=16, h=2)
                    dst = slot[:, s, :].rearrange("p (b h r) -> p b h r", b=GB, h=2)[:, :, :, 16 * q:16 * q + 16]
                    last = copy(dst, src)
                else:
                    for m in range(2):
                        c = 2 * (q % 2) + m
                        src = bank[:, 512 * m:512 * (m + 1)].rearrange("p (r h b) -> p b h r", r=8, h=2)
                        dst = slot[:, s, :].rearrange("p (k b h r) -> p k b h r", k=KD, b=GB, h=2)[
                            :, c, :, :, 8 * (q // 2):8 * (q // 2) + 8]
                        last = copy(dst, src)
                last.then_inc(done, 1)

            @block.scalar
            def _(act):
                def copy(dst, src):
                    return nc.scalar.activation(dst, src, ACT.Copy)

                def keep_act(u, second, s, q):
                    keep(act, copy, u, second, s, q, kept_act)

                def first_out(g, f, ab, bank):
                    k = FIRST.index("L" + "ab"[ab] + str(bank))
                    act.wait_ge(work, first_index(g, f, k))
                    nc.scalar.activation(hid[:, 8 * bank:8 * bank + 8, 64 * ab:64 * ab + 64],
                                         ps_w[:, k % 4, :].rearrange("p (i f) -> p i f", f=64),
                                         ACT.Copy).then_inc(work_act, 1)

                def relu(g, f, q):
                    k = FIRST.index(f"T{q}")
                    act.wait_ge(work, first_index(g, f, k))
                    for b in range(8):
                        bb = 8 * q + b
                        last = nc.scalar.activation(hT[:, bb * NODES:(bb + 1) * NODES],
                                                    ps_w[:, k % 4, b * NODES:(b + 1) * NODES], ACT.Relu,
                                                    bias=bnow[:, bb:bb + 1])
                    last.then_inc(work_act, 1)

                def norm_rows(g, rows):
                    for i in rows:
                        nc.scalar.activation(acc[:, i, :], acc[:, i, :], ACT.Identity, bias=shift[:, i:i + 1],
                                             scale=rs[:, i:i + 1]).then_inc(normed, 1)

                def gates_of(g, is_first):
                    if not is_first:
                        act.wait_ge(merged, 8 + 8 * UNITS * g)
                    nc.scalar.activation(gnow[:].rearrange("p (h b) -> p h b", b=GB).unsqueeze(1),
                                         gblk[0:KROWS, bass.ds(g, 1)], ACT.Copy).then_inc(g_ready, 1)

                def tile(g, f, following, unfinished=False):
                    u = g * UNITS + f * 4
                    nc.scalar.activation(bnow[:].unsqueeze(1), b1m[:, bass.ds(f, 1), bass.ds(g * GB, GB)],
                                         ACT.Copy).then_inc(b_ready, 1)
                    act.wait_ge(b_ready, g * FT + f + 1)
                    if unfinished:
                        act.wait_ge(shift_ready, g)
                    for q in range(8):
                        if q % 2 == 0:
                            keep_act(u + 1, False, 1, q)
                            if unfinished:
                                norm_rows(g - 1, range(q, q + 2))
                        if q % 4 == 3:
                            first_out(g, f, 0, q // 4)
                    for q in range(8):
                        if q % 2 == 0:
                            keep_act(u + 2, True, 0, q)
                            if unfinished:
                                norm_rows(g - 1, range(8 + q, 8 + q + 2))
                        if q == 3:
                            first_out(g, f, 1, 0)
                        if q == 4:
                            relu(g, f, 0)
                        if q == 6:
                            relu(g, f, 1)
                    first_out(g, f, 1, 1)
                    keep_act(u + 3, True, 1, 0)
                    relu(g, f, 2)
                    relu(g, f, 3)
                    for q in (2, 4, 6):
                        keep_act(u + 3, True, 1, q)
                    if following == 2:
                        gates_of(g + 1, False)
                    if following:
                        for q in (0, 2, 4, 6):
                            keep_act(u + 4, False, 0, q)

                def group(g, first, last):
                    tile(g, 0, 1, not first)
                    with act.Fori(1, FT - 1) as f:
                        tile(g, f, 1)
                    tile(g, FT - 1, 0 if last else 2)
                    if last:
                        act.wait_ge(shift_ready, GROUPS)
                        norm_rows(g, range(PR))

                act.sem_inc(kept_act, KEPT)
                gates_of(0, True)
                for q in (0, 2, 4, 6):
                    keep_act(0, False, 0, q)
                all_groups(act, group)

            @block.vector
            def _(dve):
                LINKS = 2 + PR

                def copy(dst, src):
                    return nc.vector.tensor_copy(dst, src)

                def keep_dve(u, second, s, q):
                    keep(dve, copy, u, second, s, q, kept_dve)

                def add_second(g, f, cd, q):
                    k = 8 * cd + q
                    if q % 4 == 0:
                        dve.wait_ge(work_dve, CREDIT + g * DVE_G + INIT + f * NL2 + k - 4)
                    dve.wait_ge(work, second_index(g, f, k))
                    part = acc[:, 2 * q:2 * q + 2, 256 * cd:256 * cd + 256]
                    nc.vector.tensor_tensor(part, ps_w[:, k % 4, :].rearrange("p (i d) -> p i d", d=256),
                                            part, ALU.add).then_inc(work_dve, 1)

                def second_bias(g):
                    def spread(i):
                        if i >= 2:
                            dve.wait_ge(work, init_index(g, i - 2))
                        for h in range(2):
                            last = nc.vector.tensor_copy(
                                gtok[:, i % 2, h * NODES:(h + 1) * NODES],
                                g9[:, bass.ds(g * GB + 2 * i + h, 1)].broadcast_to([E + 1, NODES]))
                        last.then_inc(gtok_ready, 1)

                    spread(0)
                    spread(1)
                    for i in range(INIT):
                        dve.wait_ge(acc_in[i // 4], 16 * (g + 1))
                        dve.wait_ge(work, init_index(g, i))
                        nc.vector.tensor_tensor(acc[:, i, :], ps_w[:, i % 4, :], acc[:, i, :],
                                                ALU.add).then_inc(work_dve, 1)
                        if i + 2 < INIT:
                            spread(i + 2)

                def link(ins, g, k, by_stats=False):
                    ins.then_inc(link_f, 1)
                    if by_stats:
                        wait_apart(dve, link_f, g * LINKS + k, power_set, 1)
                    else:
                        dve.wait_ge(link_f, g * LINKS + k)

                def stats(g):
                    dve.wait_ge(work_dve, CREDIT + (g + 1) * DVE_G)
                    for i in range(PR):
                        ins = nc.vector.bn_stats(st[:, i, :], acc[:, i, :])
                    link(ins, g, 1, True)
                    for i in range(PR):
                        ins = nc.vector.bn_aggr(ag[:, i, :], st[:, i, :])
                    link(ins, g, 2)
                    nc.vector.tensor_scalar(ve[:], ag[:, :, 1], EPS, None, ALU.add).then_inc(var_f, 1)
                    dve.wait_ge(rstd_f, g + 1)
                    nc.vector.scalar_tensor_tensor(out=shift[:], in0=ag[:, :, 0], scalar=-1.0, in1=rs[:],
                                                   op0=ALU.mult, op1=ALU.mult).then_inc(shift_ready, 1)

                def scale_rows(g, rows):
                    for i in rows:
                        dve.wait_ge(normed, g * PR + i + 1)
                        link(nc.vector.tensor_tensor(acc[:, i, :], acc[:, i, :], lnw[:, 0, :], ALU.mult),
                             g, 3 + i)
                        nc.vector.tensor_tensor(acc[:, i, :], acc[:, i, :], lnw[:, 1, :], ALU.add).then_inc(scaled, 1)

                def tile(g, f, following, unfinished=False):
                    u = g * UNITS + f * 4
                    if unfinished:
                        stats(g - 1)
                    for q in (1, 3, 5, 7):
                        keep_dve(u + 1, False, 1, q)
                        if unfinished:
                            scale_rows(g - 1, range(q - 1, q + 1))
                    for q in (1, 3, 5, 7):
                        keep_dve(u + 2, True, 0, q)
                        if unfinished:
                            scale_rows(g - 1, range(8 + q - 1, 8 + q + 1))
                    if isinstance(f, int) and f == 0:
                        second_bias(g)
                    for q in range(8):
                        if q % 2:
                            keep_dve(u + 3, True, 1, q)
                        add_second(g, f, 0, q)
                    for q in range(8):
                        if q % 2 and following:
                            keep_dve(u + 4, False, 0, q)
                        add_second(g, f, 1, q)

                def group(g, first, last):
                    tile(g, 0, 1, not first)
                    with dve.Fori(1, FT - 1) as f:
                        tile(g, f, 1)
                    tile(g, FT - 1, 0 if last else 2)
                    if last:
                        stats(g)
                        scale_rows(g, range(PR))

                nc.vector.memset(power[:], -0.5).then_inc(power_set, 1)
                dve.sem_inc(work_dve, CREDIT)
                dve.sem_inc(kept_dve, KEPT)
                for q in (1, 3, 5, 7):
                    keep_dve(0, False, 0, q)
                all_groups(dve, group)

            @block.gpsimd
            def _(pool):
                def load_nT(g):
                    pool.dma_start(nT[:], nTt[bass.ds(g, 1)].rearrange("g p k c -> (g p) k c")).then_inc(nT_loaded, 16)

                def load_acc(g, a):
                    pool.dma_start(acc[:, 4 * a:4 * a + 4, :],
                                   n2t[bass.ds(g * (PR // 4) + a, 1)].rearrange("a p i d -> (a p) i d")
                                   ).then_inc(acc_in[a], 16)

                PAIR = PR // 2

                def load_x(g, i):
                    pool.dma_start(x_row[:, i % 2], x1t[bass.ds(g * PAIR + i, 1)].rearrange("a p i d -> (a p) i d")
                                   ).then_inc(x_in[i % 2], 16)

                def group(g, first, last):
                    for i in range(2):
                        if not first:
                            wait_apart(pool, y_out[i], 16 * g * (PAIR // 2), power_set, 1)
                        load_x(g, i)
                    if not last:
                        wait_apart(pool, work, first_index(g, FT - 1, FIRST.index("Lb1")), power_set, 1)
                        load_nT(g + 1)
                    pool.wait_ge(var_f, g + 1)
                    nc.gpsimd.tensor_tensor(rs[:], ve[:], power[:], ALU.pow).then_inc(rstd_f, 1)
                    for i in range(PAIR):
                        b = i % 2
                        pool.wait_ge(x_in[b], 16 * (g * (PAIR // 2) + i // 2 + 1))
                        pool.wait_ge(scaled, g * PR + 2 * i + 2)
                        nc.gpsimd.tensor_tensor(x_row[:, b], acc[:, 2 * i:2 * i + 2, :], x_row[:, b],
                                                ALU.add).then_inc(y_ready, 1)
                        wait_apart(pool, y_ready, g * PAIR + i + 1, power_set, 1)
                        if i % 2 and not last:
                            load_acc(g + 1, i // 2)
                        pool.dma_start(yt[bass.ds(g * PAIR + i, 1)].rearrange("a p i d -> (a p) i d"),
                                       x_row[:, b]).then_inc(y_out[b], 16)
                        if 1 <= i < PAIR - 1:
                            wait_apart(pool, y_out[1 - b], 16 * (g * (PAIR // 2) + (i - 1) // 2 + 1), power_set, 1)
                            load_x(g, i + 1)

                pool.wait_ge(power_set, 1)
                load_nT(0)
                for a in range(PR // 4):
                    load_acc(0, a)
                all_groups(pool, group)
                for b in range(2):
                    pool.wait_ge(y_out[b], 16 * GROUPS * PAIR // 2)


def graph_ffn(nc, t):
    with ExitStack() as ctx:
        def sb(name, shape, dt=F32):
            return ctx.enter_context(nc.sbuf_tensor(name, shape, dt))

        keep = {
            "ident": sb("ident", [P, P]),
            "gate_sum": sb("gate_sum", [P, KD, GRAPHS]),
            "gblk": sb("gblk", [P, GROUPS, 2, GB], BF16),
            "g9": sb("g9", [E + 1, GRAPHS]),
            "b1m": sb("b1m", [P, FT, GRAPHS]),
            "lnw": sb("lnw", [P, 2, D]),
            "tvb2": sb("tvb2", [E + 1, D]),
        }
        ident_in = ctx.enter_context(nc.semaphore("ident_in"))
        with nc.Block() as block:
            @block.sync
            def _(sp):
                sp.dma_start(keep["ident"][:], t["ident"]).then_inc(ident_in, 16)
                sp.wait_ge(ident_in, 16)
        attend(nc, t, keep)
        gates(nc, t, keep)
        feed(nc, t, keep)


def kernel(**inputs):
    import concourse.bacc as bacc
    from concourse.bass_utils import run_bass_kernel_spmd

    i = {k: np.asarray(v) for k, v in inputs.items()}

    def rows_of(w, matrix):
        n = w.shape[0]
        if matrix == 1:
            return w.reshape(n, F // 64, 2, 32, D).transpose(0, 2, 1, 3, 4).reshape(n, 2, HROW)
        return w.reshape(n, 2, 2, P, FT, P).transpose(0, 2, 1, 4, 3, 5).reshape(n, 2, HROW)

    def shares(w, matrix, count):
        r = rows_of(w, matrix)
        return r.reshape(r.shape[0], 2, count, -1).transpose(0, 2, 1, 3).reshape(-1)

    sel9 = np.zeros((E + 1, 2), np.float32)
    sel9[:E, 0] = 1.0
    sel9[E, 1] = 1.0
    arrays = {
        "x": i["x"].reshape(TOK, D),
        "adj": i["adj"],
        "wqkv": i["L0_gnn_w_qkv"],
        "wproj": i["L0_gnn_w_proj"],
        "bproj": i["L0_gnn_b_proj"],
        "gamma": i["L0_gnn_ln_gamma"],
        "beta": i["L0_gnn_ln_beta"],
        "gfc1T": i["L0_ffn_gfc1_w"].T,
        "gfc1_b": i["L0_ffn_gfc1_b"].reshape(KD, P).T,
        "fc2T": i["L0_ffn_gfc2_w"].T,
        "fc2_b": i["L0_ffn_gfc2_b"].reshape(E, 1),
        "W1": shares(i["L0_ffn_W1"][None], 1, NST),
        "b1": i["L0_ffn_b1"],
        "W2": shares(i["L0_ffn_W2"][None], 2, NST),
        "b2": i["L0_ffn_b2"],
        "ln_g": i["L0_ffn_ln_g"],
        "ln_b": i["L0_ffn_ln_b"],
        "tvW1": shares(i["L0_ffn_tv_W1"], 1, NST // E),
        "tvb1": i["L0_ffn_tv_b1"],
        "tvW2": shares(i["L0_ffn_tv_W2"], 2, NST // E),
        "tvb2": i["L0_ffn_tv_b2"],
        "tv_ln_g": i["L0_ffn_tv_ln_g"],
        "tv_ln_b": i["L0_ffn_tv_ln_b"],
        "ident": np.eye(P, dtype=np.float32),
        "sel": selection(),
        "sel9": sel9,
    }
    arrays = {k: np.ascontiguousarray(v) for k, v in arrays.items()}
    nc = bacc.Bacc("TRN2", target_bir_lowering=False, num_devices=1)
    t = {}
    for name, a in arrays.items():
        t[name] = nc.dram_tensor(f"in_{name}", a.shape, mybir.dt.from_np(a.dtype), kind="ExternalInput").ap()
    t["y"] = nc.dram_tensor("out_y", (TOK, D), F32, kind="ExternalOutput").ap()
    for name, shape, dt in (("x1", (TOK, D), F32), ("n2", (TOK, D), F32), ("n2T", (KD, P, TOK), F32),
                            ("s1", (KROWS * HROW,), BF16), ("s2", (KROWS * HROW,), BF16)):
        t[name] = nc.dram_tensor(f"scratch_{name}", shape, dt, kind="Internal").ap()
    graph_ffn(nc, t)
    r = run_bass_kernel_spmd(nc, [{f"in_{k}": v for k, v in arrays.items()}], core_ids=[0])
    return r.results[0]["out_y"].reshape(GRAPHS, NODES, D)
```

```python
from contextlib import ExitStack

import concourse.bass as bass
import numpy as np
from concourse import mybir

P = 128
GRAPHS, NODES, D = 128, 64, 512
F, E, H = 2048, 8, 8
HD = D // H
TOK = GRAPHS * NODES
KD = D // P
EPS = 1e-5
LN_MERGE = 0.03
NEG = -1e30

T_PART = [0, 1, 2, 0, 1, 0]
G_PART = [0, 0, 0, 1, 1, 2]
PAIRS = len(T_PART)
BASE_ROW = PAIRS * E
HALF = 56
KROWS = 2 * HALF
MAT = F * D
HROW = MAT // 2

GB = 32
GROUPS = GRAPHS // GB
GT = GB * NODES
PR = GT // P
FT = F // P
UNIT = 16384
PIECE = UNIT // 4

ALU = mybir.AluOpType
ACT = mybir.ActivationFunctionType
AX = mybir.AxisListType
F32 = mybir.dt.float32
BF16 = mybir.dt.bfloat16
F32R = mybir.dt.float32r


def wait_apart(eng, sem, value, met, met_value):
    if not isinstance(value, int):
        value = eng.to_reg(value)
        eng.wait_ge(met, met_value)
    eng.wait_ge(sem, value)


def selection():
    sel = np.zeros((P, 2, 4), np.float32)
    for half in range(2):
        for c in range(PAIRS):
            for e in range(E):
                sel[half * HALF + c * E + e, half, G_PART[c]] = 1.0
        for part in range(3):
            sel[half * HALF + BASE_ROW + part, half, 3] = 1.0
    return sel.reshape(P, 8)


class Step:

    def __init__(self, j, par):
        self.j, self.par = j, par
        self.n = 2 * j + par

    def __add__(self, k):
        q = self.par + k
        return Step(self.j + q // 2, q % 2)

    def exists(self):
        return not isinstance(self.n, int) or self.n >= 0


ST = 256
NST = TOK // ST
TI = ST // P
CUT_E = E * MAT // NST // P
CUT_B = MAT // NST // P
CUT = CUT_E + CUT_B


def attend(nc, t, keep):
    gate_sum = keep["gate_sum"]
    ident = keep["ident"]
    with ExitStack() as ctx:
        def sb(name, shape, dt=F32):
            return ctx.enter_context(nc.sbuf_tensor(name, shape, dt))

        def sem(name):
            return ctx.enter_context(nc.semaphore(name))

        wqkv = sb("wqkv", [P, 2, KD, 3 * D], F32R)
        wproj = sb("wproj", [P, KD, D])
        gfc1 = sb("gfc1", [P, KD, D])
        gfc1_b = sb("gfc1_b", [P, KD])
        bproj = sb("bproj", [P, D])
        gamma = sb("gamma", [P, D])
        beta = sb("beta", [P, D])
        adj = sb("adj", [P, NODES])
        mask = sb("mask", [P, NODES])
        power = sb("power", [P, TI])
        x_in = sb("x_in", [P, 2, TI, D])
        x_res = sb("x_res", [P, TI, D])
        n1 = sb("n1", [P, TI, D])
        n1T = sb("n1T", [P, 2, KD, ST], F32R)
        qkT = sb("qkT", [P, 2 * KD, ST])
        v = sb("v", [P, TI, D])
        scores = sb("scores", [P, 2, H, NODES])
        top = sb("top", [P, 2, H])
        total = sb("total", [P, 2, H])
        inv = sb("inv", [P, 2, H])
        probs = sb("probs", [P, TI, 2, H // 2, P])
        probsT = sb("probsT", [P, TI, H, P])
        oT = sb("oT", [P, TI, KD, P])
        o2 = sb("o2", [P, TI, D])
        x1 = sb("x1", [P, TI, D])
        n2 = sb("n2", [P, TI, D])
        n2T = sb("n2T", [P, KD, ST])
        gate_h = sb("gate_h", [P, 2, 2, ST])
        whole = sb("whole", [P, 2, CUT])
        part = [sb(f"part{k}", [P, 2, CUT], BF16) for k in range(3)]
        zero = sb("zero", [P, 512], BF16)
        st_x, ag_x, rs_x = sb("st_x", [P, TI, 6]), sb("ag_x", [P, TI, 2]), sb("rs_x", [P, TI])
        ve_x = sb("ve_x", [P, TI])
        st_y, ag_y, rs_y = sb("st_y", [P, 2 * TI, 6]), sb("ag_y", [P, 2 * TI, 2]), sb("rs_y", [P, 2 * TI])
        ve_y = sb("ve_y", [P, 2 * TI])

        ps_x = ctx.enter_context(nc.psum_tensor("ps_x", [P, 4, 512], F32))
        ps_y = ctx.enter_context(nc.psum_tensor("ps_y", [P, 2, 512], F32))
        ps_z = ctx.enter_context(nc.psum_tensor("ps_z", [P, 2, 512], F32))

        consts_in, consts_set = sem("consts_in"), sem("consts_set")
        rest_added = sem("rest_added")
        adj_in, qkv_in, wqkv_high, wqkv_cut = sem("adj_in"), sem("qkv_in"), sem("wqkv_high"), sem("wqkv_cut")
        n1T_cut = sem("n1T_cut")
        x_loaded = [sem("x_loaded0"), sem("x_loaded1")]
        res_loaded = sem("res_loaded")
        x_filled, y_filled, z_filled = sem("x_filled"), sem("y_filled"), sem("z_filled")
        x_emptied = sem("x_emptied")
        y_emptied_act, y_emptied_dve = sem("y_emptied_act"), sem("y_emptied_dve")
        z_emptied = sem("z_emptied")
        gate_summed = sem("gate_summed")
        n1_ready, var_x, rstd_x = sem("n1_ready"), sem("var_x"), sem("rstd_x")
        shifted, exp_done, inv_ready, probs_ready = sem("shifted"), sem("exp_done"), sem("inv_ready"), sem("probs_ready")
        var_y, rstd_y = sem("var_y"), sem("rstd_y")
        x1_ready, n2_ready = sem("x1_ready"), sem("n2_ready")
        x1_stored, n2_stored, n2T_stored = sem("x1_stored"), sem("n2_stored"), sem("n2T_stored")
        dve_link = sem("dve_link")
        whole_in = [sem(f"whole_in{m}") for m in range(2)]
        high_cut = [sem(f"high_cut{m}") for m in range(2)]
        high_off = [sem(f"high_off{m}") for m in range(2)]
        mid_cut = [sem(f"mid_cut{m}") for m in range(2)]
        low_cut = [sem(f"low_cut{m}") for m in range(2)]
        parts_stored = [sem(f"parts_stored{m}") for m in range(2)]
        zero_set, zero_stored = sem("zero_set"), sem("zero_stored")

        rows_e = [t[f"s{m}"].rearrange("(h a p c) -> a h p c", h=2, p=64, c=CUT_E) for m in (1, 2)]
        rows_b = [t[f"s{m}"].rearrange("(h a p c) -> a h p c", h=2, p=64, c=CUT_B) for m in (1, 2)]
        BLOCKS_E = HROW // (64 * CUT_E)
        BLOCKS_B = HROW // (64 * CUT_B)
        STORES = 16 * (PAIRS + 3)

        XU, YU, ZU = 8, 10, 4
        Y_ORDER = ["S0", "S1", "P0a", "P0b", "O0", "P1a", "P1b", "R0", "O1", "R1"]
        Y_DVE = [u[0] in "SR" for u in Y_ORDER]
        NDVE = sum(Y_DVE)

        def yi(name):
            return Y_ORDER.index(name)

        def y_free(pe, s, k, needed=None):
            if needed is not None:
                rank = act_rank(needed)
                if not Y_DVE[k - 2]:
                    rank = max(rank, act_rank(Y_ORDER[k - 2]))
                pe.wait_ge(y_emptied_act, s.n * (YU - NDVE) + rank)
                if not Y_DVE[k - 2]:
                    return
            prev, back = (k - 2) % YU, k < 2
            ps = s + (-1) if back else s
            if not ps.exists():
                return
            rank = sum(1 for i in range(prev + 1) if Y_DVE[i] == Y_DVE[prev])
            if Y_DVE[prev]:
                wait_apart(pe, y_emptied_dve, ps.n * NDVE + rank, consts_in, 16 * NCONST)
            else:
                wait_apart(pe, y_emptied_act, ps.n * (YU - NDVE) + rank, consts_in, 16 * NCONST)

        def bank_y(k):
            return ps_y[:, k % 2, :]

        def act_rank(name):
            return sum(1 for i in range(yi(name) + 1) if not Y_DVE[i])

        def dve_rank(name):
            return sum(1 for i in range(yi(name) + 1) if Y_DVE[i])

        xt = t["x"].rearrange("(s i p) d -> s p i d", i=TI, p=P)
        x1t = t["x1"].rearrange("(s i p) d -> s p i d", i=TI, p=P)
        n2t = t["n2"].rearrange("(s i p) d -> s p i d", i=TI, p=P)
        n2Tt = t["n2T"].rearrange("k p (s c) -> s p k c", c=ST)

        def tile_of(dram, s):
            return dram[bass.ds(s.n, 1)].rearrange("s p i d -> (s p) i d")

        def run(engine, body, before, after):
            before()
            for n in range(4):
                body(Step(n // 2, n % 2), True, True)
            with engine.Fori(2, NST // 2 - 1) as j:
                body(Step(j, 0), True, True)
                body(Step(j, 1), True, True)
            body(Step(NST // 2 - 1, 0), True, False)
            body(Step(NST // 2 - 1, 1), False, False)
            after()

        def raw_wqkv(m):
            place = [whole[:, 0, 0:KD * D], whole[:, 1, 0:KD * D], qkT[:].rearrange("p c n -> p (c n)")][m]
            return place.rearrange("p (c n) -> p c n", n=D)

        NCONST = 6
        with nc.Block() as block:
            @block.sync
            def _(sp):
                def load_x(s):
                    q = s + (-2)
                    if q.exists():
                        sp.wait_ge(n1_ready, q.n + 1)
                    sp.dma_start(x_in[:, s.par], tile_of(xt, s)).then_inc(x_loaded[s.par], 16)

                def load_whole(s, m):
                    for src, at, n in ((t[f"tvW{m + 1}"], 0, CUT_E), (t[f"W{m + 1}"], CUT_E, CUT_B)):
                        src = src.rearrange("(s p c) -> s p c", p=P, c=n)
                        sp.dma_start(whole[:, m, at:at + n], src[bass.ds(s.n, 1)].rearrange("s p c -> (s p) c")
                                     ).then_inc(whole_in[m], 16)

                def store_parts(s, m):
                    wait_apart(sp, low_cut[m], s.n + 1, zero_set, 1)
                    for c in range(PAIRS):
                        sp.dma_start(rows_e[m][bass.ds(c * E * BLOCKS_E + s.n, 1)].rearrange("a h p c -> (a h) p c"),
                                     part[T_PART[c]][:, m, 0:CUT_E]).then_inc(parts_stored[m], 16)
                    for k in range(3):
                        sp.dma_start(rows_b[m][bass.ds((BASE_ROW + k) * BLOCKS_B + s.n, 1)
                                               ].rearrange("a h p c -> (a h) p c"),
                                     part[k][:, m, CUT_E:CUT]).then_inc(parts_stored[m], 16)

                def store_n2T(s):
                    sp.wait_ge(z_emptied, ZU * s.n + 2)
                    sp.dma_start(n2Tt[bass.ds(s.n, 1)].rearrange("s p k c -> (s p) k c"),
                                 n2T[:]).then_inc(n2T_stored, 16)

                def store_x1(s):
                    sp.wait_ge(x1_ready, s.n + 1)
                    sp.dma_start(tile_of(x1t, s), x1[:]).then_inc(x1_stored, 16)

                def store_n2(s):
                    sp.wait_ge(n2_ready, s.n + 1)
                    sp.dma_start(tile_of(n2t, s), n2[:]).then_inc(n2_stored, 16)

                def before():
                    load_x(Step(0, 0))
                    for h in range(2):
                        sp.dma_start(adj[64 * h:64 * h + 64, :], t["adj"]).then_inc(adj_in, 16)
                    for m in range(3):
                        sp.dma_start(raw_wqkv(m), t["wqkv"][:, m * D:(m + 1) * D].rearrange("(k p) n -> p k n", p=P)
                                     ).then_inc(qkv_in, 16)
                    for dst, src in ((gfc1, "gfc1T"), (wproj, "wproj")):
                        sp.dma_start(dst[:], t[src].rearrange("(k p) n -> p k n", p=P)).then_inc(consts_in, 16)
                    sp.dma_start(gfc1_b[:], t["gfc1_b"]).then_inc(consts_in, 16)
                    for dst, src in ((bproj, "bproj"), (gamma, "gamma"), (beta, "beta")):
                        sp.dma_start(dst[:], t[src].partition_broadcast(P)).then_inc(consts_in, 16)
                    load_x(Step(0, 1))
                    for m in range(2):
                        sp.wait_ge(wqkv_cut, m + 1)
                        load_whole(Step(0, 0), m)
                    sp.wait_ge(zero_set, 1)
                    for m in (1, 2):
                        for row in range(KROWS):
                            if row % HALF >= BASE_ROW + 3:
                                dst = t[f"s{m}"][row * HROW:(row + 1) * HROW].rearrange("(p a c) -> p a c", p=P, c=512)
                                sp.dma_start(dst, zero[:].unsqueeze(1).broadcast_to([P, dst.shape[1], 512])
                                             ).then_inc(zero_stored, 16)

                def body(s, has_x, has_l):
                    if has_l:
                        load_x(s + 2)
                    store_parts(s, 0)
                    if has_x:
                        load_whole(s + 1, 0)
                    q = s + (-1)
                    if q.exists():
                        store_x1(q)
                    sp.dma_start(x_res[:], tile_of(xt, s)).then_inc(res_loaded, 16)
                    if q.exists():
                        store_n2(q)
                    z = s + (-2)
                    if z.exists():
                        store_n2T(z)
                    store_parts(s, 1)
                    if has_x:
                        load_whole(s + 1, 1)

                def after():
                    end = Step(NST // 2 - 1, 1)
                    store_n2T(end + (-1))
                    store_x1(end)
                    store_n2(end)
                    store_n2T(end)
                    sp.wait_ge(n2T_stored, 16 * NST)
                    sp.wait_ge(x1_stored, 16 * NST)
                    sp.wait_ge(n2_stored, 16 * NST)
                    sp.wait_ge(zero_stored, 16 * 2 * 2 * (HALF - BASE_ROW - 3))
                    for m in range(2):
                        sp.wait_ge(parts_stored[m], STORES * NST)

                run(sp, body, before, after)

            @block.tensor
            def _(pe):
                def product(out, left, right):
                    steps = [(c, a, b) for c in range(KD) for a, b in ((0, 0), (0, 1), (1, 0))]
                    for n, (c, a, b) in enumerate(steps):
                        last = pe.matmul(out, left(a, c), right(b, c),
                                         start=(n == 0), stop=(n == len(steps) - 1))
                    return last

                def x_fill(s, k):
                    q, prev = (s, k - 4) if k >= 4 else (s + (-1), k + 4)
                    if k == 2:
                        pe.wait_ge(n1T_cut, s.n + 1)
                    elif q.exists():
                        pe.wait_ge(x_emptied, XU * q.n + prev + 1)
                    bank = ps_x[:, k % 4, :]
                    if k < 2:
                        if k == 0:
                            pe.wait_ge(n1_ready, s.n + 1)
                        for c in range(KD):
                            last = pe.transpose(bank[:, c * P:(c + 1) * P], n1[:, k, c * P:(c + 1) * P], ident[:])
                    elif k < 6:
                        for m in range(2):
                            ch = 2 * (k - 2) + m
                            last = product(bank[:, m * ST:(m + 1) * ST],
                                           lambda part, c: wqkv[:, part, c, ch * P:(ch + 1) * P],
                                           lambda part, c: n1T[:, part, c, :])
                    else:
                        i = k - 6
                        last = product(bank[:], lambda part, c: n1T[:, part, c, i * P:(i + 1) * P],
                                       lambda part, c: wqkv[:, part, c, 2 * D:3 * D])
                    last.then_inc(x_filled, 1)

                def y_fill(s, name):
                    k, i = yi(name), int(name[1])
                    y_free(pe, s, k, {"O": f"P{i}b", "R": f"O{i}"}.get(name[0]))
                    bank = bank_y(k)
                    if name[0] == "S":
                        if i == 0:
                            wait_apart(pe, x_emptied, XU * s.n + 6, consts_in, 16 * NCONST)
                        r = HD * i
                        for at in range(0, ST, NODES):
                            g = at // NODES
                            out_rows = slice(NODES * (g % 2), NODES * (g % 2) + NODES)
                            for h in range(H // 2):
                                col = ((g // 2) * (H // 2) + h) * NODES
                                last = pe.matmul(bank[out_rows, col:col + NODES],
                                                 qkT[r:r + HD, h, at:at + NODES],
                                                 qkT[r:r + HD, KD + h, at:at + NODES],
                                                 start=True, stop=True)
                    elif name[0] == "P":
                        odd = int(name[2] == "b")
                        pe.wait_ge(probs_ready, 2 * s.n + odd + 1)
                        for h in range(4):
                            last = pe.transpose(bank[:, h * P:(h + 1) * P], probs[:, i, odd, h, :], ident[:])
                    elif name[0] == "O":
                        if i == 0:
                            wait_apart(pe, x_emptied, XU * (s.n + 1), consts_in, 16 * NCONST)
                        for h in range(H):
                            r = HD * (h % 2)
                            last = pe.matmul(bank[r:r + HD, (h // 2) * P:(h // 2 + 1) * P],
                                             v[:, i, h * HD:(h + 1) * HD],
                                             probsT[:, i, (h % 2) * (H // 2) + h // 2, :],
                                             start=True, stop=True)
                    else:
                        for c in range(KD):
                            last = pe.matmul(bank[:], oT[:, i, c, :], wproj[:, c, :],
                                             start=(c == 0), stop=(c == KD - 1))
                    last.then_inc(y_filled, 1)

                def z_fill(s, k):
                    if not s.exists():
                        return
                    q, prev = (s, k - 2) if k >= 2 else (s + (-1), k + 2)
                    if k == 2:
                        pe.wait_ge(z_emptied, ZU * s.n + 2)
                    elif q.exists():
                        pe.wait_ge(z_emptied, ZU * q.n + prev + 1)
                    bank = ps_z[:, k % 2, :]
                    if k < 2:
                        if k == 0:
                            pe.wait_ge(n2_ready, s.n + 1)
                        for c in range(KD):
                            last = pe.transpose(bank[:, c * P:(c + 1) * P], n2[:, k, c * P:(c + 1) * P], ident[:])
                    else:
                        for m in range(2):
                            ch = 2 * (k - 2) + m
                            for c in range(KD):
                                last = pe.matmul(bank[:, m * ST:(m + 1) * ST], gfc1[:, c, ch * P:(ch + 1) * P],
                                                 n2T[:, c, :], start=(c == 0), stop=(c == KD - 1))
                    last.then_inc(z_filled, 1)

                def before():
                    pe.wait_ge(wqkv_cut, 3)
                    for k in range(XU):
                        x_fill(Step(0, 0), k)
                    pe.wait_ge(consts_in, 16 * NCONST)

                def body(s, has_x, has_l):
                    z = s + (-2)

                    def x(k):
                        if has_x:
                            x_fill(s + 1, k)
                    y_fill(s, "S0")
                    x(0)
                    x(1)
                    y_fill(s, "S1")
                    z_fill(z, 0)
                    z_fill(z, 1)
                    x(2)
                    z_fill(z, 2)
                    x(3)
                    y_fill(s, "P0a")
                    y_fill(s, "P0b")
                    z_fill(z, 3)
                    y_fill(s, "O0")
                    y_fill(s, "P1a")
                    y_fill(s, "P1b")
                    x(4)
                    y_fill(s, "R0")
                    y_fill(s, "O1")
                    x(5)
                    x(6)
                    x(7)
                    y_fill(s, "R1")

                def after():
                    for s in (Step(NST // 2 - 1, 0), Step(NST // 2 - 1, 1)):
                        for k in range(ZU):
                            z_fill(s, k)

                run(pe, body, before, after)

            @block.scalar
            def _(act):
                def x_empty(s, k):
                    act.wait_ge(x_filled, XU * s.n + k + 1)
                    bank = ps_x[:, k % 4, :]
                    if k < 2:
                        dst = n1T[:, 0, :, k * P:(k + 1) * P]
                        src = bank.rearrange("p (c n) -> p c n", n=P)
                    elif k < 6:
                        dst = qkT[:, 2 * (k - 2):2 * (k - 2) + 2, :]
                        src = bank.rearrange("p (c n) -> p c n", n=ST)
                    else:
                        dst, src = v[:, k - 6, :], bank
                    nc.scalar.activation(dst, src, ACT.Copy).then_inc(x_emptied, 1)

                def y_empty(s, name):
                    k, i = yi(name), int(name[1])
                    act.wait_ge(y_filled, YU * s.n + k + 1)
                    src = bank_y(k).rearrange("p (c n) -> p c n", n=P)
                    if name[0] == "P":
                        h = (H // 2) * (name[2] == "b")
                        dst = probsT[:, i, h:h + 4, :]
                    else:
                        dst = oT[:, i]
                    nc.scalar.activation(dst, src, ACT.Copy).then_inc(y_emptied_act, 1)

                def exponent(s, i):
                    act.wait_ge(shifted, TI * s.n + i + 1)
                    nc.scalar.activation(scores[:, i], scores[:, i], ACT.Exp).then_inc(exp_done, 1)

                def z_empty(s, k):
                    if not s.exists():
                        return
                    q = s + (-1)
                    act.wait_ge(z_filled, ZU * s.n + k + 1)
                    bank = ps_z[:, k % 2, :]
                    if k < 2:
                        if k == 0 and q.exists():
                            act.wait_ge(n2T_stored, 16 * (q.n + 1))
                        nc.scalar.activation(n2T[:, :, k * P:(k + 1) * P], bank.rearrange("p (c n) -> p c n", n=P),
                                             ACT.Copy).then_inc(z_emptied, 1)
                        return
                    if q.exists():
                        act.wait_ge(gate_summed, 2 * q.n + k - 1)
                    for m in range(2):
                        ch = 2 * (k - 2) + m
                        last = nc.scalar.activation(gate_h[:, k - 2, m, :], bank[:, m * ST:(m + 1) * ST], ACT.Relu,
                                                    bias=gfc1_b[:, ch:ch + 1])
                    last.then_inc(z_emptied, 1)

                def cut_high(s, m):
                    act.wait_ge(whole_in[m], 32 * (s.n + 1))
                    q = s + (-1)
                    if q.exists():
                        act.wait_ge(parts_stored[m], STORES * (q.n + 1))
                    nc.scalar.activation(part[0][:, m, :], whole[:, m, :], ACT.Copy).then_inc(high_cut[m], 1)

                def cut_mid(s, m):
                    act.wait_ge(high_off[m], s.n + 1)
                    nc.scalar.activation(part[1][:, m, :], whole[:, m, :], ACT.Copy).then_inc(mid_cut[m], 1)

                def before():
                    act.wait_ge(qkv_in, 48)
                    for m in range(3):
                        nc.scalar.activation(wqkv[:, 0, :, m * D:(m + 1) * D], raw_wqkv(m),
                                             ACT.Copy).then_inc(wqkv_high, 1)
                    for k in range(XU):
                        x_empty(Step(0, 0), k)
                    act.wait_ge(consts_in, 16 * NCONST)

                def body(s, has_x, has_l):
                    z = s + (-2)

                    def x(k):
                        if has_x:
                            x_empty(s + 1, k)
                    x(0)
                    x(1)
                    exponent(s, 0)
                    z_empty(z, 0)
                    z_empty(z, 1)
                    exponent(s, 1)
                    cut_high(s, 0)
                    x(2)
                    z_empty(z, 2)
                    cut_mid(s, 0)
                    x(3)
                    y_empty(s, "P0a")
                    y_empty(s, "P0b")
                    z_empty(z, 3)
                    y_empty(s, "O0")
                    cut_high(s, 1)
                    y_empty(s, "P1a")
                    y_empty(s, "P1b")
                    x(4)
                    y_empty(s, "O1")
                    cut_mid(s, 1)
                    x(5)
                    x(6)
                    x(7)

                def after():
                    for s in (Step(NST // 2 - 1, 0), Step(NST // 2 - 1, 1)):
                        for k in range(ZU):
                            z_empty(s, k)

                run(act, body, before, after)

            @block.vector
            def _(dve):
                L_LINKS, Y_LINKS, W_LINKS = 2, TI * 2, 6

                def linker(base):
                    count = [0]

                    def link(ins, by_stats=False):
                        count[0] += 1
                        ins.then_inc(dve_link, 1)
                        if by_stats:
                            wait_apart(dve, dve_link, base + count[0], consts_in, 16 * NCONST)
                        else:
                            dve.wait_ge(dve_link, base + count[0])
                    return link, count

                def normalise(s, base):
                    link, count = linker(base)
                    q = s + (-1)
                    dve.wait_ge(x_loaded[s.par], 16 * (s.j + 1))
                    for i in range(TI):
                        last = nc.vector.bn_stats(st_x[:, i, :], x_in[:, s.par, i, :])
                    link(last, True)
                    for i in range(TI):
                        last = nc.vector.bn_aggr(ag_x[:, i, :], st_x[:, i, :])
                    link(last)
                    if q.exists():
                        dve.wait_ge(rstd_x, q.n + 1)
                    nc.vector.tensor_scalar(ve_x[:], ag_x[:, :, 1], EPS, None, ALU.add).then_inc(var_x, 1)
                    dve.wait_ge(rstd_x, s.n + 1)
                    if q.exists():
                        dve.wait_ge(x_filled, XU * q.n + 2)
                    for i in range(TI):
                        last = nc.vector.tensor_scalar(n1[:, i, :], x_in[:, s.par, i, :], ag_x[:, i, 0:1],
                                                       rs_x[:, i:i + 1], ALU.subtract, ALU.mult)
                    last.then_inc(n1_ready, 1)
                    assert count[0] == L_LINKS

                def cut_n1T(s):
                    dve.wait_ge(x_emptied, XU * s.n + 2)
                    high, low = (n1T[:, part].rearrange("p c (k n) -> p k c n", n=P) for part in range(2))
                    nc.vector.tensor_tensor(low, ps_x[:, 0:2, :].rearrange("p k (c n) -> p k c n", n=P),
                                            high.bitcast(F32), ALU.subtract).then_inc(n1T_cut, 1)

                def softmax_shift(s, i, link):
                    q = s + (-1)
                    dve.wait_ge(y_filled, YU * s.n + yi(f"S{i}") + 1)
                    if q.exists():
                        dve.wait_ge(probs_ready, 2 * q.n + i + 1)
                    nc.vector.scalar_tensor_tensor(
                        out=scores[:, i], in0=bank_y(yi(f"S{i}")).rearrange("p (h m) -> p h m", h=H),
                        scalar=float(HD) ** -0.5, in1=mask[:].unsqueeze(1).broadcast_to([P, H, NODES]),
                        op0=ALU.mult, op1=ALU.add).then_inc(y_emptied_dve, 1)
                    dve.wait_ge(y_emptied_dve, NDVE * s.n + dve_rank(f"S{i}"))
                    link(nc.vector.tensor_reduce(top[:, i, :], scores[:, i], AX.X, ALU.max))
                    nc.vector.tensor_tensor(scores[:, i], scores[:, i],
                                            top[:, i, :].unsqueeze(2).broadcast_to([P, H, NODES]),
                                            ALU.subtract).then_inc(shifted, 1)

                def softmax_total(s, i, link):
                    dve.wait_ge(exp_done, TI * s.n + i + 1)
                    link(nc.vector.tensor_reduce(total[:, i, :], scores[:, i], AX.X, ALU.add))
                    nc.vector.reciprocal(inv[:, i, :], total[:, i, :]).then_inc(inv_ready, 1)

                def gate_total(s, k):
                    if not s.exists():
                        return
                    dve.wait_ge(z_emptied, ZU * s.n + k + 1)
                    nc.vector.tensor_reduce(
                        gate_sum[:, 2 * (k - 2):2 * (k - 2) + 2, bass.ds(4 * s.n, 4)],
                        gate_h[:, k - 2].rearrange("p m (b n) -> p m b n", n=NODES), AX.X,
                        ALU.add).then_inc(gate_summed, 1)

                def statistics(s, which, src, link):
                    c = slice(TI * which, TI * which + TI)
                    q = s + (-1)
                    for i in range(TI):
                        last = nc.vector.bn_stats(st_y[:, TI * which + i, :], src[:, i, :])
                    link(last, True)
                    for i in range(TI):
                        last = nc.vector.bn_aggr(ag_y[:, TI * which + i, :], st_y[:, TI * which + i, :])
                    link(last)
                    if q.exists():
                        dve.wait_ge(rstd_y, 2 * q.n + which + 1)
                    nc.vector.tensor_scalar(ve_y[:, c], ag_y[:, c, 1], EPS, None, ALU.add).then_inc(var_y, 1)

                def norm(s, which, dst, src):
                    dve.wait_ge(rstd_y, 2 * s.n + which + 1)
                    for i in range(TI):
                        c = TI * which + i
                        last = nc.vector.tensor_scalar(dst[:, i, :], src[:, i, :], ag_y[:, c, 0:1],
                                                       rs_y[:, c:c + 1], ALU.subtract, ALU.mult)
                    return last

                def empty_projection(s, i):
                    dve.wait_ge(y_filled, YU * s.n + yi(f"R{i}") + 1)
                    nc.vector.tensor_tensor(o2[:, i, :], bank_y(yi(f"R{i}")), bproj[:],
                                            ALU.add).then_inc(y_emptied_dve, 1)

                def residual(s, link):
                    q = s + (-1)
                    if q.exists():
                        dve.wait_ge(x1_stored, 16 * (q.n + 1))
                    link(norm(s, 0, x1, o2))
                    link(nc.vector.tensor_tensor(x1[:], x1[:], gamma[:].unsqueeze(1).broadcast_to([P, TI, D]),
                                                 ALU.mult))
                    dve.wait_ge(rest_added, 2 * s.n + 2)
                    nc.vector.tensor_tensor(x1[:], x_res[:], x1[:], ALU.add).then_inc(x1_ready, 1)
                    dve.wait_ge(x1_ready, s.n + 1)

                def next_norm(s):
                    q = s + (-1)
                    if q.exists():
                        dve.wait_ge(n2_stored, 16 * (q.n + 1))
                        dve.wait_ge(z_filled, ZU * q.n + 2)
                    norm(s, 1, n2, x1).then_inc(n2_ready, 1)

                def take_high(s, m):
                    dve.wait_ge(high_cut[m], s.n + 1)
                    nc.vector.tensor_tensor(whole[:, m, :], whole[:, m, :], part[0][:, m, :],
                                            ALU.subtract).then_inc(high_off[m], 1)

                def cut_low(s, m):
                    dve.wait_ge(mid_cut[m], s.n + 1)
                    nc.vector.tensor_tensor(part[2][:, m, :], whole[:, m, :], part[1][:, m, :],
                                            ALU.subtract).then_inc(low_cut[m], 1)

                def before():
                    nc.vector.memset(zero[:], 0.0).then_inc(zero_set, 1)
                    nc.vector.memset(power[:], -0.5).then_inc(consts_set, 1)
                    nc.vector.memset(probs[:], 0.0).then_inc(consts_set, 1)
                    dve.wait_ge(adj_in, 32)
                    nc.vector.tensor_scalar(mask[:], adj[:], 0.0, NEG, ALU.is_equal, ALU.mult).then_inc(consts_set, 1)
                    dve.wait_ge(consts_set, 3)
                    normalise(Step(0, 0), 0)
                    for m in range(3):
                        dve.wait_ge(wqkv_high, m + 1)
                        cols = slice(m * D, (m + 1) * D)
                        nc.vector.tensor_tensor(wqkv[:, 1, :, cols], raw_wqkv(m), wqkv[:, 0, :, cols].bitcast(F32),
                                                ALU.subtract).then_inc(wqkv_cut, 1)
                    cut_n1T(Step(0, 0))
                    normalise(Step(0, 1), L_LINKS)
                    dve.wait_ge(consts_in, 16 * NCONST)

                def body(s, has_x, has_l):
                    base = (L_LINKS + Y_LINKS + W_LINKS) * s.n + 2 * L_LINKS
                    w, z = s + (-1), s + (-2)
                    if w.exists():
                        base -= W_LINKS
                    if not has_x:
                        base -= L_LINKS
                    link, count = linker(base)
                    softmax_shift(s, 0, link)
                    if has_x:
                        cut_n1T(s + 1)
                    softmax_shift(s, 1, link)
                    if w.exists():
                        statistics(w, 0, o2, link)
                    for i in range(TI):
                        softmax_total(s, i, link)
                    take_high(s, 0)
                    if w.exists():
                        residual(w, link)
                        statistics(w, 1, x1, link)
                    cut_low(s, 0)
                    if w.exists():
                        next_norm(w)
                    gate_total(z, 2)
                    take_high(s, 1)
                    empty_projection(s, 0)
                    assert count[0] == Y_LINKS + (W_LINKS if w.exists() else 0)
                    if has_l:
                        normalise(s + 2, base + count[0])
                    gate_total(z, 3)
                    cut_low(s, 1)
                    empty_projection(s, 1)

                def after():
                    end = Step(NST // 2 - 1, 1)
                    link, _ = linker((L_LINKS + Y_LINKS + W_LINKS) * NST - W_LINKS)
                    gate_total(end + (-1), 2)
                    gate_total(end + (-1), 3)
                    dve.wait_ge(y_emptied_dve, NDVE * (end.n + 1))
                    statistics(end, 0, o2, link)
                    residual(end, link)
                    statistics(end, 1, x1, link)
                    next_norm(end)
                    gate_total(end, 2)
                    gate_total(end, 3)
                    dve.wait_ge(gate_summed, 2 * NST)

                run(dve, body, before, after)

            @block.gpsimd
            def _(pool):
                def power_x(s):
                    pool.wait_ge(var_x, s.n + 1)
                    if (s + (-1)).exists():
                        pool.wait_ge(n1_ready, s.n)
                    nc.gpsimd.tensor_tensor(rs_x[:], ve_x[:], power[:], ALU.pow).then_inc(rstd_x, 1)

                def scale(s, i):
                    q = s + (-1)
                    pool.wait_ge(inv_ready, TI * s.n + i + 1)
                    if q.exists():
                        pool.wait_ge(y_filled, YU * q.n + yi("P1" + "ab"[i]) + 1)
                    for g in range(2):
                        r = slice(g * NODES, (g + 1) * NODES)
                        for tile in range(TI):
                            hs = slice(tile * (H // 2), (tile + 1) * (H // 2))
                            last = nc.gpsimd.tensor_tensor(
                                probs[r, tile, i, :, g * NODES:(g + 1) * NODES], scores[r, i, hs],
                                inv[r, i, hs].unsqueeze(2).broadcast_to([NODES, H // 2, NODES]), ALU.mult)
                    last.then_inc(probs_ready, 1)

                def power_y(s, which):
                    c = slice(TI * which, TI * which + TI)
                    pool.wait_ge(var_y, 2 * s.n + which + 1)
                    nc.gpsimd.tensor_tensor(rs_y[:, c], ve_y[:, c], power[:], ALU.pow).then_inc(rstd_y, 1)

                def add_rest(s):
                    pool.wait_ge(res_loaded, 16 * (s.n + 1))
                    nc.gpsimd.tensor_tensor(x_res[:], x_res[:], beta[:].unsqueeze(1).broadcast_to([P, TI, D]),
                                            ALU.add).then_inc(rest_added, 1)
                    pool.wait_ge(rest_added, 2 * s.n + 1)
                    pool.wait_ge(y_emptied_dve, NDVE * (s.n + 1))
                    nc.gpsimd.tensor_tensor(x_res[:], x_res[:], o2[:], ALU.add).then_inc(rest_added, 1)

                def before():
                    pool.wait_ge(consts_set, 3)
                    power_x(Step(0, 0))
                    power_x(Step(0, 1))
                    pool.wait_ge(consts_in, 16 * NCONST)

                def body(s, has_x, has_l):
                    w = s + (-1)
                    if w.exists():
                        add_rest(w)
                        power_y(w, 0)
                        pool.wait_ge(rstd_y, 2 * w.n + 1)
                    scale(s, 0)
                    scale(s, 1)
                    pool.wait_ge(probs_ready, 2 * s.n + 2)
                    if w.exists():
                        power_y(w, 1)
                    if has_l:
                        power_x(s + 2)

                def after():
                    end = Step(NST // 2 - 1, 1)
                    add_rest(end)
                    power_y(end, 0)
                    power_y(end, 1)

                run(pool, body, before, after)


def gates(nc, t, keep):
    with ExitStack() as ctx:
        def sb(name, shape, dt=F32):
            return ctx.enter_context(nc.sbuf_tensor(name, shape, dt))

        def sem(name):
            return ctx.enter_context(nc.semaphore(name))

        fc2 = sb("fc2", [P, KD, P])
        fc2_b = sb("fc2_b", [P, 1])
        sel = sb("sel", [P, 8])
        sel9 = sb("sel9", [E + 1, 2])
        g = sb("g", [P, GRAPHS])
        rest = sb("g_rest", [P, GRAPHS])
        part = [sb(f"g_part{k}", [P, GRAPHS], BF16) for k in range(3)]
        mix = sb("g_mix", [P, 2, GRAPHS])
        tvb1 = sb("tvb1", [E + 1, F])
        lnp = sb("lnp", [E, 2, D])
        lnq = sb("lnq", [E, 2, D])
        lnr = sb("lnr", [P, 2, D])
        ones = sb("ones", [E, P])
        ps = ctx.enter_context(nc.psum_tensor("ps_g", [P, 8, 512], F32))
        loaded, cleared, filled, cut, emptied = sem("g_loaded"), sem("g_cleared"), sem("g_filled"), sem("g_cut"), sem("g_emptied")
        gate_sum, gblk, g9, b1m, lnw = keep["gate_sum"], keep["gblk"], keep["g9"], keep["b1m"], keep["lnw"]
        nload = [0]

        with nc.Block() as block:
            @block.sync
            def _(sp):
                def load(dst, src):
                    sp.dma_start(dst, src).then_inc(loaded, 16)
                    nload[0] += 1
                sp.wait_ge(cleared, 3)
                for half in range(2):
                    for c in range(PAIRS):
                        at = half * HALF + c * E
                        load(fc2[:, :, at:at + E], t["fc2T"].rearrange("(k p) e -> p k e", p=P))
                        load(fc2_b[at:at + E, :], t["fc2_b"])
                load(sel[:], t["sel"])
                load(sel9[:], t["sel9"])
                load(tvb1[0:E, :], t["tvb1"])
                load(tvb1[E:E + 1, :], t["b1"].unsqueeze(0))
                load(keep["tvb2"][0:E, :], t["tvb2"])
                load(keep["tvb2"][E:E + 1, :], t["b2"].unsqueeze(0))
                for m, (w, tvw) in enumerate((("ln_g", "tv_ln_g"), ("ln_b", "tv_ln_b"))):
                    load(lnp[:, m, :], t[tvw])
                    load(lnq[:, m, :], t[w].partition_broadcast(E))
                    load(lnr[:, m, :], t[w].partition_broadcast(P))

            NLOAD = 2 * PAIRS * 2 + 6 + 6

            @block.vector
            def _(dve):
                nc.vector.memset(fc2[:], 0.0).then_inc(cleared, 1)
                nc.vector.memset(fc2_b[:], 0.0).then_inc(cleared, 1)
                nc.vector.memset(ones[:], 1.0).then_inc(cleared, 1)
                dve.wait_ge(loaded, 16 * NLOAD)
                count = [0]

                def link(ins):
                    count[0] += 1
                    ins.then_inc(cut, 1)
                    dve.wait_ge(cut, count[0])

                link(nc.vector.tensor_tensor(lnp[:], lnp[:], lnq[:], ALU.subtract))
                dve.wait_ge(filled, 1)
                link(nc.vector.tensor_scalar(g[:], ps[:, 0, 0:GRAPHS], 1.0 / NODES, fc2_b[:, 0:1],
                                             ALU.mult, ALU.add))
                link(nc.vector.tensor_scalar(g9[:], g[0:E + 1, :], sel9[:, 0:1], sel9[:, 1:2],
                                             ALU.mult, ALU.add))
                link(nc.vector.tensor_copy(part[0][:], g[:]))
                link(nc.vector.tensor_tensor(rest[:], g[:], part[0][:], ALU.subtract))
                link(nc.vector.tensor_copy(part[1][:], rest[:]))
                link(nc.vector.tensor_tensor(part[2][:], rest[:], part[1][:], ALU.subtract))
                for half in range(2):
                    one = sel[:, 4 * half + 3:4 * half + 4]
                    link(nc.vector.tensor_scalar(mix[:, 0, :], part[0][:], sel[:, 4 * half:4 * half + 1], one,
                                                 ALU.mult, ALU.add))
                    link(nc.vector.scalar_tensor_tensor(out=mix[:, 1, :], in0=part[1][:],
                                                        scalar=sel[:, 4 * half + 1:4 * half + 2],
                                                        in1=mix[:, 0, :], op0=ALU.mult, op1=ALU.add))
                    link(nc.vector.scalar_tensor_tensor(
                        out=gblk[:, :, half, :], in0=part[2][:].rearrange("p (g b) -> p g b", b=GB),
                        scalar=sel[:, 4 * half + 2:4 * half + 3],
                        in1=mix[:, 1, :].rearrange("p (g b) -> p g b", b=GB), op0=ALU.mult, op1=ALU.add))
                for m in range(2):
                    dve.wait_ge(filled, 2 + m)
                    link(nc.vector.scalar_tensor_tensor(out=lnw[:, m, :], in0=ps[:, 1 + m, :], scalar=LN_MERGE,
                                                        in1=lnr[:, m, :], op0=ALU.mult, op1=ALU.add))
                for k in range(4):
                    dve.wait_ge(filled, 4 + k)
                    link(nc.vector.tensor_copy(b1m[:, 4 * k:4 * k + 4, :],
                                               ps[:, 3 + k, :].rearrange("p (a b) -> p a b", b=GRAPHS)))

            @block.tensor
            def _(pe):
                pe.wait_ge(loaded, 16 * NLOAD)
                for c in range(KD):
                    last = pe.matmul(ps[:, 0, 0:GRAPHS], fc2[:, c, :], gate_sum[:, c, :],
                                     start=(c == 0), stop=(c == KD - 1))
                last.then_inc(filled, 1)
                pe.wait_ge(cut, 1)
                for m in range(2):
                    pe.matmul(ps[:, 1 + m, :], ones[:], lnp[:, m, :], start=True, stop=True).then_inc(filled, 1)
                pe.wait_ge(cut, 3)
                for k in range(4):
                    for a in range(4):
                        last = pe.matmul(ps[:, 3 + k, a * GRAPHS:(a + 1) * GRAPHS],
                                         tvb1[:, (4 * k + a) * P:(4 * k + a + 1) * P], g9[:],
                                         start=True, stop=True)
                    last.then_inc(filled, 1)


def feed(nc, t, keep):
    gblk, g9, b1m, lnw, ident = keep["gblk"], keep["g9"], keep["b1m"], keep["lnw"], keep["ident"]
    tvb2 = keep["tvb2"]
    with ExitStack() as ctx:
        def sb(name, shape, dt=F32):
            return ctx.enter_context(nc.sbuf_tensor(name, shape, dt))

        def sem(name):
            return ctx.enter_context(nc.semaphore(name))

        SLOT = 8192
        ROWS = 3
        slot = sb("slot", [P, 2, SLOT])
        nT = sb("nT", [P, KD, GT])
        acc = sb("acc", [P, PR, D])
        pieces = sb("pieces", [KROWS, 4, PIECE], BF16)
        hid = sb("hid", [P, PR, P])
        hT = sb("hT", [P, GT])
        gnow = sb("gnow", [KROWS, 2 * GB], BF16)
        bnow = sb("bnow", [P, GB])
        gtok = sb("gtok", [E + 1, 2, P])
        x_row = sb("x_row", [P, ROWS, 2, D])
        st, ag = sb("st_f", [P, PR, 6]), sb("ag_f", [P, PR, 2])
        ve, rs, shift = sb("ve_f", [P, PR]), sb("rs_f", [P, PR]), sb("shift_f", [P, PR])
        power = sb("power_f", [P, PR])
        x_rest = nT[:].rearrange("p k (a d) -> p (k a) d", d=D)
        ps_m = ctx.enter_context(nc.psum_tensor("ps_m", [P, 2, 1024], F32))
        ps_w = ctx.enter_context(nc.psum_tensor("ps_w", [P, 4, 512], F32))

        nT_loaded = sem("nT_loaded")
        piece_in = [sem(f"piece_in{k}") for k in range(4)]
        merged = sem("merged")
        kept_act, kept_dve = sem("kept_act"), sem("kept_dve")
        work = sem("work")
        work_act, work_dve = sem("work_act"), sem("work_dve")
        g_ready, b_ready, gtok_ready = sem("g_ready"), sem("b_ready"), sem("gtok_ready")
        power_set = sem("power_set")
        var_f, rstd_f = sem("var_f"), sem("rstd_f")
        x_in = [sem(f"x_in{b}") for b in range(ROWS)]
        acc_in = [sem(f"acc_in{a}") for a in range(PR // 4)]
        y_out = [sem(f"y_out{b}") for b in range(ROWS)]
        y_last, x_last, rest_ready = sem("y_last"), sem("x_last"), sem("rest_ready")
        shift_ready, normed, scaled, y_ready = sem("shift_ready"), sem("normed"), sem("scaled"), sem("y_ready")
        link_f = sem("link_f")

        FIRST = ["La0", "La1", "Lb0", "T0", "T1", "Lb1", "T2", "T3"]
        INIT, NL1, NL2 = PR, len(FIRST), 16
        PER_T = NL1 + NL2
        PER_G = INIT + FT * PER_T
        DVE_G = INIT + FT * NL2
        CREDIT = 4
        UNITS = 4 * FT
        KEPT = 1

        def first_index(g, f, k):
            start = 0 if isinstance(f, int) and f == 0 else INIT + f * PER_T
            return g * PER_G + start + k + 1

        def second_index(g, f, k):
            return g * PER_G + INIT + f * PER_T + NL1 + k + 1

        def init_index(g, i):
            return g * PER_G + NL1 + i + 1

        def all_groups(engine, group):
            group(0, True, False)
            with engine.Fori(1, GROUPS - 1) as g:
                group(g, False, False)
            group(GROUPS - 1, False, True)

        s1 = t["s1"].rearrange("(p v c) -> v p c", p=KROWS, c=PIECE)
        s2 = t["s2"].rearrange("(p v c) -> v p c", p=KROWS, c=PIECE)
        nTt = t["n2T"].rearrange("k p (g c) -> g p k c", c=GT)
        n2t = t["n2"].rearrange("(a i p) d -> a p i d", i=4, p=P)
        x1t = t["x1"].rearrange("(a i p) d -> a p i d", i=2, p=P)
        yt = t["y"].rearrange("(a i p) d -> a p i d", i=2, p=P)
        PAIR = PR // 2
        USES = [len(range(b, PAIR, ROWS)) for b in range(ROWS)]

        def rows_after(q):
            return range(0) if q == 0 else range(2 * q - 2, 2 * q if q < 7 else PR)

        with nc.Block() as block:
            @block.sync
            def _(sp):
                def unit(u, src, at):
                    for k in range(4):
                        sp.wait_ge(merged, 8 * u + 2 * k + 2)
                        sp.dma_start(pieces[:, k, :], src[bass.ds(at + k, 1)].rearrange("a p c -> (a p) c")
                                     ).then_inc(piece_in[k], 16)

                with sp.Fori(0, GROUPS) as g:
                    with sp.Fori(0, FT) as f:
                        u = g * UNITS + f * 4
                        unit(u, s1, f * 8)
                        unit(u + 1, s1, f * 8 + 4)
                        unit(u + 2, s2, f * 4)
                        unit(u + 3, s2, f * 4 + 4 * FT)
                for i in range(PAIR):
                    sp.wait_ge(scaled, (GROUPS - 1) * PR + 2 * i + 2)
                    sp.dma_start(yt[(GROUPS - 1) * PAIR + i], acc[:, 2 * i:2 * i + 2, :]).then_inc(y_last, 16)
                sp.wait_ge(y_last, 16 * PAIR)

            @block.tensor
            def _(pe):
                def merge(u, second, q):
                    if q % 2 == 0:
                        pe.wait_ge(piece_in[q // 2], 16 * (u + 1))
                    pe.wait_ge(kept_act if q % 2 == 0 else kept_dve, KEPT + 4 * u + q // 2)
                    for r in range(16):
                        if second:
                            at = ((q % 2) * 16 + r) * P
                        else:
                            at = (r % 8) * D + ((q % 2) * 2 + r // 8) * P
                        last = pe.matmul(ps_m[:, q % 2, r * 64:(r + 1) * 64], pieces[:, q // 2, at:at + P],
                                         gnow[:], start=True, stop=True)
                    last.then_inc(merged, 1)

                def kept(u):
                    pe.wait_ge(kept_act, KEPT + 4 * u + 4)
                    pe.wait_ge(kept_dve, KEPT + 4 * u + 4)

                def act_base(g, f):
                    return (g * FT + f) * NL1

                def dve_base(g, f):
                    return CREDIT + g * DVE_G + INIT + f * NL2

                def free_first(g, f, k):
                    before = dve_base(g, f) - (INIT if isinstance(f, int) and f == 0 else 0)
                    pe.wait_ge(work_dve, before - 4 + k + 1)

                def first_graphs(g, f, ab, bank, graphs):
                    k = FIRST.index("L" + "ab"[ab] + str(bank))
                    w = slot[:, ab, :].rearrange("p (k b f) -> p k b f", k=KD, b=GB)
                    for b in graphs:
                        bb, r = bank * 16 + b, NODES * (b % 2)
                        for c in range(KD):
                            last = pe.matmul(ps_w[r:r + NODES, k % 4, (b // 2) * 64:(b // 2 + 1) * 64],
                                             nT[:, c, bb * NODES:(bb + 1) * NODES], w[:, c, bb, :],
                                             start=(c == 0), stop=(c == KD - 1))
                    if graphs[-1] == 15:
                        last.then_inc(work, 1)

                def turn(g, f, q):
                    k = FIRST.index(f"T{q}")
                    if q == 0:
                        free_first(g, f, k)
                    pe.wait_ge(work_act, act_base(g, f) + FIRST.index("Lb0" if q < 2 else "Lb1") + 1)
                    for p in range(4):
                        last = pe.transpose(ps_w[:, k % 4, p * P:(p + 1) * P], hid[:, 4 * q + p, :], ident[:])
                    last.then_inc(work, 1)

                def second_graphs(g, f, cd, q):
                    k = 8 * cd + q
                    if k >= 4:
                        pe.wait_ge(work_dve, dve_base(g, f) + k - 4 + 1)
                    elif isinstance(f, int) and f == 0:
                        pe.wait_ge(work_dve, dve_base(g, f) - 4 + k + 1)
                    else:
                        pe.wait_ge(work_act, act_base(g, f) + 4 + k + 1)
                    w = slot[:, cd, :].rearrange("p (b d) -> p b d", b=GB)
                    for b in range(4):
                        bb, r = 4 * q + b, NODES * (b % 2)
                        last = pe.matmul(ps_w[r:r + NODES, k % 4, (b // 2) * 256:(b // 2 + 1) * 256],
                                         hT[:, bb * NODES:(bb + 1) * NODES], w[:, bb, :], start=True, stop=True)
                    last.then_inc(work, 1)

                def second_bias(g):
                    for i in range(INIT):
                        if i < 4:
                            pe.wait_ge(work_act, act_base(g, 0) + 4 + i + 1)
                        else:
                            pe.wait_ge(work_dve, CREDIT + g * DVE_G + i - 4 + 1)
                        pe.wait_ge(gtok_ready, g * INIT + i + 1)
                        pe.matmul(ps_w[:, i % 4, :], gtok[:, i % 2, :], tvb2[:], start=True, stop=True
                                  ).then_inc(work, 1)

                def tile(g, f, following):
                    u = g * UNITS + f * 4
                    merge(u + 1, False, 0)
                    kept(u)
                    for q in range(8):
                        if q < 7:
                            merge(u + 1, False, q + 1)
                        if q % 4 == 0:
                            free_first(g, f, q // 4)
                        first_graphs(g, f, 0, q // 4, range(4 * (q % 4), 4 * (q % 4) + 4))
                    merge(u + 2, True, 0)
                    kept(u + 1)
                    for q in range(8):
                        if q < 7:
                            merge(u + 2, True, q + 1)
                        if q == 0:
                            free_first(g, f, 2)
                        if q == 4:
                            pe.wait_ge(work_act, act_base(g, f) + 2)
                        first_graphs(g, f, 1, q // 4, range(4 * (q % 4), 4 * (q % 4) + 4))
                        if q == 4:
                            turn(g, f, 0)
                        if q == 6:
                            turn(g, f, 1)
                    merge(u + 3, True, 0)
                    merge(u + 3, True, 1)
                    turn(g, f, 2)
                    turn(g, f, 3)
                    if isinstance(f, int) and f == 0:
                        second_bias(g)
                    kept(u + 2)
                    for q in range(8):
                        if 0 < q < 7:
                            merge(u + 3, True, q + 1)
                        second_graphs(g, f, 0, q)
                    if following == 2:
                        pe.wait_ge(g_ready, g + 2)
                    if following:
                        merge(u + 4, False, 0)
                    kept(u + 3)
                    for q in range(8):
                        if following and q < 7:
                            merge(u + 4, False, q + 1)
                        second_graphs(g, f, 1, q)

                def group(g, first, last):
                    wait_apart(pe, nT_loaded, 16 * (g + 1), power_set, 1)
                    tile(g, 0, 1)
                    with pe.Fori(1, FT - 1) as f:
                        tile(g, f, 1)
                    tile(g, FT - 1, 0 if last else 2)

                pe.sem_inc(merged, 8)
                pe.wait_ge(g_ready, 1)
                for q in range(8):
                    merge(0, False, q)
                all_groups(pe, group)

            def keep(eng, copy, u, second, s, q, done):
                eng.wait_ge(merged, 8 + 8 * u + q + 1)
                bank = ps_m[:, q % 2, :]
                if second:
                    src = bank.rearrange("p (r h b) -> p b h r", r=16, h=2)
                    dst = slot[:, s, :].rearrange("p (b h r) -> p b h r", b=GB, h=2)[:, :, :, 16 * q:16 * q + 16]
                    last = copy(dst, src)
                else:
                    for m in range(2):
                        c = 2 * (q % 2) + m
                        src = bank[:, 512 * m:512 * (m + 1)].rearrange("p (r h b) -> p b h r", r=8, h=2)
                        dst = slot[:, s, :].rearrange("p (k b h r) -> p k b h r", k=KD, b=GB, h=2)[
                            :, c, :, :, 8 * (q // 2):8 * (q // 2) + 8]
                        last = copy(dst, src)
                last.then_inc(done, 1)

            @block.scalar
            def _(act):
                def copy(dst, src):
                    return nc.scalar.activation(dst, src, ACT.Copy)

                def keep_act(u, second, s, q):
                    keep(act, copy, u, second, s, q, kept_act)

                def first_out(g, f, ab, bank):
                    k = FIRST.index("L" + "ab"[ab] + str(bank))
                    act.wait_ge(work, first_index(g, f, k))
                    nc.scalar.activation(hid[:, 8 * bank:8 * bank + 8, 64 * ab:64 * ab + 64],
                                         ps_w[:, k % 4, :].rearrange("p (i f) -> p i f", f=64),
                                         ACT.Copy).then_inc(work_act, 1)

                def relu(g, f, q):
                    k = FIRST.index(f"T{q}")
                    act.wait_ge(work, first_index(g, f, k))
                    for b in range(8):
                        bb = 8 * q + b
                        last = nc.scalar.activation(hT[:, bb * NODES:(bb + 1) * NODES],
                                                    ps_w[:, k % 4, b * NODES:(b + 1) * NODES], ACT.Relu,
                                                    bias=bnow[:, bb:bb + 1])
                    last.then_inc(work_act, 1)

                def norm_rows(g, rows):
                    for i in rows:
                        nc.scalar.activation(acc[:, i, :], acc[:, i, :], ACT.Identity, bias=shift[:, i:i + 1],
                                             scale=rs[:, i:i + 1]).then_inc(normed, 1)

                def gates_of(g, is_first):
                    if not is_first:
                        act.wait_ge(merged, 8 + 8 * UNITS * g)
                    nc.scalar.activation(gnow[:].rearrange("p (h b) -> p h b", b=GB).unsqueeze(1),
                                         gblk[0:KROWS, bass.ds(g, 1)], ACT.Copy).then_inc(g_ready, 1)

                def tile(g, f, following, unfinished=False):
                    u = g * UNITS + f * 4
                    nc.scalar.activation(bnow[:].unsqueeze(1), b1m[:, bass.ds(f, 1), bass.ds(g * GB, GB)],
                                         ACT.Copy).then_inc(b_ready, 1)
                    act.wait_ge(b_ready, g * FT + f + 1)
                    for q in range(8):
                        if q % 2 == 0:
                            keep_act(u + 1, False, 1, q)
                            if unfinished:
                                if q == 2:
                                    act.wait_ge(shift_ready, g)
                                norm_rows(g - 1, rows_after(q // 2))
                        if q == 4:
                            first_out(g, f, 0, 0)
                    first_out(g, f, 0, 1)
                    for q in range(8):
                        if q % 2 == 0:
                            keep_act(u + 2, True, 0, q)
                            if unfinished:
                                norm_rows(g - 1, rows_after(4 + q // 2))
                        if q == 4:
                            first_out(g, f, 1, 0)
                            relu(g, f, 0)
                        if q == 6:
                            relu(g, f, 1)
                    first_out(g, f, 1, 1)
                    keep_act(u + 3, True, 1, 0)
                    relu(g, f, 2)
                    relu(g, f, 3)
                    for q in (2, 4, 6):
                        keep_act(u + 3, True, 1, q)
                    if following == 2:
                        gates_of(g + 1, False)
                    if following:
                        for q in (0, 2, 4, 6):
                            keep_act(u + 4, False, 0, q)

                def group(g, first, last):
                    tile(g, 0, 1, not first)
                    with act.Fori(1, FT - 1) as f:
                        tile(g, f, 1)
                    tile(g, FT - 1, 0 if last else 2)
                    if last:
                        act.wait_ge(shift_ready, GROUPS)
                        norm_rows(g, range(PR))

                act.sem_inc(kept_act, KEPT)
                gates_of(0, True)
                for q in (0, 2, 4, 6):
                    keep_act(0, False, 0, q)
                all_groups(act, group)

            @block.vector
            def _(dve):
                LINKS = 2 + PR

                def copy(dst, src):
                    return nc.vector.tensor_copy(dst, src)

                def keep_dve(u, second, s, q):
                    keep(dve, copy, u, second, s, q, kept_dve)

                def add_second(g, f, cd, q):
                    k = 8 * cd + q
                    if q % 4 == 0:
                        dve.wait_ge(work_dve, CREDIT + g * DVE_G + INIT + f * NL2 + k - 4)
                    dve.wait_ge(work, second_index(g, f, k))
                    part = acc[:, 2 * q:2 * q + 2, 256 * cd:256 * cd + 256]
                    nc.vector.tensor_tensor(part, ps_w[:, k % 4, :].rearrange("p (i d) -> p i d", d=256),
                                            part, ALU.add).then_inc(work_dve, 1)

                def second_bias(g):
                    def spread(i):
                        if i >= 2:
                            dve.wait_ge(work, init_index(g, i - 2))
                        for h in range(2):
                            last = nc.vector.tensor_copy(
                                gtok[:, i % 2, h * NODES:(h + 1) * NODES],
                                g9[:, bass.ds(g * GB + 2 * i + h, 1)].broadcast_to([E + 1, NODES]))
                        last.then_inc(gtok_ready, 1)

                    spread(0)
                    spread(1)
                    for i in range(INIT):
                        dve.wait_ge(acc_in[i // 4], 16 * (g + 1))
                        dve.wait_ge(work, init_index(g, i))
                        nc.vector.tensor_tensor(acc[:, i, :], ps_w[:, i % 4, :], acc[:, i, :],
                                                ALU.add).then_inc(work_dve, 1)
                        if i + 2 < INIT:
                            spread(i + 2)

                def link(ins, g, k, by_stats=False):
                    ins.then_inc(link_f, 1)
                    if by_stats:
                        wait_apart(dve, link_f, g * LINKS + k, power_set, 1)
                    else:
                        dve.wait_ge(link_f, g * LINKS + k)

                def row_stats(g, q):
                    wait_apart(dve, work_dve, CREDIT + g * DVE_G + INIT + (FT - 1) * NL2 + 8 + q + 1, power_set, 1)
                    for i in range(2 * q, 2 * q + 2):
                        last = nc.vector.bn_stats(st[:, i, :], acc[:, i, :])
                    return last

                def variances(g, last):
                    link(last, g, 1, True)
                    for i in range(PR):
                        ins = nc.vector.bn_aggr(ag[:, i, :], st[:, i, :])
                    link(ins, g, 2)
                    nc.vector.tensor_scalar(ve[:], ag[:, :, 1], EPS, None, ALU.add).then_inc(var_f, 1)

                def shifts(g):
                    dve.wait_ge(rstd_f, g + 1)
                    nc.vector.scalar_tensor_tensor(out=shift[:], in0=ag[:, :, 0], scalar=-1.0, in1=rs[:],
                                                   op0=ALU.mult, op1=ALU.mult).then_inc(shift_ready, 1)

                def scale_rows(g, rows, last=False):
                    for i in rows:
                        dve.wait_ge(normed, g * PR + i + 1)
                        link(nc.vector.tensor_tensor(acc[:, i, :], acc[:, i, :], lnw[:, 0, :], ALU.mult),
                             g, 3 + i)
                        if last and i % 2 == 0:
                            dve.wait_ge(rest_ready, i // 2 + 1)
                        nc.vector.tensor_tensor(acc[:, i, :], acc[:, i, :], x_rest[:, i, :] if last else lnw[:, 1, :],
                                                ALU.add).then_inc(scaled, 1)

                def tile(g, f, following, unfinished=False):
                    u = g * UNITS + f * 4
                    for q in (1, 3, 5, 7):
                        keep_dve(u + 1, False, 1, q)
                        if unfinished:
                            if q == 1:
                                shifts(g - 1)
                            scale_rows(g - 1, rows_after(q // 2))
                    for q in (1, 3, 5, 7):
                        keep_dve(u + 2, True, 0, q)
                        if unfinished:
                            scale_rows(g - 1, rows_after(4 + q // 2))
                    keep_dve(u + 3, True, 1, 1)
                    if isinstance(f, int) and f == 0:
                        second_bias(g)
                    for q in range(8):
                        if q % 2 == 0 and q:
                            keep_dve(u + 3, True, 1, q + 1)
                        add_second(g, f, 0, q)
                    for q in range(8):
                        if q % 2 == 0 and following:
                            keep_dve(u + 4, False, 0, q + 1)
                        add_second(g, f, 1, q)
                        if following != 1 and q:
                            row_stats(g, q - 1)
                    if following != 1:
                        variances(g, row_stats(g, 7))

                def group(g, first, last):
                    tile(g, 0, 1, not first)
                    with dve.Fori(1, FT - 1) as f:
                        tile(g, f, 1)
                    tile(g, FT - 1, 0 if last else 2)
                    if last:
                        shifts(g)
                        scale_rows(g, range(PR), True)

                nc.vector.memset(power[:], -0.5).then_inc(power_set, 1)
                dve.sem_inc(work_dve, CREDIT)
                dve.sem_inc(kept_dve, KEPT)
                for q in (1, 3, 5, 7):
                    keep_dve(0, False, 0, q)
                all_groups(dve, group)

            @block.gpsimd
            def _(pool):
                def load_nT(g):
                    pool.dma_start(nT[:], nTt[bass.ds(g, 1)].rearrange("g p k c -> (g p) k c")).then_inc(nT_loaded, 16)

                def load_acc(g, a):
                    pool.dma_start(acc[:, 4 * a:4 * a + 4, :],
                                   n2t[bass.ds(g * (PR // 4) + a, 1)].rearrange("a p i d -> (a p) i d")
                                   ).then_inc(acc_in[a], 16)

                def load_x(g, i):
                    pool.dma_start(x_row[:, i % ROWS], x1t[bass.ds(g * PAIR + i, 1)].rearrange("a p i d -> (a p) i d")
                                   ).then_inc(x_in[i % ROWS], 16)

                def last_group(g):
                    wait_apart(pool, work, first_index(g, FT - 1, FIRST.index("Lb1")), power_set, 1)
                    pool.dma_start(x_rest, t["x1"].rearrange("(g i p) d -> g p i d", i=PR, p=P)[g]).then_inc(x_last, 16)
                    pool.wait_ge(x_last, 16)
                    for i in range(PAIR):
                        if i == PAIR // 2:
                            pool.wait_ge(var_f, g + 1)
                            nc.gpsimd.tensor_tensor(rs[:], ve[:], power[:], ALU.pow).then_inc(rstd_f, 1)
                        two = x_rest[:, 2 * i:2 * i + 2, :]
                        nc.gpsimd.tensor_tensor(two, two, lnw[:, 1, :].unsqueeze(1).broadcast_to([P, 2, D]),
                                                ALU.add).then_inc(rest_ready, 1)

                def group(g, first, last):
                    if last:
                        return last_group(g)
                    for i in range(ROWS):
                        if not first:
                            wait_apart(pool, y_out[i], 16 * g * USES[i], power_set, 1)
                        load_x(g, i)
                    wait_apart(pool, work, first_index(g, FT - 1, FIRST.index("Lb1")), power_set, 1)
                    load_nT(g + 1)
                    pool.wait_ge(var_f, g + 1)
                    nc.gpsimd.tensor_tensor(rs[:], ve[:], power[:], ALU.pow).then_inc(rstd_f, 1)
                    for i in range(PAIR):
                        b = i % ROWS
                        pool.wait_ge(x_in[b], 16 * (g * USES[b] + i // ROWS + 1))
                        pool.wait_ge(scaled, g * PR + 2 * i + 2)
                        nc.gpsimd.tensor_tensor(x_row[:, b], acc[:, 2 * i:2 * i + 2, :], x_row[:, b],
                                                ALU.add).then_inc(y_ready, 1)
                        wait_apart(pool, y_ready, g * PAIR + i + 1, power_set, 1)
                        if i % 2:
                            load_acc(g + 1, i // 2)
                        pool.dma_start(yt[bass.ds(g * PAIR + i, 1)].rearrange("a p i d -> (a p) i d"),
                                       x_row[:, b]).then_inc(y_out[b], 16)
                        following = i + ROWS - 1
                        if ROWS <= following < PAIR:
                            b = (i - 1) % ROWS
                            wait_apart(pool, y_out[b], 16 * (g * USES[b] + (i - 1) // ROWS + 1), power_set, 1)
                            load_x(g, following)

                pool.wait_ge(power_set, 1)
                load_nT(0)
                for a in range(PR // 4):
                    load_acc(0, a)
                all_groups(pool, group)
                for b in range(ROWS):
                    pool.wait_ge(y_out[b], 16 * (GROUPS - 1) * USES[b])


def graph_ffn(nc, t):
    with ExitStack() as ctx:
        def sb(name, shape, dt=F32):
            return ctx.enter_context(nc.sbuf_tensor(name, shape, dt))

        keep = {
            "ident": sb("ident", [P, P]),
            "gate_sum": sb("gate_sum", [P, KD, GRAPHS]),
        }
        ident_in = ctx.enter_context(nc.semaphore("ident_in"))
        with nc.Block() as block:
            @block.sync
            def _(sp):
                sp.dma_start(keep["ident"][:], t["ident"]).then_inc(ident_in, 16)
                sp.wait_ge(ident_in, 16)
        attend(nc, t, keep)
        keep |= {
            "gblk": sb("gblk", [P, GROUPS, 2, GB], BF16),
            "g9": sb("g9", [E + 1, GRAPHS]),
            "b1m": sb("b1m", [P, FT, GRAPHS]),
            "lnw": sb("lnw", [P, 2, D]),
            "tvb2": sb("tvb2", [E + 1, D]),
        }
        gates(nc, t, keep)
        feed(nc, t, keep)


def kernel(**inputs):
    import concourse.bacc as bacc
    from concourse.bass_utils import run_bass_kernel_spmd

    i = {k: np.asarray(v) for k, v in inputs.items()}

    def rows_of(w, matrix):
        n = w.shape[0]
        if matrix == 1:
            return w.reshape(n, F // 64, 2, 32, D).transpose(0, 2, 1, 3, 4).reshape(n, 2, HROW)
        return w.reshape(n, 2, 2, P, FT, P).transpose(0, 2, 1, 4, 3, 5).reshape(n, 2, HROW)

    def shares(w, matrix, count):
        r = rows_of(w, matrix)
        return r.reshape(r.shape[0], 2, count, -1).transpose(0, 2, 1, 3).reshape(-1)

    sel9 = np.zeros((E + 1, 2), np.float32)
    sel9[:E, 0] = 1.0
    sel9[E, 1] = 1.0
    arrays = {
        "x": i["x"].reshape(TOK, D),
        "adj": i["adj"],
        "wqkv": i["L0_gnn_w_qkv"],
        "wproj": i["L0_gnn_w_proj"],
        "bproj": i["L0_gnn_b_proj"],
        "gamma": i["L0_gnn_ln_gamma"],
        "beta": i["L0_gnn_ln_beta"],
        "gfc1T": i["L0_ffn_gfc1_w"].T,
        "gfc1_b": i["L0_ffn_gfc1_b"].reshape(KD, P).T,
        "fc2T": i["L0_ffn_gfc2_w"].T,
        "fc2_b": i["L0_ffn_gfc2_b"].reshape(E, 1),
        "W1": shares(i["L0_ffn_W1"][None], 1, NST),
        "b1": i["L0_ffn_b1"],
        "W2": shares(i["L0_ffn_W2"][None], 2, NST),
        "b2": i["L0_ffn_b2"],
        "ln_g": i["L0_ffn_ln_g"],
        "ln_b": i["L0_ffn_ln_b"],
        "tvW1": shares(i["L0_ffn_tv_W1"], 1, NST // E),
        "tvb1": i["L0_ffn_tv_b1"],
        "tvW2": shares(i["L0_ffn_tv_W2"], 2, NST // E),
        "tvb2": i["L0_ffn_tv_b2"],
        "tv_ln_g": i["L0_ffn_tv_ln_g"],
        "tv_ln_b": i["L0_ffn_tv_ln_b"],
        "ident": np.eye(P, dtype=np.float32),
        "sel": selection(),
        "sel9": sel9,
    }
    arrays = {k: np.ascontiguousarray(v) for k, v in arrays.items()}
    nc = bacc.Bacc("TRN2", target_bir_lowering=False, num_devices=1)
    t = {}
    for name, a in arrays.items():
        t[name] = nc.dram_tensor(f"in_{name}", a.shape, mybir.dt.from_np(a.dtype), kind="ExternalInput").ap()
    t["y"] = nc.dram_tensor("out_y", (TOK, D), F32, kind="ExternalOutput").ap()
    for name, shape, dt in (("x1", (TOK, D), F32), ("n2", (TOK, D), F32), ("n2T", (KD, P, TOK), F32),
                            ("s1", (KROWS * HROW,), BF16), ("s2", (KROWS * HROW,), BF16)):
        t[name] = nc.dram_tensor(f"scratch_{name}", shape, dt, kind="Internal").ap()
    graph_ffn(nc, t)
    r = run_bass_kernel_spmd(nc, [{f"in_{k}": v for k, v in arrays.items()}], core_ids=[0])
    return r.results[0]["out_y"].reshape(GRAPHS, NODES, D)
```
